# Optimizing a Trainium2 kernel written in Bass

```python
import numpy as np
import jax
import jax.numpy as jnp

def _softmax(x, axis=-1):
    return jax.nn.softmax(x, axis=axis)

def _gelu(x):
    return jax.nn.gelu(x, approximate=True)

def _silu(x):
    return jax.nn.silu(x)

def _sigmoid(x):
    return jax.nn.sigmoid(x)

def _layernorm(x, axis=-1, eps=1e-05):
    m = jnp.mean(x, axis=axis, keepdims=True)
    v = jnp.var(x, axis=axis, keepdims=True)
    return (x - m) / jnp.sqrt(v + eps)

def _scatter_add(tgt, idx, src, axis=0):
    return tgt.at[idx].add(src)

def _segment_sum(src, seg, n):
    return jax.ops.segment_sum(src, seg, n)
kernel_name = 'mk_seq_postln_d2_jaxref_r8_4a166e'

def setup_inputs(seed: int=0):
    np.random.seed(seed)
    _w = jnp.asarray

    def _L0_attn_setup():
        import jax, jax.numpy as jnp
        import numpy as np
        D = 128
        H = 16
        KVH = 4
        HD = D // H
        LAT = 32
        WIN = 32
        B, S = (1, 256)
        BASE_G, BASE_L = (1000000.0, 10000.0)
        EPS = 1e-06

        def rmsnorm(x, w):
            return x * jax.lax.rsqrt(jnp.mean(x * x, axis=-1, keepdims=True) + EPS) * w

        def qk_norm(x):
            return x * jax.lax.rsqrt(jnp.mean(x * x, axis=-1, keepdims=True) + EPS)

        def rope(x, base):
            s, hd = (x.shape[-2], x.shape[-1])
            inv_freq = 1.0 / base ** (jnp.arange(0, hd, 2, dtype=jnp.float32) / hd)
            freqs = jnp.arange(s, dtype=jnp.float32)[:, None] * inv_freq[None, :]
            cos, sin = (jnp.cos(freqs), jnp.sin(freqs))
            xe, xo = (x[..., ::2], x[..., 1::2])
            out = jnp.stack([xe * cos - xo * sin, xe * sin + xo * cos], axis=-1)
            return out.reshape(x.shape)

        def split_heads(x, n_heads):
            b, s, _ = x.shape
            return x.reshape(b, s, n_heads, HD).transpose(0, 2, 1, 3)

        def repeat_kv(x):
            return jnp.repeat(x, H // KVH, axis=1)

        def sdpa(q, k, v, mask):
            scores = jnp.einsum('bhqd,bhkd->bhqk', q, k) / np.sqrt(HD).astype(np.float32)
            scores = jnp.where(mask, scores, jnp.float32(-1e+30))
            probs = jax.nn.softmax(scores, axis=-1)
            return jnp.einsum('bhqk,bhkd->bhqd', probs, v)

        def merge_heads(x):
            b, h, s, hd = x.shape
            return x.transpose(0, 2, 1, 3).reshape(b, s, h * hd)

        def global_latent_attn(x, wq, w_kv_down, w_k_up, w_v_up, wo):
            q = split_heads(x @ wq, H)
            latent = x @ w_kv_down
            k = split_heads(latent @ w_k_up, KVH)
            v = split_heads(latent @ w_v_up, KVH)
            q, k = (rope(q, BASE_G), rope(k, BASE_G))
            q, k = (qk_norm(q), qk_norm(k))
            k, v = (repeat_kv(k), repeat_kv(v))
            i = jnp.arange(x.shape[1])
            causal = i[:, None] >= i[None, :]
            return merge_heads(sdpa(q, k, v, causal)) @ wo

        def local_gqa_attn(x, wq, wk, wv, wo):
            q = split_heads(x @ wq, H)
            k = split_heads(x @ wk, KVH)
            v = split_heads(x @ wv, KVH)
            q, k = (rope(q, BASE_L), rope(k, BASE_L))
            q, k = (qk_norm(q), qk_norm(k))
            k, v = (repeat_kv(k), repeat_kv(v))
            i = jnp.arange(x.shape[1])
            diff = i[:, None] - i[None, :]
            mask = (diff >= 0) & (diff < WIN)
            return merge_heads(sdpa(q, k, v, mask)) @ wo
        key = jax.random.key(seed)
        ks = jax.random.split(key, 12)
        std = 0.02
        return {'hidden': jax.random.normal(ks[0], (B, S, D), dtype=jnp.float32), 'norm1_w': jnp.ones((D,), jnp.float32), 'norm2_w': jnp.ones((D,), jnp.float32), 'g_wq': jax.random.normal(ks[1], (D, H * HD), jnp.float32) * std, 'g_kv_down': jax.random.normal(ks[2], (D, LAT), jnp.float32) * std, 'g_k_up': jax.random.normal(ks[3], (LAT, KVH * HD), jnp.float32) * std, 'g_v_up': jax.random.normal(ks[4], (LAT, KVH * HD), jnp.float32) * std, 'g_wo': jax.random.normal(ks[5], (D, D), jnp.float32) * std, 'l_wq': jax.random.normal(ks[6], (D, H * HD), jnp.float32) * std, 'l_wk': jax.random.normal(ks[7], (D, KVH * HD), jnp.float32) * std, 'l_wv': jax.random.normal(ks[8], (D, KVH * HD), jnp.float32) * std, 'l_wo': jax.random.normal(ks[9], (D, D), jnp.float32) * std}
    _L0_attn_in = _L0_attn_setup()

    def _L0_ffn_setup():
        import jax, jax.numpy as jnp
        import numpy as np
        B, S, F, E, K = (4, 128, 128, 8, 2)
        H = 4 * F
        key = jax.random.key(seed)
        ks = jax.random.split(key, 7)

        def xavier(k, shape):
            fan_in, fan_out = (shape[-2], shape[-1])
            scale = jnp.sqrt(6.0 / (fan_in + fan_out))
            return jax.random.uniform(k, shape, jnp.float32, -scale, scale)
        return {'x': jax.random.normal(ks[0], (B, S, F), jnp.float32), 'Wg': xavier(ks[1], (F, E)), 'bg': jnp.zeros((E,), jnp.float32), 'W1': xavier(ks[2], (E, F, H)), 'b1': jnp.zeros((E, H), jnp.float32), 'W2': xavier(ks[3], (E, H, F)), 'b2': jnp.zeros((E, F), jnp.float32)}
    _L0_ffn_in = _L0_ffn_setup()

    def _L1_attn_setup():
        import jax, jax.numpy as jnp
        import numpy as np
        from jax import lax

        def _phi(x):
            return jax.nn.elu(x) + 1.0
        key = jax.random.key(seed)
        ks = jax.random.split(key, 5)
        B, T, D, H = (8, 512, 128, 64)
        x = jax.random.normal(ks[0], (B, T, D), dtype=jnp.float32)
        W_q = jax.random.normal(ks[1], (D, H), dtype=jnp.float32) * (1.0 / np.sqrt(D))
        W_k = jax.random.normal(ks[2], (D, H), dtype=jnp.float32) * (1.0 / np.sqrt(D))
        W_v = jax.random.normal(ks[3], (D, H), dtype=jnp.float32) * (1.0 / np.sqrt(D))
        W_o = jax.random.normal(ks[4], (H, D), dtype=jnp.float32) * (1.0 / np.sqrt(H))
        return {'x': x, 'W_q': W_q, 'W_k': W_k, 'W_v': W_v, 'W_o': W_o}
    _L1_attn_in = _L1_attn_setup()

    def _L1_ffn_setup():
        import jax, jax.numpy as jnp
        import numpy as np
        DIM = 128
        DEPTH = 2
        HEADS = 8
        DIM_HEAD = 64
        WINDOW = 64
        INNER = HEADS * DIM_HEAD
        HID = int(DIM * 4 * 2 / 3)
        B, N = (2, 1024)
        QK_SCALE = 8.0

        def shift_token(t):
            t1, t2 = jnp.split(t, 2, axis=-1)
            t2 = jnp.pad(t2, ((0, 0), (1, 0), (0, 0)))[:, :-1]
            return jnp.concatenate([t1, t2], axis=-1)

        def l2norm(t):
            return t / jnp.clip(jnp.linalg.norm(t, axis=-1, keepdims=True), 1e-12)

        def rotate_half(x):
            x1, x2 = jnp.split(x, 2, axis=-1)
            return jnp.concatenate([-x2, x1], axis=-1)

        def rotary_xpos(q, k):
            n = q.shape[-2]
            half_idx = jnp.arange(0, DIM_HEAD, 2, dtype=jnp.float32)
            inv_freq = 1.0 / 10000.0 ** (half_idx / DIM_HEAD)
            t = jnp.arange(n, dtype=jnp.float32)
            freqs = t[:, None] * inv_freq[None, :]
            freqs = jnp.concatenate([freqs, freqs], axis=-1)
            base = (half_idx + 0.4 * DIM_HEAD) / (1.4 * DIM_HEAD)
            power = (t - n // 2) / float(WINDOW // 2)
            scale = base[None, :] ** power[:, None]
            scale = jnp.concatenate([scale, scale], axis=-1)
            cos, sin = (jnp.cos(freqs), jnp.sin(freqs))
            q = q * cos * scale + rotate_half(q) * sin * scale
            k = k * cos / scale + rotate_half(k) * sin / scale
            return (q, k)

        def local_attention(q, k, v):
            b, h, n, d = q.shape
            w = n // WINDOW
            bq = q.reshape(b, h, w, WINDOW, d) * QK_SCALE
            bk = k.reshape(b, h, w, WINDOW, d)
            bv = v.reshape(b, h, w, WINDOW, d)

            def look_around(t):
                p = jnp.pad(t, ((0, 0), (0, 0), (1, 0), (0, 0), (0, 0)))
                return jnp.concatenate([p[:, :, :w], p[:, :, 1:]], axis=3)
            bk, bv = (look_around(bk), look_around(bv))
            bt = jnp.arange(n).reshape(w, WINDOW)
            btp = jnp.pad(bt, ((1, 0), (0, 0)), constant_values=-1)
            btk = jnp.concatenate([btp[:w], btp[1:]], axis=1)
            sim = jnp.einsum('bhwid,bhwjd->bhwij', bq, bk)
            i = bt[:, :, None]
            j = btk[:, None, :]
            mask = (i < j) | (i > j + WINDOW) | (j == -1)
            sim = jnp.where(mask, -jnp.finfo(sim.dtype).max, sim)
            attn = jax.nn.softmax(sim, axis=-1)
            out = jnp.einsum('bhwij,bhwjd->bhwid', attn, bv)
            return out.reshape(b, h, n, d)

        def _layer(x, wqkv, qs, ksc, wo, lg, lb, w1, b1, w2, b2):
            b, n, _ = x.shape
            h = shift_token(x)
            qkv = h @ wqkv
            q, k, v = jnp.split(qkv, 3, axis=-1)
            to_heads = lambda t: t.reshape(b, n, HEADS, DIM_HEAD).transpose(0, 2, 1, 3)
            q, k, v = (to_heads(q), to_heads(k), to_heads(v))
            q = l2norm(q) * qs
            k = l2norm(k) * ksc
            q, k = rotary_xpos(q, k)
            o = local_attention(q, k, v)
            o = o.transpose(0, 2, 1, 3).reshape(b, n, INNER)
            x = x + o @ wo
            h = shift_token(x)
            mu = h.mean(-1, keepdims=True)
            var = h.var(-1, keepdims=True)
            h = (h - mu) / jnp.sqrt(var + 1e-05) * lg + lb
            h = h @ w1 + b1
            a, g = jnp.split(h, 2, axis=-1)
            h = a * jax.nn.gelu(g, approximate=False)
            x = x + h @ w2 + b2
            return x
        key = jax.random.key(seed)
        ks = jax.random.split(key, 6)
        return {'x': jax.random.normal(ks[0], (B, N, DIM), jnp.float32), 'wqkv': jax.random.normal(ks[1], (DEPTH, DIM, 3 * INNER), jnp.float32) * 0.02, 'q_scale': jnp.ones((DEPTH, DIM_HEAD), jnp.float32), 'k_scale': jnp.ones((DEPTH, DIM_HEAD), jnp.float32), 'wo': jax.random.normal(ks[2], (DEPTH, INNER, DIM), jnp.float32) * 0.02, 'ln_g': jnp.ones((DEPTH, DIM), jnp.float32), 'ln_b': jnp.zeros((DEPTH, DIM), jnp.float32), 'w1': jax.random.normal(ks[3], (DEPTH, DIM, 2 * HID), jnp.float32) * 0.02, 'b1': jnp.zeros((DEPTH, 2 * HID), jnp.float32), 'w2': jax.random.normal(ks[4], (DEPTH, HID, DIM), jnp.float32) * 0.02, 'b2': jnp.zeros((DEPTH, DIM), jnp.float32)}
    _L1_ffn_in = _L1_ffn_setup()
    _d = {'L0_attn_hidden': _L0_attn_in['hidden'], 'L0_attn_norm1_w': _L0_attn_in['norm1_w'], 'L0_attn_norm2_w': _L0_attn_in['norm2_w'], 'L0_attn_g_wq': _L0_attn_in['g_wq'], 'L0_attn_g_kv_down': _L0_attn_in['g_kv_down'], 'L0_attn_g_k_up': _L0_attn_in['g_k_up'], 'L0_attn_g_v_up': _L0_attn_in['g_v_up'], 'L0_attn_g_wo': _L0_attn_in['g_wo'], 'L0_attn_l_wq': _L0_attn_in['l_wq'], 'L0_attn_l_wk': _L0_attn_in['l_wk'], 'L0_attn_l_wv': _L0_attn_in['l_wv'], 'L0_attn_l_wo': _L0_attn_in['l_wo'], 'L0_ffn_Wg': _L0_ffn_in['Wg'], 'L0_ffn_bg': _L0_ffn_in['bg'], 'L0_ffn_W1': _L0_ffn_in['W1'], 'L0_ffn_b1': _L0_ffn_in['b1'], 'L0_ffn_W2': _L0_ffn_in['W2'], 'L0_ffn_b2': _L0_ffn_in['b2'], 'L1_attn_W_q': _L1_attn_in['W_q'], 'L1_attn_W_k': _L1_attn_in['W_k'], 'L1_attn_W_v': _L1_attn_in['W_v'], 'L1_attn_W_o': _L1_attn_in['W_o'], 'L1_ffn_wqkv': _L1_ffn_in['wqkv'], 'L1_ffn_q_scale': _L1_ffn_in['q_scale'], 'L1_ffn_k_scale': _L1_ffn_in['k_scale'], 'L1_ffn_wo': _L1_ffn_in['wo'], 'L1_ffn_ln_g': _L1_ffn_in['ln_g'], 'L1_ffn_ln_b': _L1_ffn_in['ln_b'], 'L1_ffn_w1': _L1_ffn_in['w1'], 'L1_ffn_b1': _L1_ffn_in['b1'], 'L1_ffn_w2': _L1_ffn_in['w2'], 'L1_ffn_b2': _L1_ffn_in['b2']}
    _x0 = _d['L0_attn_hidden']
    _d['L0_attn_hidden'] = jax.random.normal(jax.random.fold_in(jax.random.key(seed), 1), (4, 1024, 128), dtype=_x0.dtype)
    del _x0
    return _d

def reference(L0_attn_hidden, L0_attn_norm1_w, L0_attn_norm2_w, L0_attn_g_wq, L0_attn_g_kv_down, L0_attn_g_k_up, L0_attn_g_v_up, L0_attn_g_wo, L0_attn_l_wq, L0_attn_l_wk, L0_attn_l_wv, L0_attn_l_wo, L0_ffn_Wg, L0_ffn_bg, L0_ffn_W1, L0_ffn_b1, L0_ffn_W2, L0_ffn_b2, L1_attn_W_q, L1_attn_W_k, L1_attn_W_v, L1_attn_W_o, L1_ffn_wqkv, L1_ffn_q_scale, L1_ffn_k_scale, L1_ffn_wo, L1_ffn_ln_g, L1_ffn_ln_b, L1_ffn_w1, L1_ffn_b1, L1_ffn_w2, L1_ffn_b2):

    def _L0_attn_ref(hidden, norm1_w, norm2_w, g_wq, g_kv_down, g_k_up, g_v_up, g_wo, l_wq, l_wk, l_wv, l_wo):
        import jax, jax.numpy as jnp
        import numpy as np
        D = 128
        H = 16
        KVH = 4
        HD = D // H
        LAT = 32
        WIN = 32
        B, S = (1, 256)
        BASE_G, BASE_L = (1000000.0, 10000.0)
        EPS = 1e-06

        def rmsnorm(x, w):
            return x * jax.lax.rsqrt(jnp.mean(x * x, axis=-1, keepdims=True) + EPS) * w

        def qk_norm(x):
            return x * jax.lax.rsqrt(jnp.mean(x * x, axis=-1, keepdims=True) + EPS)

        def rope(x, base):
            s, hd = (x.shape[-2], x.shape[-1])
            inv_freq = 1.0 / base ** (jnp.arange(0, hd, 2, dtype=jnp.float32) / hd)
            freqs = jnp.arange(s, dtype=jnp.float32)[:, None] * inv_freq[None, :]
            cos, sin = (jnp.cos(freqs), jnp.sin(freqs))
            xe, xo = (x[..., ::2], x[..., 1::2])
            out = jnp.stack([xe * cos - xo * sin, xe * sin + xo * cos], axis=-1)
            return out.reshape(x.shape)

        def split_heads(x, n_heads):
            b, s, _ = x.shape
            return x.reshape(b, s, n_heads, HD).transpose(0, 2, 1, 3)

        def repeat_kv(x):
            return jnp.repeat(x, H // KVH, axis=1)

        def sdpa(q, k, v, mask):
            scores = jnp.einsum('bhqd,bhkd->bhqk', q, k) / np.sqrt(HD).astype(np.float32)
            scores = jnp.where(mask, scores, jnp.float32(-1e+30))
            probs = jax.nn.softmax(scores, axis=-1)
            return jnp.einsum('bhqk,bhkd->bhqd', probs, v)

        def merge_heads(x):
            b, h, s, hd = x.shape
            return x.transpose(0, 2, 1, 3).reshape(b, s, h * hd)

        def global_latent_attn(x, wq, w_kv_down, w_k_up, w_v_up, wo):
            q = split_heads(x @ wq, H)
            latent = x @ w_kv_down
            k = split_heads(latent @ w_k_up, KVH)
            v = split_heads(latent @ w_v_up, KVH)
            q, k = (rope(q, BASE_G), rope(k, BASE_G))
            q, k = (qk_norm(q), qk_norm(k))
            k, v = (repeat_kv(k), repeat_kv(v))
            i = jnp.arange(x.shape[1])
            causal = i[:, None] >= i[None, :]
            return merge_heads(sdpa(q, k, v, causal)) @ wo

        def local_gqa_attn(x, wq, wk, wv, wo):
            q = split_heads(x @ wq, H)
            k = split_heads(x @ wk, KVH)
            v = split_heads(x @ wv, KVH)
            q, k = (rope(q, BASE_L), rope(k, BASE_L))
            q, k = (qk_norm(q), qk_norm(k))
            k, v = (repeat_kv(k), repeat_kv(v))
            i = jnp.arange(x.shape[1])
            diff = i[:, None] - i[None, :]
            mask = (diff >= 0) & (diff < WIN)
            return merge_heads(sdpa(q, k, v, mask)) @ wo
        x = hidden
        x = x + global_latent_attn(rmsnorm(x, norm1_w), g_wq, g_kv_down, g_k_up, g_v_up, g_wo)
        x = x + local_gqa_attn(rmsnorm(x, norm2_w), l_wq, l_wk, l_wv, l_wo)
        return x

    def _L0_ffn_ref(x, Wg, bg, W1, b1, W2, b2):
        import jax, jax.numpy as jnp
        import numpy as np
        B, S, F, E, K = (4, 128, 128, 8, 2)
        H = 4 * F
        gate_probs = jax.nn.softmax(x @ Wg + bg, axis=-1)
        k = K
        _, top_idx = jax.lax.top_k(gate_probs, k)
        expert_mask = jax.nn.one_hot(top_idx, gate_probs.shape[-1], dtype=gate_probs.dtype).sum(-2)
        selected = gate_probs * expert_mask
        selected = selected / (selected.sum(-1, keepdims=True) + 1e-08)
        h = jax.nn.gelu(jnp.einsum('bsf,efh->bseh', x, W1) + b1)
        expert_out = jnp.einsum('bseh,ehf->bsef', h, W2) + b2[None, None]
        return jnp.einsum('bsef,bse->bsf', expert_out, selected)

    def _L1_attn_ref(x, W_q, W_k, W_v, W_o):
        import jax, jax.numpy as jnp
        import numpy as np
        from jax import lax

        def _phi(x):
            return jax.nn.elu(x) + 1.0
        B, T, D = x.shape
        H = W_q.shape[1]
        q = _phi(jnp.einsum('btd,dh->bth', x, W_q))
        k = _phi(jnp.einsum('btd,dh->bth', x, W_k))
        v = jnp.einsum('btd,dh->bth', x, W_v)
        qT = jnp.swapaxes(q, 0, 1)
        kT = jnp.swapaxes(k, 0, 1)
        vT = jnp.swapaxes(v, 0, 1)
        S0 = jnp.zeros((B, H, H), dtype=x.dtype)
        z0 = jnp.zeros((B, H), dtype=x.dtype)

        def step(carry, inp):
            S, z = carry
            q_t, k_t, v_t = inp
            S = S + k_t[:, :, None] * v_t[:, None, :]
            z = z + k_t
            o_t = jnp.einsum('bij,bj->bi', S, q_t)
            denom = jnp.maximum(jnp.sum(z * q_t, axis=-1, keepdims=True), 1e-06)
            return ((S, z), o_t / denom)
        (_, _), oT = lax.scan(step, (S0, z0), (qT, kT, vT))
        o = jnp.swapaxes(oT, 0, 1)
        return jnp.einsum('bth,hd->btd', o, W_o)

    def _L1_ffn_ref(x, wqkv, q_scale, k_scale, wo, ln_g, ln_b, w1, b1, w2, b2):
        import jax, jax.numpy as jnp
        import numpy as np
        DIM = 128
        DEPTH = 2
        HEADS = 8
        DIM_HEAD = 64
        WINDOW = 64
        INNER = HEADS * DIM_HEAD
        HID = int(DIM * 4 * 2 / 3)
        B, N = (2, 1024)
        QK_SCALE = 8.0

        def shift_token(t):
            t1, t2 = jnp.split(t, 2, axis=-1)
            t2 = jnp.pad(t2, ((0, 0), (1, 0), (0, 0)))[:, :-1]
            return jnp.concatenate([t1, t2], axis=-1)

        def l2norm(t):
            return t / jnp.clip(jnp.linalg.norm(t, axis=-1, keepdims=True), 1e-12)

        def rotate_half(x):
            x1, x2 = jnp.split(x, 2, axis=-1)
            return jnp.concatenate([-x2, x1], axis=-1)

        def rotary_xpos(q, k):
            n = q.shape[-2]
            half_idx = jnp.arange(0, DIM_HEAD, 2, dtype=jnp.float32)
            inv_freq = 1.0 / 10000.0 ** (half_idx / DIM_HEAD)
            t = jnp.arange(n, dtype=jnp.float32)
            freqs = t[:, None] * inv_freq[None, :]
            freqs = jnp.concatenate([freqs, freqs], axis=-1)
            base = (half_idx + 0.4 * DIM_HEAD) / (1.4 * DIM_HEAD)
            power = (t - n // 2) / float(WINDOW // 2)
            scale = base[None, :] ** power[:, None]
            scale = jnp.concatenate([scale, scale], axis=-1)
            cos, sin = (jnp.cos(freqs), jnp.sin(freqs))
            q = q * cos * scale + rotate_half(q) * sin * scale
            k = k * cos / scale + rotate_half(k) * sin / scale
            return (q, k)

        def local_attention(q, k, v):
            b, h, n, d = q.shape
            w = n // WINDOW
            bq = q.reshape(b, h, w, WINDOW, d) * QK_SCALE
            bk = k.reshape(b, h, w, WINDOW, d)
            bv = v.reshape(b, h, w, WINDOW, d)

            def look_around(t):
                p = jnp.pad(t, ((0, 0), (0, 0), (1, 0), (0, 0), (0, 0)))
                return jnp.concatenate([p[:, :, :w], p[:, :, 1:]], axis=3)
            bk, bv = (look_around(bk), look_around(bv))
            bt = jnp.arange(n).reshape(w, WINDOW)
            btp = jnp.pad(bt, ((1, 0), (0, 0)), constant_values=-1)
            btk = jnp.concatenate([btp[:w], btp[1:]], axis=1)
            sim = jnp.einsum('bhwid,bhwjd->bhwij', bq, bk)
            i = bt[:, :, None]
            j = btk[:, None, :]
            mask = (i < j) | (i > j + WINDOW) | (j == -1)
            sim = jnp.where(mask, -jnp.finfo(sim.dtype).max, sim)
            attn = jax.nn.softmax(sim, axis=-1)
            out = jnp.einsum('bhwij,bhwjd->bhwid', attn, bv)
            return out.reshape(b, h, n, d)

        def _layer(x, wqkv, qs, ksc, wo, lg, lb, w1, b1, w2, b2):
            b, n, _ = x.shape
            h = shift_token(x)
            qkv = h @ wqkv
            q, k, v = jnp.split(qkv, 3, axis=-1)
            to_heads = lambda t: t.reshape(b, n, HEADS, DIM_HEAD).transpose(0, 2, 1, 3)
            q, k, v = (to_heads(q), to_heads(k), to_heads(v))
            q = l2norm(q) * qs
            k = l2norm(k) * ksc
            q, k = rotary_xpos(q, k)
            o = local_attention(q, k, v)
            o = o.transpose(0, 2, 1, 3).reshape(b, n, INNER)
            x = x + o @ wo
            h = shift_token(x)
            mu = h.mean(-1, keepdims=True)
            var = h.var(-1, keepdims=True)
            h = (h - mu) / jnp.sqrt(var + 1e-05) * lg + lb
            h = h @ w1 + b1
            a, g = jnp.split(h, 2, axis=-1)
            h = a * jax.nn.gelu(g, approximate=False)
            x = x + h @ w2 + b2
            return x
        for l in range(DEPTH):
            x = _layer(x, wqkv[l], q_scale[l], k_scale[l], wo[l], ln_g[l], ln_b[l], w1[l], b1[l], w2[l], b2[l])
        return x
    x = L0_attn_hidden
    x = _layernorm(x + _L0_attn_ref(x, L0_attn_norm1_w, L0_attn_norm2_w, L0_attn_g_wq, L0_attn_g_kv_down, L0_attn_g_k_up, L0_attn_g_v_up, L0_attn_g_wo, L0_attn_l_wq, L0_attn_l_wk, L0_attn_l_wv, L0_attn_l_wo), axis=-1)
    x = _layernorm(x + _L0_ffn_ref(x, L0_ffn_Wg, L0_ffn_bg, L0_ffn_W1, L0_ffn_b1, L0_ffn_W2, L0_ffn_b2), axis=-1)
    x = _layernorm(x + _L1_attn_ref(x, L1_attn_W_q, L1_attn_W_k, L1_attn_W_v, L1_attn_W_o), axis=-1)
    x = _layernorm(x + _L1_ffn_ref(x, L1_ffn_wqkv, L1_ffn_q_scale, L1_ffn_k_scale, L1_ffn_wo, L1_ffn_ln_g, L1_ffn_ln_b, L1_ffn_w1, L1_ffn_b1, L1_ffn_w2, L1_ffn_b2), axis=-1)
    return x

_drawn_inputs = setup_inputs


def setup_inputs(seed=0):
    import zlib

    import numpy as np

    out = dict(_drawn_inputs(seed))
    spreads = {'L0_attn_norm1_w': (1.0, 0.6),
     'L0_attn_norm2_w': (1.0, 0.6),
     'L0_ffn_bg': (0.0, 0.1),
     'L0_ffn_b1': (0.0, 0.1),
     'L0_ffn_b2': (0.0, 0.1),
     'L1_ffn_q_scale': (1.0, 0.6),
     'L1_ffn_k_scale': (1.0, 0.6),
     'L1_ffn_ln_g': (1.0, 0.6),
     'L1_ffn_ln_b': (0.0, 0.8),
     'L1_ffn_b1': (0.0, 0.8),
     'L1_ffn_b2': (0.0, 0.525)}
    factors = {'L0_attn_g_wq': 8.0,
     'L0_attn_g_kv_down': 8.0,
     'L0_attn_g_k_up': 8.0,
     'L0_attn_g_v_up': 8.0,
     'L0_attn_g_wo': 8.0,
     'L0_attn_l_wq': 3.746,
     'L0_attn_l_wk': 3.538,
     'L0_attn_l_wv': 2.907,
     'L0_attn_l_wo': 3.008,
     'L1_attn_W_q': 5.258,
     'L1_attn_W_k': 5.702,
     'L1_attn_W_v': 3.098,
     'L1_attn_W_o': 3.431,
     'L1_ffn_wqkv': 3.718,
     'L1_ffn_wo': 3.656,
     'L1_ffn_w1': 6.62,
     'L1_ffn_w2': 6.472}
    for name, (base, spread) in spreads.items():
        noise = np.random.default_rng([zlib.crc32(name.encode()), seed]).standard_normal(out[name].shape)
        drawn = base * np.exp(spread * noise) if base else spread * noise
        out[name] = jnp.asarray(drawn.astype(out[name].dtype))
    for name, factor in factors.items():
        out[name] = (out[name] * factor).astype(out[name].dtype)
    return out
```

```python
import numpy as np
import concourse.bass as bass
from concourse import mybir
from concourse.alu_op_type import AluOpType as ALU
from contextlib import ExitStack

ACT = mybir.ActivationFunctionType
AX = mybir.AxisListType.X
F32, F16, BF16, I32 = mybir.dt.float32, mybir.dt.float16, mybir.dt.bfloat16, mybir.dt.int32

B, S, D = 4, 1024, 128
NT = S // 128
H, KV, HD = 16, 4, 8
GQ = H // KV
LAT = 32
WIN = 32
PAD = WIN
E, HF = 8, 512
HC = HF // 128
HL = 64
NH, DH, W2 = 8, 64, 64
INNER = NH * DH
DEPTH = 2
HID = int(D * 4 * 2 / 3)
CH = [(c * 128, min(128, HID - c * 128)) for c in range((HID + 127) // 128)]
PRING = 6
INV_SQRT_HD = 1.0 / float(np.sqrt(np.float32(HD)))


def constant_tables():
    f = np.float32
    t = {}
    t["c_ident"] = np.eye(128, dtype=f)
    k, q = np.arange(128)[None, :], np.arange(128)[:, None]
    t["c_causal"] = np.where(k > q, -30000.0, 0.0).astype(np.float16)
    loc = np.zeros((128, 128), np.float16)
    kk = np.arange(64)[None, :]
    qq = np.arange(WIN)[:, None]
    ok = (kk <= qq + WIN) & (qq + WIN - kk < WIN)
    loc[:WIN] = np.tile(np.where(ok, 0.0, -30000.0), (1, 2))
    t["c_local"] = loc
    t["c_tri"] = (np.arange(128)[:, None] <= np.arange(128)[None, :]).astype(f)
    jl = np.arange(128)[:, None]
    il = np.arange(64)[None, :]
    ok = (il <= jl) & (jl <= il + W2)
    m = np.tile(np.where(ok, 0.0, -1e30), (1, 2)).astype(f)
    first = m.copy()
    first[:64, :64] = -1e30
    t["c_win"] = np.stack([first, m], 1)
    for name, base in (("g", 1000000.0), ("l", 10000.0)):
        inv = (f(1.0) / (f(base) ** (np.arange(0, HD, 2, dtype=f) / f(HD)))).astype(f)
        fr = (np.arange(S, dtype=f)[:, None] * inv[None, :]).astype(f)
        c, s = np.cos(fr), np.sin(fr)
        tab = np.stack([np.repeat(c, 2, axis=1), np.stack([-s, s], -1).reshape(S, HD)], 1)
        t["c_rope_" + name] = np.ascontiguousarray(tab.reshape(NT, 128, 2, HD).transpose(1, 0, 2, 3)).astype(f)
    half = np.arange(0, DH, 2, dtype=f)
    inv = (f(1.0) / (f(10000.0) ** (half / f(DH)))).astype(f)
    pos = np.arange(S, dtype=f)
    fr = (pos[:, None] * inv[None, :]).astype(f)
    base = ((half + f(0.4 * DH)) / f(1.4 * DH)).astype(f)
    power = ((pos - f(S // 2)) / f(W2 // 2)).astype(f)
    sc = (base[None, :] ** power[:, None]).astype(f)
    c, s = np.cos(fr), np.sin(fr)
    cc, ss, scc = (np.concatenate([a, a], 1) for a in (c, s, sc))
    sg = np.concatenate([-ss[:, :DH // 2], ss[:, DH // 2:]], 1)
    tab = np.stack([np.stack([cc * scc, cc / scc], 1), np.stack([sg * scc, sg / scc], 1)], 1)
    t["c_xpos"] = np.ascontiguousarray(tab.reshape(NT, 128, 2, 2, DH).transpose(1, 0, 2, 3, 4)).astype(f)
    return t


class Tickets:

    def __init__(self):
        self.at, self.used, self.next = {}, {}, {"D": 0, "H": 0}
        self.size = {"D": 3, "H": 2}

    def add(self, kind, *key):
        k = self.next[kind] % self.size[kind]
        self.next[kind] += 1
        n = self.used.get((kind, k), 0)
        self.used[(kind, k)] = n + 1
        assert key not in self.at, key
        self.at[key] = (kind, k, n)


def to_t_count():
    return 4 + 4 * DEPTH


def attention_units(a, half):
    if a == 0:
        return [(g, kc, jp) for g in range(KV) for kc in range(4 * half + 4) for jp in range(2)]
    return [(g,) for g in range(KV)]


def plan():
    t = Tickets()
    for a in range(2):
        t.add("D", "toT", a)
        for i in range(2):
            t.add("D", "qkv", a, i)
        if a == 1:
            t.add("D", "vwin")
        for i in range(2):
            t.add("D", "qT", a, i)
        for i in range(2):
            t.add("D", "kT", a, i)
        for half in range(2):
            units = attention_units(a, half)
            if a == 0:
                for u in units:
                    t.add("D", "S", a, half, *u)
                for g in range(KV):
                    t.add("H", "O", a, half, g)
                for i in range(2):
                    t.add("D", "Ot", a, half, i)
            else:
                for u in units:
                    t.add("D", "S", a, half, *u)
                t.add("D", "O", a, half)
                t.add("D", "Ot", a, half, 0)
            t.add("H", "At", a, half)
            t.add("H", "wo", a, half)
    t.add("D", "toT", 2)
    t.add("H", "gate")
    for i in range(2 * E + 1):
        if i < 2 * E:
            t.add("D", "h", i, 0)
            t.add("D", "h", i, 1)
        if i > 0:
            t.add("H", "eo", i - 1)
    t.add("D", "GT")
    t.add("D", "b2")
    t.add("D", "toT", 3)
    for n in ("lq", "lk", "lkv", "lv"):
        t.add("D", n)
    t.add("H", "lM")
    for n in ("ls", "lo", "loT", "lwo"):
        t.add("D", n)
    for l in range(DEPTH):
        t.add("D", "toT", 4 + 4 * l)
        for i in range(NT + 3):
            if 0 <= i - 1 < NT:
                t.add("D", "fT", l, i - 1)
            if i < NT:
                t.add("D", "fqk", l, i)
                t.add("H", "fv", l, i)
            if 0 <= i - 3 < NT:
                t.add("H", "fOT", l, i - 3)
            if 0 <= i - 2 < NT:
                t.add("D", "fPT", l, i - 2)
            if 0 <= i - 1 < NT:
                t.add("D", "fS", l, i - 1)
            if 0 <= i - 2 < NT:
                t.add("H", "fO", l, i - 2)
            if i - 3 in (3, 7):
                t.add("H", "fwo", l, (i - 3) // 4)
        for i in range(1, 4):
            t.add("D", "toT", 4 + 4 * l + i)
        for hb in range(2):
            for c in range(len(CH)):
                t.add("D", "fw1", l, hb, c)
            t.add("H", "fw2", l, hb)
    return t


def build(nc, A):
    tk = plan()
    ctx = ExitStack()
    with ctx:
        def sb(name, shape, dt=F32):
            return ctx.enter_context(nc.sbuf_tensor(name, shape, dt))

        ident = sb("ident", [128, 128])
        ident16 = sb("ident16", [128, 128], F16)
        causal = sb("causal", [128, 128], F16)
        local = sb("local", [128, 128], F16)
        identb = sb("identb", [128, 128], BF16)
        win = sb("win", [128, 2, 128], BF16)
        tri = sb("tri", [128, 128])
        ones = sb("ones", [128, 1])
        rope = [sb(f"rope{a}", [128, NT, 2, HD]) for a in range(2)]
        w_att = [sb("w_global", [128, 192]), sb("w_local", [128, 192])]
        w_ao = [sb("wo_global", [128, 128]), sb("wo_local", [128, 128])]
        wgate = sb("wgate", [128, E])
        bgate = sb("bgate", [128, E])
        rank = sb("rank", [128, E])
        W1 = sb("W1", [128, E, HF])
        b1 = sb("b1", [128, E, HC])
        W2m = sb("W2m", [128, E, HC, 128])
        b2m = sb("b2m", [E, 128])
        lw = sb("lw", [128, 3, HL])
        lwo = sb("lwo", [HL, 128])
        wqkv = sb("wqkv", [128, DEPTH, 3 * INNER])
        wo = sb("wo", [128, DEPTH, 4, 128])
        w1 = sb("w1", [128, DEPTH, 2 * HID])
        fb1 = sb("fb1", [128, DEPTH, 2, len(CH)])
        w2 = sb("w2", [128, DEPTH, len(CH), 128])
        xpos = sb("xpos", [128, DEPTH, NT, 2, 2, DH])

        X = sb("X", [128, NT, 128])
        R = sb("R", [128, NT, 128])
        N = sb("N", [128, NT, 128])
        Q = sb("Q", [128, NT, 128])
        xT = sb("xT", [128, PAD + S])
        hT = sb("hT", [128, S])
        st_a = sb("st_a", [128, 160])
        st_m = sb("st_m", [128, 160])
        st_i = sb("st_i", [128, 160], I32)
        st_y = sb("st_y", [128, 160])
        st_t = sb("st_t", [128, 160])
        rden = sb("rden", [128, 64])
        gates = sb("gates", [128, NT, E])
        gtmp = [sb(f"gtmp{i}", [128, NT, E]) for i in range(4)]
        gone = [sb(f"gone{i}", [128, NT]) for i in range(3)]

        arena_bytes = 97 * 1024
        arena = sb("arena", [128, arena_bytes // 4])
        cursor = [0]

        def carve(shape, dt=F32):
            n = int(np.prod(shape[1:]))
            size = {F32: 4, F16: 2}[dt]
            words = (n * size + 31) // 32 * 8
            v = arena[0:shape[0], cursor[0]:cursor[0] + words]
            if dt is F16:
                v = v.bitcast(F16)
            v = v[:, 0:n]
            cursor[0] += words
            assert cursor[0] * 4 <= arena_bytes, cursor[0] * 4
            names = "abcde"[:len(shape) - 1]
            if len(shape) > 2:
                v = v.rearrange(f"p ({' '.join(names)}) -> p {' '.join(names)}", **{c: s for c, s in zip(names[1:], shape[2:])})
            return v

        cursor[0] = 0
        QK = carve([128, NT, 160])
        QR = carve([128, NT, 160])
        Qs = carve([128, NT, GQ, 4, 32], F16)
        arena_rope = carve([128, NT, 160])
        QT = carve([128, GQ, S], F16)
        KT = carve([128, KV, PAD + S], F16)
        P = [carve([128, 1024]) for _ in range(PRING)]
        OT = carve([128, KV, 512])
        At = carve([128, NT // 2, 128])
        AT = carve([128, 512])
        Kpad = carve([128, NT, KV, 4, KV, HD], F16)
        Vaug = carve([128, NT, KV, 32])
        Vwin = carve([128, 16, KV, 2, 16])

        cursor[0] = 0
        hbuf = [carve([128, HC, 512]) for _ in range(3)]
        GT = carve([E, S])

        cursor[0] = 0
        lqT, lkT, lvT, lz, lqz = (carve([HL, S]) for _ in range(5))
        lm = [carve([128, S]) for _ in range(3)]
        lone = carve([HL, S])
        lkt = carve([128, NT, HL])
        lvt = carve([128, NT, HL])
        lM = carve([HL, NT, HL])
        lA = carve([128, NT, 128])
        lO = carve([128, NT, HL])
        lOT = carve([HL, S])

        cursor[0] = 0
        QKs = carve([128, 2, 16, DH])
        SQb = carve([128, 16, DH])
        T1 = [carve([128, 16, DH]) for _ in range(2)]
        T2 = carve([128, 16, DH])
        fqT = [carve([128, 4, 128]) for _ in range(2)]
        fkT = [carve([128, 4, 192]) for _ in range(2)]
        V = [carve([128, INNER]) for _ in range(5)]
        Vsh = [carve([128, INNER]) for _ in range(5)]
        fP = [carve([128, NH, 128]) for _ in range(2)]
        fPT = [carve([128, NH, 128]) for _ in range(1)]
        fO = [carve([128, INNER]) for _ in range(1)]
        fOT = carve([128, 4, 512])
        U = carve([128, 3, 512])
        GL = [T1[i].rearrange("p a b -> p (a b)")[:, 0:512] for i in range(2)]

        fss = sb("fss", [128, 16])
        fm = sb("fm", [128, 2, 16])
        fi = sb("fi", [128, 16], I32)
        fy = sb("fy", [128, 2, 16])
        ft = sb("ft", [128, 16])
        frq = sb("frq", [128, 4, NH])
        fnm = sb("fnm", [128, 2, NH])
        fden = sb("fden", [128, 2, NH])
        frd = sb("frd", [128, 2, NH])

        PD = [ctx.enter_context(nc.psum_tensor(f"PD{i}", [128, 1024], F32)) for i in range(3)]
        PH = [ctx.enter_context(nc.psum_tensor(f"PH{i}", [128, 512], F32)) for i in range(2)]

        sems = {}

        def sg(name):
            if name not in sems:
                sems[name] = ctx.enter_context(nc.semaphore("s_" + name))
            return sems[name]

        def slot(*key):
            kind, k, n = tk.at[key]
            return (PD if kind == "D" else PH)[k]

        def fill(pe, *key):
            kind, k, n = tk.at[key]
            if n:
                pe.wait_ge(sg(f"free_{kind}{k}"), n)
            return (PD if kind == "D" else PH)[k][:, :]

        def filled(*key):
            kind, k, n = tk.at[key]
            return sg(f"full_{kind}{k}")

        def read(eng, *key):
            kind, k, n = tk.at[key]
            eng.wait_ge(sg(f"full_{kind}{k}"), n + 1)
            return (PD if kind == "D" else PH)[k][:, :]

        def freed(*key):
            kind, k, n = tk.at[key]
            return sg(f"free_{kind}{k}")

        def spread(ap):
            return ap.rearrange("p (T u w q) -> p T w u q", T=4, u=4, w=2)

        raw = {}
        cursor[0] = 0
        for n, shape in (("g_wq", [128, 128]), ("g_kv_down", [128, LAT]), ("l_wq", [128, 128]), ("l_wk", [128, 32]),
                         ("l_wv", [128, 32]), ("n1", [128, 1]), ("n2", [128, 1]), ("up", [LAT, 64]), ("downT", [LAT, 128]),
                         ("lg", [128, DEPTH]), ("lb", [128, DEPTH]), ("b1c", [128, DEPTH, 2, len(CH)]),
                         ("w1", [128, DEPTH, 2 * HID]), ("qs", [128, DEPTH, 2, DH]), ("xp", [128, NT, 2, 2, DH]),
                         ("win", [128, 2, 128]), ("identf", [128, 128])):
            raw[n] = carve(shape)

        loads = []

        def ld(dst, src):
            loads.append((dst, src))

        ld(ident[:, :], A["c_ident"])
        ld(causal[:, :], A["c_causal"])
        ld(local[:, :], A["c_local"])
        ld(raw["win"], A["c_win"])
        ld(tri[:, :], A["c_tri"])
        ld(rope[0][:, :, :, :], A["c_rope_g"])
        ld(rope[1][:, :, :, :], A["c_rope_l"])
        ld(raw["xp"], A["c_xpos"])
        ld(raw["g_wq"], A["L0_attn_g_wq"])
        ld(raw["g_kv_down"], A["L0_attn_g_kv_down"])
        ld(raw["up"][:, 0:32], A["L0_attn_g_k_up"])
        ld(raw["up"][:, 32:64], A["L0_attn_g_v_up"])
        ld(raw["l_wq"], A["L0_attn_l_wq"])
        ld(raw["l_wk"], A["L0_attn_l_wk"])
        ld(raw["l_wv"], A["L0_attn_l_wv"])
        ld(raw["n1"], A["L0_attn_norm1_w"].rearrange("(p a) -> p a", a=1))
        ld(raw["n2"], A["L0_attn_norm2_w"].rearrange("(p a) -> p a", a=1))
        ld(w_ao[0][:, :], A["L0_attn_g_wo"])
        ld(w_ao[1][:, :], A["L0_attn_l_wo"])
        ld(wgate[:, :], A["L0_ffn_Wg"])
        ld(bgate[:, :], A["L0_ffn_bg"].partition_broadcast(128))
        ld(rank[:, :], A["c_rank"].partition_broadcast(128))
        for e in range(E):
            ld(W1[:, e, :], A["L0_ffn_W1"][e])
            ld(W2m[:, e, :, :], A["L0_ffn_W2"][e].rearrange("(c p) f -> p c f", p=128))
        ld(b1[:, :, :], A["L0_ffn_b1"])
        ld(b2m[:, :], A["L0_ffn_b2"])
        for i, n in enumerate(("L1_attn_W_q", "L1_attn_W_k", "L1_attn_W_v")):
            ld(lw[:, i, :], A[n])
        ld(lwo[:, :], A["L1_attn_W_o"])
        for l in range(DEPTH):
            ld(wqkv[:, l, :], A["L1_ffn_wqkv"][l])
            ld(wo[:, l, :, :], A["L1_ffn_wo"][l].rearrange("(c p) f -> p c f", p=128))
            ld(raw["w1"][:, l, :], A["L1_ffn_w1"][l])
            for c, (c0, m) in enumerate(CH):
                ld(w2[0:m, l, c, :], A["L1_ffn_w2"][l][c0:c0 + m, :])
                for i in range(2):
                    ld(raw["b1c"][0:m, l, i, c:c + 1],
                       A["L1_ffn_b1"][l][i * HID + c0:i * HID + c0 + m].rearrange("(p a) -> p a", a=1))
            ld(w2[CH[-1][1]:CH[-1][1] + 1, l, len(CH) - 1, :], A["L1_ffn_b2"][l:l + 1, :])
            ld(raw["lg"][:, l:l + 1], A["L1_ffn_ln_g"][l].rearrange("(p a) -> p a", a=1))
            ld(raw["lb"][:, l:l + 1], A["L1_ffn_ln_b"][l].rearrange("(p a) -> p a", a=1))
            ld(raw["qs"][:, l, 0, :], A["L1_ffn_q_scale"][l].partition_broadcast(128))
            ld(raw["qs"][:, l, 1, :], A["L1_ffn_k_scale"][l].partition_broadcast(128))

        with nc.Block() as block:
            @block.sync
            def _(sp):
                for dst, src in loads:
                    sp.dma_start(dst, src).then_inc(sg("weights"), 16)

            @block.gpsimd
            def _(pool):
                pool.memset(xT[:, 0:PAD], 0.0)
                pool.memset(hT[:, :], 0.0)
                pool.memset(ones[:, :], 1.0)

            @block.vector
            def _(dve):
                dve.wait_ge(sg("weights"), 16 * len(loads))
                dve.tensor_copy(ident16[:, :], ident[:, :])
                dve.tensor_copy(identb[:, :], ident[:, :])
                dve.tensor_copy(win[:, :, :], raw["win"])
                dve.tensor_scalar(w_att[0][:, 0:128], raw["g_wq"], raw["n1"][:, 0:1], None, ALU.mult)
                dve.tensor_scalar(w_att[1][:, 0:128], raw["l_wq"], raw["n2"][:, 0:1], None, ALU.mult)
                dve.tensor_scalar(w_att[1][:, 128:160], raw["l_wk"], raw["n2"][:, 0:1], None, ALU.mult)
                dve.tensor_scalar(w_att[1][:, 160:192], raw["l_wv"], raw["n2"][:, 0:1], None, ALU.mult)
                for l in range(DEPTH):
                    dve.tensor_scalar(w1[:, l, :], raw["w1"][:, l, :], raw["lg"][:, l:l + 1], None, ALU.mult)
                    for i in range(2):
                        qs = raw["qs"][:, l, i:i + 1, :]
                        dve.tensor_tensor(xpos[:, l, :, 0, i, :], raw["xp"][:, :, 0, i, :],
                                          qs.to_broadcast([128, NT, DH]), ALU.mult)
                        for hh in range(2):
                            a, b = 32 * hh, 32 * (1 - hh)
                            dve.tensor_tensor(xpos[:, l, :, 1, i, a:a + 32], raw["xp"][:, :, 1, i, a:a + 32],
                                              qs[:, :, b:b + 32].to_broadcast([128, NT, 32]), ALU.mult)
                dve.wait_ge(sg("w_down"), 1)
                dve.tensor_copy(raw["downT"], PH[0][0:LAT, 0:128]).then_inc(sg("w_downT"), 1)
                dve.wait_ge(sg("w_kv"), 1)
                dve.tensor_scalar(w_att[0][:, 128:192], PD[0][:, 0:64], raw["n1"][:, 0:1], None, ALU.mult)
                for l in range(DEPTH):
                    for i in range(2):
                        for c, (c0, m) in enumerate(CH):
                            k = (l * 2 + i) * len(CH) + c
                            dve.tensor_tensor(fb1[0:m, l, i, c:c + 1], PD[1][0:m, k:k + 1],
                                              raw["b1c"][0:m, l, i, c:c + 1], ALU.add)

            @block.tensor
            def _(pe):
                pe.wait_ge(sg("weights"), 16 * len(loads))
                pe.transpose(PH[0][0:LAT, 0:128], raw["g_kv_down"], ident[:, :]).then_inc(sg("w_down"), 1)
                for l in range(DEPTH):
                    for i in range(2):
                        for c, (c0, m) in enumerate(CH):
                            k = (l * 2 + i) * len(CH) + c
                            pe.matmul(PD[1][0:m, k:k + 1], raw["w1"][:, l, i * HID + c0:i * HID + c0 + m],
                                      raw["lb"][:, l:l + 1], start=True, stop=True)
                pe.wait_ge(sg("w_downT"), 1)
                pe.matmul(PD[0][:, 0:64], raw["downT"], raw["up"], start=True, stop=True).then_inc(sg("w_kv"), 1)

        x_in, x_out = A["L0_attn_hidden"], A["out"]
        with nc.Fori(0, B) as b:
            with nc.Block() as block:
                @block.sync
                def _(sp):
                    src = x_in[bass.ds(b, 1)].rearrange("b (T u w q) d -> (b u) q T w d", T=4, u=4, w=2)
                    dst = x_out[bass.ds(b, 1)].rearrange("b (T u w q) d -> (b u) q T w d", T=4, u=4, w=2)
                    Xv = X[:, :, :].rearrange("p (T w) d -> p T w d", w=2)
                    Nv = N[:, :, :].rearrange("p (T w) d -> p T w d", w=2)
                    for u in range(4):
                        for T in range(4):
                            sp.dma_start(Xv[32 * u:32 * u + 32, T], src[u, :, T]).then_inc(sg("x_in"), 16)
                    for l in range(DEPTH):
                        for t in range(NT):
                            i = l * NT + t
                            sp.wait_ge(sg("v_tile"), i + 1)
                            if i >= 5:
                                kind, k, n = tk.at[("fO", (i - 5) // NT, (i - 5) % NT)]
                                sp.wait_ge(sg(f"full_{kind}{k}"), n + 1)
                            if t > 0:
                                sp.dma_start(Vsh[i % 5][0:64, :], V[(i - 1) % 5][64:128, :]).then_inc(sg(f"v_shift{i % 5}"), 16)
                            else:
                                sp.dma_start(Vsh[i % 5][0:64, :], V[i % 5][0:64, :]).then_inc(sg(f"v_shift{i % 5}"), 16)
                            sp.dma_start(Vsh[i % 5][64:128, :], V[i % 5][0:64, :]).then_inc(sg(f"v_shift{i % 5}"), 16)
                    sp.wait_ge(sg("final"), 1)
                    for u in range(4):
                        for T in range(4):
                            sp.dma_start(dst[u, :, T], Nv[32 * u:32 * u + 32, T]).then_inc(sg("x_out"), 16)
                    sp.wait_ge(sg("x_out"), 256)

                @block.tensor
                def _(pe):
                    def by_tiles(p, t):
                        v = p.rearrange("p (T w u q) -> p T u w q", T=4, w=2, u=4)
                        return v[:, t // 2, 2 * (t % 2):2 * (t % 2) + 2]

                    def to_t(i, src, place):
                        pe.wait_ge(sg("src"), i + 1)
                        p = fill(pe, "toT", i)
                        for t in range(NT):
                            ins = pe.transpose(place(p, t), src[:, t, :], ident[:, :])
                        ins.then_inc(filled("toT", i), 1)

                    def in_order(p, t):
                        return spread(p)[:, t // 2, t % 2]

                    def as_is(p, t):
                        return p[:, 128 * t:128 * t + 128]

                    nP = 0
                    for a in range(2):
                        to_t(a, N, in_order)
                        pe.wait_ge(sg("xT"), a + 1)
                        nq = 192 if a == 0 else 160
                        for i in range(2):
                            p = fill(pe, "qkv", a, i).rearrange("p (t n) -> p t n", t=4)
                            for t in range(4):
                                c = PAD + 128 * (4 * i + t)
                                ins = pe.matmul(p[:, t, 0:nq], xT[:, c:c + 128], w_att[a][:, 0:nq], start=True, stop=True)
                            ins.then_inc(filled("qkv", a, i), 1)
                        if a == 1:
                            p = fill(pe, "vwin").rearrange("p (u n) -> p u n", u=16)
                            for u in range(16):
                                for w in range(2):
                                    c = 64 * u + 32 * w
                                    ins = pe.matmul(p[64 * w:64 * w + 64, u, 0:32], xT[:, c:c + 64], w_att[1][:, 160:192],
                                                    start=True, stop=True)
                            ins.then_inc(filled("vwin"), 1)
                        pe.wait_ge(sg("split"), a + 1)
                        for i in range(2):
                            p = fill(pe, "qT", a, i).bitcast(F16).rearrange("p (j n) -> p j n", j=2)
                            for j in range(2):
                                for t in range(NT):
                                    src = Qs[:, t, 2 * i + j].rearrange("p s n -> p (s n)")
                                    ins = pe.transpose(p[:, j, 128 * t:128 * t + 128], src, ident16[:, :])
                            ins.then_inc(filled("qT", a, i), 1)
                        for i in range(2):
                            p = fill(pe, "kT", a, i).bitcast(F16).rearrange("p (j n) -> p j n", j=2)
                            for j in range(2):
                                for t in range(NT):
                                    src = Kpad[:, t, 2 * i + j].rearrange("p s g d -> p (s g d)")
                                    ins = pe.transpose(p[:, j, 128 * t:128 * t + 128], src, ident16[:, :])
                            ins.then_inc(filled("kT", a, i), 1)
                        pe.wait_ge(sg("QT"), 2 * a + 2)
                        pe.wait_ge(sg("KT"), 2 * a + 2)
                        pe.wait_ge(sg("V"), a + 1)
                        for half in range(2):
                            if a == 0:
                                units = attention_units(0, half)
                                ready = []

                                def values(g, kc, first):
                                    kcs = 4 * half + 4
                                    n = min(512, 512 - 128 * (kc - 4 * half))
                                    o = slot("O", 0, half, g)
                                    if kc == 0:
                                        fill(pe, "O", 0, half, g)
                                    pe.wait_ge(sg("P"), first + 2)
                                    for j in range(4):
                                        pb = P[(first + j // 2) % PRING].rearrange("p (j n) -> p j n", j=2)
                                        ins = pe.matmul(o[32 * j:32 * j + 32, 512 - n:512], Vaug[:, kc, g, :],
                                                        pb[:, j % 2, 0:n], start=(kc == 0), stop=(kc == kcs - 1),
                                                        skip_group_check=True)
                                        if j % 2 and not (j == 3 and kc == kcs - 1):
                                            ins.then_inc(sg("pv"), 1)
                                    if kc == kcs - 1:
                                        ins.then_inc(filled("O", 0, half, g), 1)

                                lag = None
                                for (g, kc, jp) in units:
                                    if jp == 0:
                                        first = nP
                                    n = min(512, 512 - 128 * (kc - 4 * half))
                                    p = fill(pe, "S", 0, half, g, kc, jp).rearrange("p (j n) -> p j n", j=2)
                                    q0 = 512 * half + 512 - n
                                    for j in range(2):
                                        diag = kc >= 4 * half
                                        c = PAD + 128 * kc
                                        if diag:
                                            pe.matmul(p[:, j, 0:128], causal[:, :], ident16[:, :],
                                                      start=True, stop=False, skip_group_check=True)
                                        ins = pe.matmul(p[:, j, 0:n], KT[:, g, c:c + 128], QT[:, 2 * jp + j, q0:q0 + n],
                                                        start=not diag, stop=True, skip_group_check=True)
                                    ins.then_inc(filled("S", 0, half, g, kc, jp), 1)
                                    nP += 1
                                    if jp == 1:
                                        if lag is not None:
                                            values(*lag)
                                        lag = (g, kc, first)
                                values(*lag)
                                for i in range(2):
                                    p = fill(pe, "Ot", 0, half, i).rearrange("p (g t n) -> p g t n", g=2, t=4)
                                    for gg in range(2):
                                        g = 2 * i + gg
                                        pe.wait_ge(sg("OT"), 4 * half + g + 1)
                                        for t in range(4):
                                            ins = pe.transpose(p[:, gg, t, :], OT[:, g, 128 * t:128 * t + 128], ident[:, :])
                                    ins.then_inc(filled("Ot", 0, half, i), 1)
                            else:
                                first = nP
                                for g in range(KV):
                                    p = fill(pe, "S", 1, half, g)
                                    for k in range(2):
                                        pe.matmul(p[:, 512 * k:512 * k + 512].rearrange("p (a b) -> p a b", b=32), local[:, :],
                                                  ident16[:, 0:32].unsqueeze(1).to_broadcast([128, 16, 32]),
                                                  start=True, stop=False, skip_group_check=True)
                                    for u8 in range(8):
                                        for w in range(2):
                                            t0 = 64 * (8 * half + u8) + 32 * w
                                            o = p[64 * w:64 * w + 64, 128 * u8:128 * u8 + 128].rearrange("p (j q) -> p j q", j=4)
                                            ins = pe.matmul(o, KT[:, g, t0:t0 + 64], QT[:, :, t0:t0 + 32],
                                                            start=False, stop=True, skip_group_check=True)
                                    ins.then_inc(filled("S", 1, half, g), 1)
                                    nP += 1
                                o = fill(pe, "O", 1, half)
                                pe.wait_ge(sg("P"), first + 4)
                                for u8 in range(8):
                                    for g in range(KV):
                                        ins = pe.matmul(o[32 * g:32 * g + 32, 128 * u8:128 * u8 + 128],
                                                        Vwin[:, 8 * half + u8, g].rearrange("p a b -> p (a b)"),
                                                        P[(first + g) % PRING][:, 128 * u8:128 * u8 + 128],
                                                        start=True, stop=True, skip_group_check=True)
                                ins.then_inc(filled("O", 1, half), 1)
                                pe.wait_ge(sg("OT"), 8 + half + 1)
                                p = fill(pe, "Ot", 1, half, 0).rearrange("p (T j n) -> p T j n", T=2, j=4)
                                for T in range(2):
                                    for j in range(4):
                                        c = 256 * j + 128 * T
                                        ins = pe.transpose(p[:, T, j, :], OT.rearrange("p g n -> p (g n)")[:, c:c + 128], ident[:, :])
                                ins.then_inc(filled("Ot", 1, half, 0), 1)
                            pe.wait_ge(sg("A"), 2 * a + half + 1)
                            p = fill(pe, "At", a, half)
                            for t in range(4):
                                ins = pe.transpose(p[:, 128 * t:128 * t + 128], At[:, t, :], ident[:, :])
                            ins.then_inc(filled("At", a, half), 1)
                            pe.wait_ge(sg("AT"), 2 * a + half + 1)
                            p = fill(pe, "wo", a, half)
                            for t in range(4):
                                ins = pe.matmul(p[:, 128 * t:128 * t + 128], AT[:, 128 * t:128 * t + 128], w_ao[a][:, :],
                                                start=True, stop=True)
                            ins.then_inc(filled("wo", a, half), 1)

                    to_t(2, X, as_is)
                    pe.wait_ge(sg("xT"), 3)
                    p = fill(pe, "gate")
                    for t in range(NT):
                        ins = pe.matmul(p[:, E * t:E * t + E], xT[:, PAD + 128 * t:PAD + 128 * t + 128], wgate[:, :], start=True, stop=True)
                    ins.then_inc(filled("gate"), 1)
                    for i in range(2 * E + 1):
                        if i < 2 * E:
                            hb, e = divmod(i, E)
                            for k in range(2):
                                p = fill(pe, "h", i, k)
                                for c in range(2):
                                    hc = 2 * k + c
                                    ins = pe.matmul(p[:, 512 * c:512 * c + 512], W1[:, e, 128 * hc:128 * hc + 128],
                                                    xT[:, PAD + 512 * hb:PAD + 512 * hb + 512], start=True, stop=True)
                                ins.then_inc(filled("h", i, k), 1)
                        if i > 0:
                            hb, e = divmod(i - 1, E)
                            p = fill(pe, "eo", i - 1)
                            pe.wait_ge(sg("gelu"), 4 * i)
                            hv = hbuf[(i - 1) % 3]
                            for t in range(4):
                                for c in range(HC):
                                    ins = pe.matmul(p[:, 128 * t:128 * t + 128], hv[:, c, 128 * t:128 * t + 128], W2m[:, e, c, :],
                                                    start=(c == 0), stop=(c == HC - 1))
                            ins.then_inc(filled("eo", i - 1), 1)
                    pe.wait_ge(sg("gates"), 1)
                    p = fill(pe, "GT")
                    for t in range(NT):
                        ins = pe.transpose(p[0:E, 128 * t:128 * t + 128], gates[:, t, :], ident[:, :])
                    ins.then_inc(filled("GT"), 1)
                    pe.wait_ge(sg("GT"), 1)
                    p = fill(pe, "b2")
                    for t in range(NT):
                        ins = pe.matmul(p[:, 128 * t:128 * t + 128], GT[:, 128 * t:128 * t + 128], b2m[:, :], start=True, stop=True)
                    ins.then_inc(filled("b2"), 1)

                    to_t(3, X, in_order)
                    pe.wait_ge(sg("xT"), 4)

                    def project(name, w):
                        p = fill(pe, name)
                        for k in range(2):
                            ins = pe.matmul(p[0:HL, 512 * k:512 * k + 512], lw[:, w, :],
                                            xT[:, PAD + 512 * k:PAD + 512 * k + 512], start=True, stop=True)
                        ins.then_inc(filled(name), 1)

                    project("lq", 0)
                    project("lk", 1)
                    p = fill(pe, "lkv")
                    for t in range(NT):
                        ins = pe.matmul(p[:, 128 * t:128 * t + 128], xT[:, PAD + 128 * t:PAD + 128 * t + 128],
                                        lw[:, 1:3, :].rearrange("p a b -> p (a b)"), start=True, stop=True)
                    ins.then_inc(filled("lkv"), 1)
                    project("lv", 2)
                    pe.wait_ge(sg("l_tok"), 1)
                    p = fill(pe, "lM")
                    for t in range(NT - 1):
                        ins = pe.matmul(p[0:HL, HL * t:HL * t + HL], lvt[:, t, :], lkt[:, t, :], start=True, stop=True)
                    ins.then_inc(filled("lM"), 1)
                    pe.wait_ge(sg("l_v"), 1)
                    p = fill(pe, "ls")
                    for t in range(NT):
                        ins = pe.matmul(p[:, 128 * t:128 * t + 128], lvT[:, 128 * t:128 * t + 128],
                                        lqT[:, 128 * t:128 * t + 128], start=True, stop=True)
                    ins.then_inc(filled("ls"), 1)
                    pe.wait_ge(sg("l_A"), 1)
                    p = fill(pe, "lo")
                    for t in range(NT):
                        c = 128 * t
                        pe.matmul(p[:, c:c + HL], lA[:, t, :], lkt[:, t, :], start=True, stop=(t == 0))
                        if t:
                            pe.matmul(p[:, c:c + HL], lqT[:, c:c + 128], lM[:, t, :], start=False, stop=True)
                        ins = pe.matmul(p[:, c + HL:c + HL + 1], lqz[:, c:c + 128], ones[0:HL, :], start=True, stop=True)
                    ins.then_inc(filled("lo"), 1)
                    pe.wait_ge(sg("l_O"), 1)
                    p = fill(pe, "loT")
                    for t in range(NT):
                        ins = pe.transpose(by_tiles(p[0:HL, :], t), lO[:, t, :], ident[:, :])
                    ins.then_inc(filled("loT"), 1)
                    pe.wait_ge(sg("l_OT"), 1)
                    p = fill(pe, "lwo")
                    for t in range(NT):
                        ins = pe.matmul(p[:, 128 * t:128 * t + 128], lOT[:, 128 * t:128 * t + 128], lwo[:, :], start=True, stop=True)
                    ins.then_inc(filled("lwo"), 1)

                    for l in range(DEPTH):
                        to_t(4 + 4 * l, X, in_order)
                        pe.wait_ge(sg("hT"), 2 * l + 1)
                        for i in range(NT + 3):
                            t = i - 1
                            k = l * NT + t
                            if 0 <= t < NT:
                                pe.wait_ge(sg("rot"), 2 * k + 2)
                                p = fill(pe, "fT", l, t)
                                for h in range(8):
                                    ins = pe.transpose(p[:, 128 * h:128 * h + 128],
                                                       T1[k % 2].rearrange("p a b -> p (a b)")[:, 128 * h:128 * h + 128], ident[:, :])
                                ins.then_inc(filled("fT", l, t), 1)
                            if i < NT:
                                p = fill(pe, "fqk", l, i)
                                for k in range(2):
                                    ins = pe.matmul(p[:, 512 * k:512 * k + 512], hT[:, 128 * i:128 * i + 128],
                                                    wqkv[:, l, 512 * k:512 * k + 512], start=True, stop=True)
                                ins.then_inc(filled("fqk", l, i), 1)
                                p = fill(pe, "fv", l, i)
                                pe.matmul(p, hT[:, 128 * i:128 * i + 128], wqkv[:, l, 1024:1536],
                                          start=True, stop=True).then_inc(filled("fv", l, i), 1)
                            t = i - 3
                            k = l * NT + t
                            if 0 <= t < NT:
                                pe.wait_ge(sg("fO"), k + 1)
                                p = fill(pe, "fOT", l, t)
                                for h in range(4):
                                    o = p[:, 128 * h:128 * h + 128].rearrange("p (w u q) -> p u w q", w=2, u=2)
                                    ins = pe.transpose(o, fO[0][:, 128 * h:128 * h + 128], ident[:, :])
                                ins.then_inc(filled("fOT", l, t), 1)
                            t = i - 2
                            k = l * NT + t
                            if 0 <= t < NT:
                                pe.wait_ge(sg("fP"), k + 1)
                                p = fill(pe, "fPT", l, t)
                                for h in range(NH):
                                    ins = pe.transpose(p[:, 128 * h:128 * h + 128], fP[k % 2][:, h, :], ident[:, :])
                                ins.then_inc(filled("fPT", l, t), 1)
                            t = i - 1
                            k = l * NT + t
                            if 0 <= t < NT:
                                p = fill(pe, "fS", l, t)
                                for n in range(2):
                                    pe.matmul(p[:, 512 * n:512 * n + 512].rearrange("p (a b) -> p a b", b=128), win[:, min(t, 1), :],
                                              identb[:, :].unsqueeze(1).to_broadcast([128, 4, 128]),
                                              start=True, stop=False, skip_group_check=True)
                                pe.wait_ge(sg("fqkT"), 3 * k + 3)
                                for h in range(NH):
                                    r = 64 * (h % 2)
                                    for w in range(2):
                                        c = 512 * (h % 2) + 128 * (h // 2)
                                        ins = pe.matmul(p[64 * w:64 * w + 64, c:c + 128],
                                                        fqT[k % 2][r:r + 64, h // 2, 64 * w:64 * w + 64],
                                                        fkT[k % 2][r:r + 64, h // 2, 64 * w:64 * w + 128],
                                                        start=False, stop=True, skip_group_check=True)
                                ins.then_inc(filled("fS", l, t), 1)
                            t = i - 2
                            k = l * NT + t
                            if 0 <= t < NT:
                                pe.wait_ge(sg("fPT"), k + 1)
                                pe.wait_ge(sg("v_tile"), k + 1)
                                pe.wait_ge(sg(f"v_shift{k % 5}"), 32 * (k // 5 + 1))
                                p = fill(pe, "fO", l, t)
                                for h in range(NH):
                                    for w in range(2):
                                        vv = (Vsh if w == 0 else V)[k % 5]
                                        ins = pe.matmul(p[64 * w:64 * w + 64, 64 * h:64 * h + 64],
                                                        fPT[0][:, 4 * (h % 2) + h // 2, 64 * w:64 * w + 64], vv[:, 64 * h:64 * h + 64],
                                                        start=True, stop=True, skip_group_check=True)
                                ins.then_inc(filled("fO", l, t), 1)
                            if i - 3 in (3, 7):
                                g = (i - 3) // 4
                                pe.wait_ge(sg("fOT"), l * NT + 4 * g + 4)
                                p = fill(pe, "fwo", l, g)
                                for t in range(4):
                                    for c in range(4):
                                        ins = pe.matmul(p[:, 128 * t:128 * t + 128], fOT[:, c, 128 * t:128 * t + 128], wo[:, l, c, :],
                                                        start=(c == 0), stop=(c == 3))
                                ins.then_inc(filled("fwo", l, g), 1)
                        to_t(5 + 4 * l, X, in_order)
                        pe.wait_ge(sg("hT"), 2 * l + 2)
                        p = fill(pe, "toT", 6 + 4 * l)
                        for t in range(NT):
                            ins = pe.transpose(p[:, 128 * t:128 * t + 128], hT[:, 128 * t:128 * t + 128], ident[:, :])
                        ins.then_inc(filled("toT", 6 + 4 * l), 1)
                        to_t(7 + 4 * l, N, by_tiles)
                        pe.wait_ge(sg("xT"), 5 + l)
                        for hb in range(2):
                            for c, (c0, m) in enumerate(CH):
                                p = fill(pe, "fw1", l, hb, c)
                                for k in range(2):
                                    ins = pe.matmul(p[0:m, 512 * k:512 * k + 512], w1[:, l, HID * k + c0:HID * k + c0 + m],
                                                    xT[:, PAD + 512 * hb:PAD + 512 * hb + 512], start=True, stop=True)
                                ins.then_inc(filled("fw1", l, hb, c), 1)
                            pe.wait_ge(sg("U"), (2 * l + hb + 1) * len(CH))
                            p = fill(pe, "fw2", l, hb)
                            for t in range(4):
                                for c, (c0, m) in enumerate(CH):
                                    last = c == len(CH) - 1
                                    mm = m + 1 if last else m
                                    ins = pe.matmul(p[:, 128 * t:128 * t + 128], U[0:mm, c, 128 * t:128 * t + 128], w2[0:mm, l, c, :],
                                                    start=(c == 0), stop=last)
                            ins.then_inc(filled("fw2", l, hb), 1)

                def numerators_read(k):
                    n = [len(attention_units(0, 0)), len(attention_units(0, 1))]
                    if k >= sum(n):
                        j = k - sum(n)
                        t = tk.at[("O", 1, j // KV)]
                        return sg(f"full_{t[0]}{t[1]}"), t[2] + 1
                    half = int(k >= n[0])
                    i = k - half * n[0]
                    g, kc, jp = attention_units(0, half)[i]
                    if kc == 4 * half + 3 and jp == 1:
                        t = tk.at[("O", 0, half, g)]
                        return sg(f"full_{t[0]}{t[1]}"), t[2] + 1
                    done = 4 * half + g
                    return sg("pv"), k + 1 - done

                @block.scalar
                def _(act):
                    def out_xT(i, k):
                        p = read(act, "toT", i)
                        act.activation(xT[:, PAD:PAD + S], p, ACT.Copy).then_inc(freed("toT", i), 1)
                        act.wait_ge(freed("toT", i), tk.at[("toT", i)][2] + 1)
                        act.sem_inc(sg("xT"), 1)

                    nP = 0
                    gone_units = 0
                    for a in range(2):
                        out_xT(a, a)
                        act.wait_ge(sg("set"), 7)
                        for i in range(2):
                            p = read(act, "qkv", a, i).rearrange("p (t n) -> p t n", t=4)
                            if a == 0:
                                act.activation(Vaug[:, 4 * i:4 * i + 4, :, 0:HD],
                                               p[:, :, 160:192].rearrange("p t (g d) -> p t g d", g=KV), ACT.Copy).then_inc(sg("V_part"), 1)
                            act.activation(QK[:, 4 * i:4 * i + 4, :], p[:, :, 0:160], ACT.Copy).then_inc(sg("qk"), 1)
                            if a == 0:
                                act.wait_ge(sg("V_part"), i + 1)
                            act.wait_ge(sg("qk"), 2 * a + i + 1)
                            act.sem_inc(freed("qkv", a, i), 1)
                        if a == 0:
                            act.sem_inc(sg("V"), 1)
                        else:
                            p = read(act, "vwin").rearrange("p (u n) -> p u n", u=16)
                            for w in range(2):
                                act.activation(Vwin[64 * w:64 * w + 64, :, :, w, 0:HD],
                                               p[64 * w:64 * w + 64, :, 0:32].rearrange("p u (g d) -> p u g d", g=KV),
                                               ACT.Copy).then_inc(sg("V_part"), 1)
                            act.wait_ge(sg("V_part"), 4)
                            act.sem_inc(freed("vwin"), 1)
                            act.sem_inc(sg("V"), 1)
                        act.wait_ge(sg("qn"), a + 1)
                        for s in range(2):
                            act.activation(Qs[:, :, :, s, :], QR[:, :, 0:128].rearrange("p t (j n) -> p t j n", j=GQ),
                                           ACT.Copy).then_inc(sg("q_hi"), 1)
                        for i in range(2):
                            p = read(act, "qT", a, i).bitcast(F16).rearrange("p (j n) -> p j n", j=2)
                            act.activation(QT[:, 2 * i:2 * i + 2, :], p, ACT.Copy).then_inc(sg("QT"), 1)
                            act.wait_ge(sg("QT"), 2 * a + i + 1)
                            act.sem_inc(freed("qT", a, i), 1)
                        for half in range(2):
                            for u in attention_units(a, half):
                                if a == 0:
                                    n = min(512, 512 - 128 * (u[1] - 4 * half))
                                else:
                                    n = 512
                                p = read(act, "S", a, half, *u).rearrange("p (j n) -> p j n", j=2)
                                if nP >= PRING:
                                    act.wait_ge(*numerators_read(nP - PRING))
                                pb = P[nP % PRING].rearrange("p (j n) -> p j n", j=2)
                                act.activation(pb[:, :, 0:n], p[:, :, 0:n], ACT.Exp, scale=INV_SQRT_HD).then_inc(freed("S", a, half, *u), 1)
                                nP += 1
                                act.wait_ge(freed("S", a, half, *u), tk.at[("S", a, half, *u)][2] + 1)
                                act.sem_inc(sg("P"), 1)
                            p = read(act, "At", a, half)
                            act.activation(AT, p, ACT.Copy).then_inc(sg("AT"), 1)
                            act.wait_ge(sg("AT"), 2 * a + half + 1)
                            act.sem_inc(freed("At", a, half), 1)
                    out_xT(2, 2)
                    act.wait_ge(sg("g_lg"), 1)
                    act.activation(gtmp[1][:, :, :], gtmp[0][:, :, :], ACT.Exp).then_inc(sg("g_exp"), 1)
                    for i in range(2 * E):
                        hb, e = divmod(i, E)
                        if i >= 3:
                            read(act, "eo", i - 3)
                        for k in range(2):
                            p = read(act, "h", i, k)
                            for c in range(2):
                                hc = 2 * k + c
                                act.activation(hbuf[i % 3][:, hc, :], p[:, 512 * c:512 * c + 512], ACT.Gelu_apprx_tanh,
                                               bias=b1[:, e, hc:hc + 1]).then_inc(sg("gelu"), 1)
                            act.wait_ge(sg("gelu"), 4 * i + 2 * k + 2)
                            act.sem_inc(freed("h", i, k), 1)
                    p = read(act, "GT")
                    act.activation(GT, p[0:E, :], ACT.Copy).then_inc(sg("GT"), 1)
                    act.wait_ge(sg("GT"), 1)
                    act.sem_inc(freed("GT"), 1)
                    out_xT(3, 3)
                    for i in range(3):
                        act.wait_ge(sg("l_min"), i + 1)
                        if i < 2:
                            act.activation(lm[i][0:HL, :], lm[i][0:HL, :], ACT.Exp).then_inc(sg("l_exp"), 1)
                        else:
                            act.activation(lm[i][:, 0:NT * HL], lm[i][:, 0:NT * HL], ACT.Exp).then_inc(sg("l_exp"), 1)
                    p = read(act, "lv")
                    act.activation(lvT, p[0:HL, :], ACT.Copy).then_inc(sg("l_v"), 1)
                    act.wait_ge(sg("l_v"), 1)
                    act.sem_inc(freed("lv"), 1)
                    p = read(act, "loT")
                    act.activation(lOT, p[0:HL, :], ACT.Copy).then_inc(sg("l_OT"), 1)
                    act.wait_ge(sg("l_OT"), 1)
                    act.sem_inc(freed("loT"), 1)
                    for l in range(DEPTH):
                        def shifted(i, k):
                            p = read(act, "toT", i)
                            act.activation(hT[0:64, :], p[0:64, :], ACT.Copy).then_inc(sg("h_part"), 1)
                            act.activation(hT[64:128, 1:S], p[64:128, 0:S - 1], ACT.Copy).then_inc(sg("h_part"), 1)
                            act.wait_ge(sg("h_part"), 2 * k)
                            act.sem_inc(freed("toT", i), 1)
                            act.sem_inc(sg("hT"), 1)

                        shifted(4 + 4 * l, 2 * l + 1)
                        for i in range(NT + 3):
                            t = i - 1
                            k = l * NT + t
                            if 0 <= t < NT:
                                p = read(act, "fT", l, t).rearrange("p (h n) -> p h n", h=8)
                                if k >= 1:
                                    read(act, "fS", (k - 1) // NT, (k - 1) % NT)
                                act.activation(fkT[k % 2][:, :, 64:192], p[:, 4:8, :], ACT.Copy).then_inc(sg("fqkT"), 1)
                                act.activation(fqT[k % 2], p[:, 0:4, :], ACT.Copy).then_inc(sg("fqkT"), 1)
                                before = p[:, 4:8, 64:128] if t == 0 else fkT[(k - 1) % 2][:, :, 128:192]
                                act.activation(fkT[k % 2][:, :, 0:64], before, ACT.Copy).then_inc(sg("fqkT"), 1)
                                act.wait_ge(sg("fqkT"), 3 * k + 3)
                                act.sem_inc(freed("fT", l, t), 1)
                            if i < NT:
                                k = l * NT + i
                                p = read(act, "fqk", l, i)
                                if k > 0:
                                    act.wait_ge(sg("f_ss"), k)
                                act.activation(SQb.rearrange("p a b -> p (a b)"), p, ACT.Square).then_inc(sg("f_sq"), 1)
                                if k >= 2:
                                    act.wait_ge(sg("f_prod"), 2 * (k - 1))
                                act.activation(QKs[:, k % 2].rearrange("p a b -> p (a b)"), p, ACT.Copy).then_inc(sg("f_qk"), 1)
                                act.wait_ge(sg("f_qk"), k + 1)
                                act.sem_inc(freed("fqk", l, i), 1)
                                p = read(act, "fv", l, i)
                                if k >= 5:
                                    read(act, "fO", (k - 5) // NT, (k - 5) % NT)
                                    act.wait_ge(sg(f"v_shift{(k - 4) % 5}"), 32 * ((k - 4) // 5 + 1))
                                act.activation(V[k % 5], p, ACT.Copy).then_inc(sg("v_tile"), 1)
                                act.wait_ge(sg("v_tile"), k + 1)
                                act.sem_inc(freed("fv", l, i), 1)
                            t = i - 3
                            k = l * NT + t
                            if 0 <= t < NT:
                                p = read(act, "fOT", l, t)
                                if k and t % 4 == 0:
                                    read(act, "fwo", (k - 4) // NT, ((k - 4) % NT) // 4)
                                ov = fOT.rearrange("p c (T w n) -> p c T w n", T=2, w=2)[:, :, (t % 4) // 2, :, 64 * (t % 2):64 * (t % 2) + 64]
                                act.activation(ov, p.rearrange("p (c w n) -> p c w n", c=4, w=2), ACT.Copy).then_inc(sg("fOT"), 1)
                                act.wait_ge(sg("fOT"), k + 1)
                                act.sem_inc(freed("fOT", l, t), 1)
                            t = i - 2
                            k = l * NT + t
                            if 0 <= t < NT:
                                p = read(act, "fPT", l, t)
                                if k:
                                    read(act, "fO", (k - 1) // NT, (k - 1) % NT)
                                act.activation(fPT[0].rearrange("p a b -> p (a b)"), p, ACT.Copy).then_inc(sg("fPT"), 1)
                                act.wait_ge(sg("fPT"), k + 1)
                                act.sem_inc(freed("fPT", l, t), 1)
                            t = i - 1
                            k = l * NT + t
                            if 0 <= t < NT:
                                p = read(act, "fS", l, t)
                                act.wait_ge(sg("f_nb"), k + 1)
                                if k >= 2:
                                    read(act, "fPT", (k - 2) // NT, (k - 2) % NT)
                                    act.wait_ge(sg("f_rd"), k - 1)
                                for h in range(NH):
                                    act.activation(fP[k % 2][:, h, :], p[:, 128 * h:128 * h + 128], ACT.Exp,
                                                   bias=fnm[:, k % 2, h:h + 1], scale=frq[:, k % 4, h:h + 1],
                                                   accum_out=fden[:, k % 2, h:h + 1]).then_inc(sg("f_exp"), 1)
                                act.wait_ge(sg("f_exp"), NH * (k + 1))
                                act.sem_inc(freed("fS", l, t), 1)
                                act.sem_inc(sg("fP"), 1)
                        shifted(5 + 4 * l, 2 * l + 2)
                        out_xT(7 + 4 * l, 4 + l)
                        for hb in range(2):
                            for c, (c0, m) in enumerate(CH):
                                p = read(act, "fw1", l, hb, c)
                                k = (2 * l + hb) * len(CH) + c
                                if k >= 2:
                                    act.wait_ge(sg("U"), k - 1)
                                act.activation(GL[k % 2][0:m, :], p[0:m, 512:1024], ACT.Gelu,
                                               bias=fb1[0:m, l, 1, c:c + 1]).then_inc(sg("GL"), 1)

                @block.vector
                def _(dve):
                    chain = [0]

                    def link(ins):
                        chain[0] += 1
                        ins.then_inc(sg("dve_chain"), 1)
                        dve.wait_ge(sg("dve_chain"), chain[0])

                    def rsqrt(n):
                        m, y, t = st_m[:, 0:n], st_y[:, 0:n], st_t[:, 0:n]
                        link(dve.tensor_scalar(st_i[:, 0:n], m.bitcast(I32), 1, None, ALU.logical_shift_right))
                        link(dve.tensor_scalar(y.bitcast(I32), st_i[:, 0:n], -1.0, 1597463007.0, ALU.mult, ALU.add))
                        for _ in range(3):
                            link(dve.tensor_tensor(t, y, y, ALU.mult))
                            link(dve.scalar_tensor_tensor(out=t, in0=t, scalar=-0.5, in1=m, op0=ALU.mult, op1=ALU.mult))
                            link(dve.scalar_tensor_tensor(out=y, in0=t, scalar=1.5, in1=y, op0=ALU.add, op1=ALU.mult))

                    def per_token(n):
                        return st_y[:, 0:NT].unsqueeze(2).to_broadcast([128, NT, n])

                    def layer_norm(src, dst, free=None):
                        link(dve.tensor_reduce(st_a[:, 0:NT], src, AX, ALU.add))
                        link(dve.tensor_scalar(st_a[:, 0:NT], st_a[:, 0:NT], -1.0 / D, None, ALU.mult))
                        link(dve.tensor_tensor(dst, src, st_a[:, 0:NT].unsqueeze(2).to_broadcast([128, NT, D]), ALU.add))
                        if free is not None:
                            dve.sem_inc(free, 1)
                        link(dve.tensor_tensor(Q[:, :, :], dst, dst, ALU.mult))
                        link(dve.tensor_reduce(st_a[:, 0:NT], Q[:, :, :], AX, ALU.add))
                        link(dve.tensor_scalar(st_m[:, 0:NT], st_a[:, 0:NT], 1.0 / D, 1e-5, ALU.mult, ALU.add))
                        rsqrt(NT)
                        link(dve.tensor_tensor(dst, dst, per_token(D), ALU.mult))

                    def signal(name):
                        dve.sem_inc(sg(name), 1)

                    dve.wait_ge(sg("x_in"), 256)
                    for a in range(2):
                        src = (X, R)[a][:, :, :]
                        link(dve.tensor_tensor(Q[:, :, :], src, src, ALU.mult))
                        link(dve.tensor_reduce(st_a[:, 0:NT], Q[:, :, :], AX, ALU.add))
                        link(dve.tensor_scalar(st_m[:, 0:NT], st_a[:, 0:NT], 1.0 / D, 1e-6, ALU.mult, ALU.add))
                        rsqrt(NT)
                        link(dve.tensor_tensor(N[:, :, :], src, per_token(D), ALU.mult))
                        signal("src")
                        dve.wait_ge(sg("qk"), 2 * a + 2)
                        nh = H + KV
                        qv = QK.rearrange("p t (h d) -> p t h d", h=nh)
                        rv = QR.rearrange("p t (h d) -> p t h d", h=nh)
                        sw = QK.rearrange("p t (h d s) -> p t h d s", h=nh, s=2)
                        tmp = arena_rope.rearrange("p t (h d s) -> p t h d s", h=nh, s=2)
                        for t in range(NT):
                            dve.tensor_tensor(rv[:, t], qv[:, t],
                                              rope[a][:, t, 0:1, :].to_broadcast([128, nh, HD]), ALU.mult)
                            for s in range(2):
                                ins = dve.tensor_tensor(tmp[:, t, :, :, s], sw[:, t, :, :, 1 - s],
                                                  rope[a][:, t, 1:2, :].rearrange("p o (d s) -> p o d s", s=2)[:, :, :, s].to_broadcast([128, nh, HD // 2]), ALU.mult)
                        link(ins)
                        link(dve.tensor_tensor(QR, QR, arena_rope, ALU.add))
                        link(dve.tensor_tensor(arena_rope, QR, QR, ALU.mult))
                        link(dve.tensor_reduce(st_a[:, 0:160], arena_rope.rearrange("p t (h d) -> p (t h) d", h=nh), AX, ALU.add))
                        link(dve.tensor_scalar(st_m[:, :], st_a[:, :], 1.0 / HD, 1e-6, ALU.mult, ALU.add))
                        rsqrt(160)
                        QRf = QR.rearrange("p t (h d) -> p (t h) d", h=nh)
                        link(dve.tensor_tensor(QRf, QRf, st_y[:, :].unsqueeze(2).to_broadcast([128, 160, HD]), ALU.mult))
                        signal("qn")
                        kv = QR[:, :, 128:160]
                        dve.wait_ge(sg("set"), 7)
                        for s in (0, 2):
                            for g in range(KV):
                                ins = dve.tensor_copy(Kpad[:, :, g, s, g, :], kv[:, :, 8 * g:8 * g + 8])
                        link(ins)
                        for s in (1, 3):
                            for g in range(KV):
                                ins = dve.tensor_tensor(Kpad[:, :, g, s, g, :], kv[:, :, 8 * g:8 * g + 8],
                                                        Kpad[:, :, g, s - 1, g, :], ALU.subtract)
                        dve.wait_ge(sg("q_hi"), 2 * a + 2)
                        for s in (2, 3):
                            ins = dve.tensor_tensor(Qs[:, :, :, s, :], QR[:, :, 0:128].rearrange("p t (j n) -> p t j n", j=GQ),
                                                    Qs[:, :, :, s - 2, :], ALU.subtract)
                        link(ins)
                        signal("split")
                        for i in range(2):
                            p = read(dve, "kT", a, i).bitcast(F16).rearrange("p (j n) -> p j n", j=2)
                            if i == 0:
                                link(dve.memset(KT[:, :, 0:PAD], 0.0))
                            link(dve.tensor_copy(KT[:, 2 * i:2 * i + 2, PAD:PAD + S], p))
                            dve.sem_inc(freed("kT", a, i), 1)
                            signal("KT")
                        for half in range(2):
                            Av = At.rearrange("p t (g j d) -> p t g j d", g=KV, j=GQ)
                            if a == 0:
                                for g in range(KV):
                                    p = read(dve, "O", 0, half, g)
                                    if half:
                                        read(dve, "Ot", 0, 0, g // 2)
                                    pv = p.rearrange("p (T u w q) -> p T w u q", T=2, u=4, w=2)
                                    ov = OT[:, g, :].rearrange("p (T w u q) -> p T w u q", T=2, u=4, w=2)
                                    for T in range(2):
                                        ins = dve.tensor_copy(ov[:, T], pv[:, T])
                                    link(ins)
                                    dve.sem_inc(freed("O", 0, half, g), 1)
                                    signal("OT")
                                for i in range(2):
                                    p = read(dve, "Ot", 0, half, i).rearrange("p (g t j n) -> p g t j n", g=2, t=4, j=4)
                                    for gg in range(2):
                                        rd = rden[:, 0:16].rearrange("p (t j) -> p t j", t=4)
                                        link(dve.reciprocal(rd, p[:, gg, :, :, HD]))
                                        link(dve.tensor_tensor(Av[:, :, 2 * i + gg], p[:, gg, :, :, 0:HD],
                                                               rd.unsqueeze(3).to_broadcast([128, 4, 4, HD]), ALU.mult))
                                    dve.sem_inc(freed("Ot", 0, half, i), 1)
                            else:
                                p = read(dve, "O", 1, half)
                                link(dve.tensor_copy(OT.rearrange("p g n -> p (g n)")[:, 0:1024].rearrange("p (j u q) -> p u j q", j=4, u=8),
                                                     p.rearrange("p (u j q) -> p u j q", u=8, j=4)))
                                dve.sem_inc(freed("O", 1, half), 1)
                                signal("OT")
                                p = read(dve, "Ot", 1, half, 0).rearrange("p (T j g w n) -> p T j g w n", T=2, j=4, g=4, w=2)
                                for T in range(2):
                                    for w in range(2):
                                        rd = rden[:, 0:16].rearrange("p (g j) -> p g j", g=4)
                                        pv = p[:, T, :, :, w].rearrange("p j g n -> p g j n")
                                        link(dve.reciprocal(rd, pv[:, :, :, HD]))
                                        link(dve.tensor_tensor(Av[:, 2 * T + w], pv[:, :, :, 0:HD],
                                                               rd.unsqueeze(3).to_broadcast([128, 4, 4, HD]), ALU.mult))
                                dve.sem_inc(freed("Ot", 1, half, 0), 1)
                            signal("A")
                            p = read(dve, "wo", a, half).rearrange("p (t n) -> p t n", t=4)
                            base_ = (X, R)[a]
                            link(dve.tensor_tensor(R[:, 4 * half:4 * half + 4, :], base_[:, 4 * half:4 * half + 4, :], p, ALU.add))
                            dve.sem_inc(freed("wo", a, half), 1)
                    link(dve.tensor_tensor(R[:, :, :], R[:, :, :], X[:, :, :], ALU.add))
                    layer_norm(R[:, :, :], X[:, :, :])
                    signal("src")
                    p = read(dve, "gate")[:, 0:NT * E].rearrange("p (t e) -> p t e", t=NT)
                    bc = lambda v: v.unsqueeze(2).to_broadcast([128, NT, E])
                    lg, pr, c0_, c1_ = (g[:, :, :] for g in gtmp)
                    one = gone[0][:, :]
                    link(dve.tensor_tensor(lg, p, bgate[:, :].unsqueeze(1).to_broadcast([128, NT, E]), ALU.add))
                    dve.sem_inc(freed("gate"), 1)
                    link(dve.tensor_reduce(one, lg, AX, ALU.max))
                    link(dve.tensor_tensor(lg, lg, bc(one), ALU.subtract))
                    signal("g_lg")
                    dve.wait_ge(sg("g_exp"), 1)
                    link(dve.tensor_reduce(one, pr, AX, ALU.add))
                    link(dve.reciprocal(gone[1][:, :], one))
                    link(dve.tensor_tensor(pr, pr, bc(gone[1][:, :]), ALU.mult))
                    link(dve.tensor_copy(lg, pr))
                    rk = rank[:, :].unsqueeze(1).to_broadcast([128, NT, E])
                    for k in range(2):
                        link(dve.tensor_reduce(one, lg, AX, ALU.max))
                        link(dve.tensor_tensor(c0_, lg, bc(one), ALU.is_equal))
                        link(dve.tensor_tensor(c0_, c0_, rk, ALU.mult))
                        link(dve.tensor_reduce(one, c0_, AX, ALU.max))
                        link(dve.tensor_tensor(c0_, c0_, bc(one), ALU.is_equal))
                        if k == 0:
                            link(dve.tensor_copy(c1_, c0_))
                            link(dve.scalar_tensor_tensor(out=lg, in0=c0_, scalar=-2.0, in1=lg, op0=ALU.mult, op1=ALU.add))
                        else:
                            link(dve.tensor_tensor(c1_, c1_, c0_, ALU.add))
                    link(dve.tensor_tensor(pr, pr, c1_, ALU.mult))
                    link(dve.tensor_reduce(one, pr, AX, ALU.add))
                    link(dve.tensor_scalar(one, one, 1e-8, None, ALU.add))
                    link(dve.reciprocal(gone[1][:, :], one))
                    link(dve.tensor_tensor(gates[:, :, :], pr, bc(gone[1][:, :]), ALU.mult))
                    signal("gates")
                    for i in range(2 * E):
                        hb, e = divmod(i, E)
                        p = read(dve, "eo", i)
                        for t in range(4):
                            tt = 4 * hb + t
                            acc = X if e == 0 else R
                            ins = dve.scalar_tensor_tensor(out=R[:, tt, :], in0=p[:, 128 * t:128 * t + 128],
                                                           scalar=gates[:, tt, e:e + 1], in1=acc[:, tt, :],
                                                           op0=ALU.mult, op1=ALU.add)
                        link(ins)
                        dve.sem_inc(freed("eo", i), 1)
                    p = read(dve, "b2").rearrange("p (t n) -> p t n", t=NT)
                    link(dve.tensor_tensor(R[:, :, :], R[:, :, :], p, ALU.add))
                    dve.sem_inc(freed("b2"), 1)
                    layer_norm(R[:, :, :], X[:, :, :])
                    signal("src")
                    dve.memset(lone, 1.0)
                    pq = read(dve, "lq")[0:HL, :]
                    link(dve.tensor_scalar(lm[0][0:HL, :], pq, 0.0, None, ALU.min))
                    signal("l_min")
                    pk = read(dve, "lk")[0:HL, :]
                    link(dve.tensor_scalar(lm[1][0:HL, :], pk, 0.0, None, ALU.min))
                    signal("l_min")
                    pt = read(dve, "lkv").rearrange("p (t n) -> p t n", t=NT)
                    m2 = lm[2][:, 0:NT * HL].rearrange("p (t n) -> p t n", t=NT)
                    link(dve.tensor_scalar(m2, pt[:, :, 0:HL], 0.0, None, ALU.min))
                    signal("l_min")
                    dve.wait_ge(sg("l_exp"), 1)
                    link(dve.scalar_tensor_tensor(out=lqT, in0=pq, scalar=0.0, in1=lm[0][0:HL, :], op0=ALU.max, op1=ALU.add))
                    dve.sem_inc(freed("lq"), 1)
                    dve.wait_ge(sg("l_exp"), 2)
                    link(dve.scalar_tensor_tensor(out=lkT, in0=pk, scalar=0.0, in1=lm[1][0:HL, :], op0=ALU.max, op1=ALU.add))
                    dve.sem_inc(freed("lk"), 1)
                    dve.wait_ge(sg("l_exp"), 3)
                    dve.tensor_copy(lvt, pt[:, :, HL:128])
                    link(dve.scalar_tensor_tensor(out=lkt, in0=pt[:, :, 0:HL], scalar=0.0, in1=m2, op0=ALU.max, op1=ALU.add))
                    dve.sem_inc(freed("lkv"), 1)
                    signal("l_tok")
                    link(dve.tensor_tensor_scan(lz, lone, lkT, 0.0, ALU.mult, ALU.add))
                    link(dve.tensor_tensor(lqz, lqT, lz, ALU.mult))
                    p = read(dve, "lM")[0:HL, :].rearrange("p (t n) -> p t n", t=NT)
                    link(dve.tensor_copy(lM[:, 1, :], p[:, 0, :]))
                    for t in range(2, NT):
                        link(dve.tensor_tensor(lM[:, t, :], lM[:, t - 1, :], p[:, t - 1, :], ALU.add))
                    dve.sem_inc(freed("lM"), 1)
                    p = read(dve, "ls").rearrange("p (t n) -> p t n", t=NT)
                    link(dve.tensor_tensor(lA, p, tri[:, :].unsqueeze(1).to_broadcast([128, NT, 128]), ALU.mult))
                    dve.sem_inc(freed("ls"), 1)
                    signal("l_A")
                    p = read(dve, "lo").rearrange("p (t n) -> p t n", t=NT)
                    link(dve.tensor_scalar(st_a[:, 0:NT], p[:, :, HL], 1e-6, None, ALU.max))
                    link(dve.reciprocal(st_y[:, 0:NT], st_a[:, 0:NT]))
                    link(dve.tensor_tensor(lO, p[:, :, 0:HL], per_token(HL), ALU.mult))
                    dve.sem_inc(freed("lo"), 1)
                    signal("l_O")
                    p = read(dve, "lwo").rearrange("p (t n) -> p t n", t=NT)
                    link(dve.tensor_tensor(R[:, :, :], X[:, :, :], p, ALU.add))
                    dve.sem_inc(freed("lwo"), 1)
                    layer_norm(R[:, :, :], X[:, :, :])
                    signal("src")
                    link(dve.tensor_copy(R[:, :, :], X[:, :, :]))
                    for l in range(DEPTH):
                        for i in range(NT + 3):
                            t = i - 3
                            k = l * NT + t
                            if 0 <= t < NT:
                                dve.wait_ge(sg("fP"), k + 1)
                                link(dve.reciprocal(frd[:, k % 2, :], fden[:, k % 2, :]))
                                signal("f_rd")
                                p = read(dve, "fO", l, t).rearrange("p (h n) -> p h n", h=NH)
                                if k:
                                    read(dve, "fOT", (k - 1) // NT, (k - 1) % NT)
                                for r in range(2):
                                    ins = dve.tensor_tensor(fO[0].rearrange("p (h r n) -> p r h n", h=4, r=2)[:, r],
                                                            p.rearrange("p (h r) n -> p r h n", r=2)[:, r],
                                                            frd[:, k % 2, 4 * r:4 * r + 4].unsqueeze(2).to_broadcast([128, 4, DH]), ALU.mult)
                                link(ins)
                                dve.sem_inc(freed("fO", l, t), 1)
                                signal("fO")
                            if i < NT:
                                k = l * NT + i
                                dve.wait_ge(sg("f_sq"), k + 1)
                                link(dve.tensor_reduce(fss[:, :], SQb, AX, ALU.add))
                                signal("f_ss")
                                if k >= 2:
                                    dve.wait_ge(sg("f_rn"), k - 1)
                                link(dve.tensor_scalar(fm[:, k % 2, :], fss[:, :], 1e-24, None, ALU.max))
                                link(dve.tensor_scalar(fi[:, :], fm[:, k % 2, :].bitcast(I32), 1, None, ALU.logical_shift_right))
                                link(dve.tensor_scalar(fy[:, k % 2, :].bitcast(I32), fi[:, :], -1.0, 1597463007.0, ALU.mult, ALU.add))
                                signal("f_guess")
                                if k >= 2:
                                    read(dve, "fT", (k - 2) // NT, (k - 2) % NT)
                                if k:
                                    dve.wait_ge(sg("rot"), 2 * k)
                                dve.wait_ge(sg("f_qk"), k + 1)
                                src = QKs[:, k % 2]
                                for s in range(2):
                                    hs = slice(NH * s, NH * s + NH)
                                    x = src[:, hs, :]
                                    if s:
                                        dve.wait_ge(sg("f_rn"), k + 1)
                                        link(dve.tensor_tensor(x, x, fy[:, k % 2, NH:16].unsqueeze(2).to_broadcast([128, NH, DH]), ALU.mult))
                                    dve.tensor_tensor(T1[k % 2][:, hs, :], x, xpos[:, l, i, 0, s:s + 1, :].to_broadcast([128, NH, DH]), ALU.mult)
                                    link(dve.tensor_tensor(T2[:, hs, :].rearrange("p h (a b) -> p h a b", a=2),
                                                           x.rearrange("p h (a b) -> p h a b", a=2)[:, :, ::-1, :],
                                                           xpos[:, l, i, 1, s:s + 1, :].rearrange("p o (a b) -> p o a b", a=2).to_broadcast([128, NH, 2, 32]),
                                                           ALU.mult))
                                    signal("f_prod")
                            t = i - 1
                            k = l * NT + t
                            if 0 <= t < NT:
                                p = read(dve, "fS", l, t).rearrange("p (h n) -> p h n", h=NH)
                                if k >= 2:
                                    dve.wait_ge(sg("fP"), k - 1)
                                link(dve.tensor_reduce(fnm[:, k % 2, :], p, AX, ALU.max, negate=True))
                                link(dve.tensor_tensor(fnm[:, k % 2, :], fnm[:, k % 2, :], frq[:, k % 4, :], ALU.mult))
                                signal("f_nb")
                            if i - 3 in (3, 7):
                                g = (i - 3) // 4
                                p = read(dve, "fwo", l, g).rearrange("p (t n) -> p t n", t=4)
                                link(dve.tensor_tensor(X[:, 4 * g:4 * g + 4, :], X[:, 4 * g:4 * g + 4, :], p, ALU.add))
                                dve.sem_inc(freed("fwo", l, g), 1)
                        signal("src")
                        p = read(dve, "toT", 6 + 4 * l).rearrange("p (t n) -> p t n", t=NT)
                        layer_norm(p, N[:, :, :], free=freed("toT", 6 + 4 * l))
                        signal("src")
                        signal("src")
                        for hb in range(2):
                            if l or hb:
                                read(dve, "fw2", l if hb else l - 1, 1 - hb)
                            link(dve.memset(U[64:96, 2, :], 1.0))
                            for c, (c0, m) in enumerate(CH):
                                k = (2 * l + hb) * len(CH) + c
                                p = read(dve, "fw1", l, hb, c)
                                dve.wait_ge(sg("GL"), k + 1)
                                link(dve.scalar_tensor_tensor(out=U[0:m, c, :], in0=p[0:m, 0:512], scalar=fb1[0:m, l, 0, c:c + 1],
                                                              in1=GL[k % 2][0:m, :], op0=ALU.add, op1=ALU.mult))
                                dve.sem_inc(freed("fw1", l, hb, c), 1)
                                signal("U")
                            p = read(dve, "fw2", l, hb).rearrange("p (t n) -> p t n", t=4)
                            link(dve.tensor_tensor(X[:, 4 * hb:4 * hb + 4, :], X[:, 4 * hb:4 * hb + 4, :], p, ALU.add))
                            dve.sem_inc(freed("fw2", l, hb), 1)
                        if l < DEPTH - 1:
                            signal("src")
                    link(dve.tensor_tensor(R[:, :, :], R[:, :, :], X[:, :, :], ALU.add))
                    layer_norm(R[:, :, :], N[:, :, :])
                    signal("final")

                @block.gpsimd
                def _(pool):
                    pool.memset(Kpad.rearrange("p a b c d e -> p (a b c d e)"), 0.0).then_inc(sg("set"), 1)
                    pool.memset(Vaug.rearrange("p a b c -> p (a b c)"), 0.0).then_inc(sg("set"), 1)
                    pool.memset(Vwin.rearrange("p a b c d -> p (a b c d)"), 0.0).then_inc(sg("set"), 1)
                    pool.wait_ge(sg("set"), 3)
                    pool.memset(Vaug[:, :, :, HD:HD + 1], 1.0).then_inc(sg("set"), 1)
                    pool.wait_ge(sg("set"), 4)
                    pool.memset(Vwin[0:64, :, :, 0, HD:HD + 1], 1.0).then_inc(sg("set"), 1)
                    pool.wait_ge(sg("set"), 5)
                    pool.memset(Vwin[64:128, :, :, 1, HD:HD + 1], 1.0).then_inc(sg("set"), 1)
                    pool.wait_ge(sg("set"), 6)
                    pool.memset(Vwin[0:WIN, 0:1, :, 0, HD:HD + 1], 0.0).then_inc(sg("set"), 1)
                    steps = [0]

                    def link(ins):
                        steps[0] += 1
                        ins.then_inc(sg("pool_chain"), 1)
                        pool.wait_ge(sg("pool_chain"), steps[0])

                    for k in range(DEPTH * NT):
                        pool.wait_ge(sg("f_guess"), k + 1)
                        m, y = fm[:, k % 2, :], fy[:, k % 2, :]
                        for _ in range(3):
                            link(pool.tensor_tensor(ft[:, :], y, y, ALU.mult))
                            link(pool.tensor_tensor(ft[:, :], ft[:, :], m, ALU.mult))
                            link(pool.tensor_scalar(ft[:, :], ft[:, :], -0.5, 1.5, ALU.mult, ALU.add))
                            link(pool.tensor_tensor(y, y, ft[:, :], ALU.mult))
                        if k >= 4:
                            pool.wait_ge(sg("fP"), k - 3)
                        link(pool.tensor_scalar(frq[:, k % 4, :].rearrange("p (r h) -> p r h", r=2),
                                                y[:, 0:NH].rearrange("p (h r) -> p r h", r=2), 8.0, None, ALU.mult))
                        pool.sem_inc(sg("f_rn"), 1)
                        for s in range(2):
                            pool.wait_ge(sg("f_prod"), 2 * k + s + 1)
                            hs = slice(NH * s, NH * s + NH)
                            pool.tensor_tensor(T1[k % 2][:, hs, :], T1[k % 2][:, hs, :], T2[:, hs, :], ALU.add).then_inc(sg("rot"), 1)
            with nc.Block() as block:
                @block.sync
                def _(sp):
                    for s in sems.values():
                        sp.sem_clear(s)


_INS = ['L0_attn_hidden', 'L0_attn_norm1_w', 'L0_attn_norm2_w', 'L0_attn_g_wq', 'L0_attn_g_kv_down', 'L0_attn_g_k_up',
        'L0_attn_g_v_up', 'L0_attn_g_wo', 'L0_attn_l_wq', 'L0_attn_l_wk', 'L0_attn_l_wv', 'L0_attn_l_wo', 'L0_ffn_Wg',
        'L0_ffn_bg', 'L0_ffn_W1', 'L0_ffn_b1', 'L0_ffn_W2', 'L0_ffn_b2', 'L1_attn_W_q', 'L1_attn_W_k', 'L1_attn_W_v',
        'L1_attn_W_o', 'L1_ffn_wqkv', 'L1_ffn_q_scale', 'L1_ffn_k_scale', 'L1_ffn_wo', 'L1_ffn_ln_g', 'L1_ffn_ln_b',
        'L1_ffn_w1', 'L1_ffn_b1', 'L1_ffn_w2', 'L1_ffn_b2']


def kernel(**inputs):
    import concourse.bacc as _bacc
    from concourse.bass_utils import run_bass_kernel_spmd as _run

    nc = _bacc.Bacc("TRN2", target_bir_lowering=False, num_devices=1)
    arrays, handles = {}, {}
    given = {n: np.ascontiguousarray(inputs[n]) for n in _INS}
    for n in ("L0_attn_g_wq", "L0_attn_l_wq"):
        given[n] = np.ascontiguousarray(given[n].reshape(D, KV, GQ, HD).transpose(0, 2, 1, 3).reshape(D, H * HD))
    given["L0_ffn_b1"] = np.ascontiguousarray(given["L0_ffn_b1"].reshape(E, HC, 128).transpose(2, 0, 1))
    given.update(constant_tables())
    given["c_rank"] = np.arange(E, 0, -1).astype(np.float32)
    for name, a in given.items():
        arrays[f"in_{name}"] = a
        handles[name] = nc.dram_tensor(f"in_{name}", a.shape, mybir.dt.from_np(a.dtype), kind="ExternalInput").ap()
    handles["out"] = nc.dram_tensor("out_y", (B, S, D), F32, kind="ExternalOutput").ap()
    build(nc, handles)
    r = _run(nc, [arrays], core_ids=[0])
    return r.results[0]["out_y"]
```

```python
import numpy as np
import concourse.bass as bass
from concourse import mybir
from concourse.alu_op_type import AluOpType as ALU
from contextlib import ExitStack

ACT = mybir.ActivationFunctionType
AX = mybir.AxisListType.X
F32, F16, BF16, I32 = mybir.dt.float32, mybir.dt.float16, mybir.dt.bfloat16, mybir.dt.int32

B, S, D = 4, 1024, 128
NT = S // 128
H, KV, HD = 16, 4, 8
GQ = H // KV
LAT = 32
WIN = 32
PAD = WIN
E, HF = 8, 512
HC = HF // 128
HL = 64
NH, DH, W2 = 8, 64, 64
INNER = NH * DH
DEPTH = 2
HID = int(D * 4 * 2 / 3)
CH = [(c * 128, min(128, HID - c * 128)) for c in range((HID + 127) // 128)]
VRING = 5
PRING = 6
INV_SQRT_HD = 1.0 / float(np.sqrt(np.float32(HD)))


def constant_tables():
    f = np.float32
    t = {}
    t["c_ident"] = np.eye(128, dtype=f)
    k, q = np.arange(128)[None, :], np.arange(128)[:, None]
    t["c_causal"] = np.where(k > q, -30000.0, 0.0).astype(np.float16)
    loc = np.zeros((128, 128), np.float16)
    kk = np.arange(64)[None, :]
    qq = np.arange(WIN)[:, None]
    ok = (kk <= qq + WIN) & (qq + WIN - kk < WIN)
    loc[:WIN] = np.tile(np.where(ok, 0.0, -30000.0), (1, 2))
    t["c_local"] = loc
    t["c_tri"] = (np.arange(128)[:, None] <= np.arange(128)[None, :]).astype(f)
    jl = np.arange(128)[:, None]
    il = np.arange(64)[None, :]
    ok = (il <= jl) & (jl <= il + W2)
    m = np.tile(np.where(ok, 0.0, -1e30), (1, 2)).astype(f)
    first = m.copy()
    first[:64] = -1e30
    t["c_win"] = np.stack([first, m], 1)
    for name, base in (("g", 1000000.0), ("l", 10000.0)):
        inv = (f(1.0) / (f(base) ** (np.arange(0, HD, 2, dtype=f) / f(HD)))).astype(f)
        fr = (np.arange(S, dtype=f)[:, None] * inv[None, :]).astype(f)
        c, s = np.cos(fr), np.sin(fr)
        tab = np.stack([np.repeat(c, 2, axis=1), np.stack([-s, s], -1).reshape(S, HD)], 1)
        t["c_rope_" + name] = np.ascontiguousarray(tab.reshape(NT, 128, 2, HD).transpose(1, 0, 2, 3)).astype(f)
    half = np.arange(0, DH, 2, dtype=f)
    inv = (f(1.0) / (f(10000.0) ** (half / f(DH)))).astype(f)
    pos = np.arange(S, dtype=f)
    fr = (pos[:, None] * inv[None, :]).astype(f)
    base = ((half + f(0.4 * DH)) / f(1.4 * DH)).astype(f)
    power = ((pos - f(S // 2)) / f(W2 // 2)).astype(f)
    sc = (base[None, :] ** power[:, None]).astype(f)
    c, s = np.cos(fr), np.sin(fr)
    cc, ss, scc = (np.concatenate([a, a], 1) for a in (c, s, sc))
    sg = np.concatenate([-ss[:, :DH // 2], ss[:, DH // 2:]], 1)
    tab = np.stack([np.stack([8 * cc * scc, cc / scc], 1), np.stack([8 * sg * scc, sg / scc], 1)], 1)
    t["c_xpos"] = np.ascontiguousarray(tab.reshape(NT, 128, 2, 2, DH).transpose(1, 0, 2, 3, 4)).astype(f)
    return t


class Tickets:

    def __init__(self):
        self.at, self.used, self.next = {}, {}, {"D": 0, "H": 0}
        self.size = {"D": 3, "H": 2}

    def add(self, kind, *key):
        k = self.next[kind] % self.size[kind]
        self.next[kind] += 1
        n = self.used.get((kind, k), 0)
        self.used[(kind, k)] = n + 1
        assert key not in self.at, key
        self.at[key] = (kind, k, n)


def to_t_count():
    return 4 + 4 * DEPTH


def attention_units(a, half):
    if a == 0:
        return [(g, kc, jp) for g in range(KV) for kc in range(4 * half + 4) for jp in range(2)]
    return [(g,) for g in range(KV)]


def plan():
    t = Tickets()
    for a in range(2):
        t.add("D", "toT", a)
        for i in range(2):
            t.add("D", "qkv", a, i)
        if a == 1:
            t.add("D", "vwin")
        for i in range(2):
            t.add("D", "qT", a, i)
        for i in range(2):
            t.add("D", "kT", a, i)
        for half in range(2):
            units = attention_units(a, half)
            if a == 0:
                for u in units:
                    t.add("D", "S", a, half, *u)
                for g in range(KV):
                    t.add("H", "O", a, half, g)
                for i in range(2):
                    t.add("D", "Ot", a, half, i)
            else:
                for u in units:
                    t.add("D", "S", a, half, *u)
                t.add("D", "O", a, half)
                t.add("D", "Ot", a, half, 0)
            t.add("H", "At", a, half)
            t.add("H", "wo", a, half)
    t.add("D", "toT", 2)
    t.add("H", "gate")
    for i in range(2 * E + 1):
        if i < 2 * E:
            t.add("D", "h", i, 0)
            t.add("D", "h", i, 1)
        if i > 0:
            t.add("H", "eo", i - 1)
    t.add("D", "GT")
    t.add("D", "b2")
    t.add("D", "toT", 3)
    for n in ("lq", "lk", "lkv", "lv"):
        t.add("D", n)
    t.add("H", "lM")
    for n in ("ls", "lo", "loT", "lwo"):
        t.add("D", n)
    for l in range(DEPTH):
        t.add("D", "toT", 4 + 4 * l)
        for i in range(NT + 4):
            if 0 <= i - 2 < NT:
                t.add("D", "fS", l, i - 2)
            if i < NT:
                t.add("D", "fqk", l, i)
            if i - 4 in (3, 7):
                t.add("H", "fwo", l, (i - 4) // 4)
            if 0 <= i - 3 < NT:
                t.add("H", "fO", l, i - 3, 0)
                t.add("H", "fO", l, i - 3, 1)
            if 0 <= i - 1 < NT:
                t.add("D", "fT", l, i - 1)
            if i < NT:
                t.add("H", "fv", l, i)
            if 0 <= i - 2 < NT:
                t.add("D", "fPT", l, i - 2)
        for i in range(1, 4):
            t.add("D", "toT", 4 + 4 * l + i)
        for hb in range(2):
            for c in range(len(CH)):
                t.add("D", "fw1", l, hb, c)
            t.add("H", "fw2", l, hb)
    return t


def build(nc, A):
    tk = plan()
    ctx = ExitStack()
    with ctx:
        def sb(name, shape, dt=F32):
            return ctx.enter_context(nc.sbuf_tensor(name, shape, dt))

        ident = sb("ident", [128, 128])
        ident16 = sb("ident16", [128, 128], F16)
        causal = sb("causal", [128, 128], F16)
        local = sb("local", [128, 128], F16)
        identb = sb("identb", [128, 128], BF16)
        win = sb("win", [128, 2, 128], BF16)
        tri = sb("tri", [128, 128])
        ones = sb("ones", [128, 1])
        rope = [sb(f"rope{a}", [128, NT, 2, HD]) for a in range(2)]
        w_att = [sb("w_global", [128, 192]), sb("w_local", [128, 192])]
        w_ao = [sb("wo_global", [128, 128]), sb("wo_local", [128, 128])]
        wgate = sb("wgate", [128, E])
        bgate = sb("bgate", [128, E])
        rank = sb("rank", [128, E])
        W1 = sb("W1", [128, E, HF])
        b1 = sb("b1", [128, E, HC])
        W2m = sb("W2m", [128, E, HC, 128])
        b2m = sb("b2m", [E, 128])
        lw = sb("lw", [128, 3, HL])
        lwo = sb("lwo", [HL, 128])
        wqkv = sb("wqkv", [128, DEPTH, 3 * INNER])
        wo = sb("wo", [128, DEPTH, 4, 128])
        w1 = sb("w1", [128, DEPTH, 2 * HID])
        fb1 = sb("fb1", [128, DEPTH, 2, len(CH)])
        w2 = sb("w2", [128, DEPTH, len(CH), 128])
        xpos = sb("xpos", [128, DEPTH, NT, 2, 2, DH])

        X = sb("X", [128, NT, 128])
        R = sb("R", [128, NT, 128])
        N = sb("N", [128, NT, 128])
        Q = sb("Q", [128, NT, 128])
        xT = sb("xT", [128, PAD + S])
        hT = sb("hT", [128, S])
        st_a = sb("st_a", [128, 160])
        st_m = sb("st_m", [128, 160])
        st_i = sb("st_i", [128, 160], I32)
        st_y = sb("st_y", [128, 160])
        st_t = sb("st_t", [128, 160])
        rden = sb("rden", [128, 64])
        gates = sb("gates", [128, NT, E])
        gtmp = [sb(f"gtmp{i}", [128, NT, E]) for i in range(4)]
        gone = [sb(f"gone{i}", [128, NT]) for i in range(3)]

        arena_bytes = 97 * 1024
        arena = sb("arena", [128, arena_bytes // 4])
        cursor = [0]

        def carve(shape, dt=F32):
            n = int(np.prod(shape[1:]))
            size = {F32: 4, F16: 2}[dt]
            words = (n * size + 31) // 32 * 8
            v = arena[0:shape[0], cursor[0]:cursor[0] + words]
            if dt is F16:
                v = v.bitcast(F16)
            v = v[:, 0:n]
            cursor[0] += words
            assert cursor[0] * 4 <= arena_bytes, cursor[0] * 4
            names = "abcde"[:len(shape) - 1]
            if len(shape) > 2:
                v = v.rearrange(f"p ({' '.join(names)}) -> p {' '.join(names)}", **{c: s for c, s in zip(names[1:], shape[2:])})
            return v

        cursor[0] = 0
        QK = carve([128, NT, 160])
        QR = carve([128, NT, 160])
        Qs = carve([128, NT, GQ, 4, 32], F16)
        arena_rope = carve([128, NT, 160])
        QT = carve([128, GQ, S], F16)
        KT = carve([128, KV, PAD + S], F16)
        P = [carve([128, 1024]) for _ in range(PRING)]
        OT = carve([128, KV, 512])
        At = carve([128, NT // 2, 128])
        AT = carve([128, 512])
        Kpad = carve([128, NT, KV, 4, KV, HD], F16)
        Vaug = carve([128, NT, KV, 32])
        Vwin = carve([128, 16, KV, 2, 16])

        cursor[0] = 0
        hbuf = [carve([128, HC, 512]) for _ in range(3)]
        GT = carve([E, S])

        cursor[0] = 0
        lqT, lkT, lvT, lz, lqz = (carve([HL, S]) for _ in range(5))
        lm = [carve([128, S]) for _ in range(3)]
        lone = carve([HL, S])
        lkt = carve([128, NT, HL])
        lvt = carve([128, NT, HL])
        lM = carve([HL, NT, HL])
        lA = carve([128, NT, 128])
        lO = carve([128, NT, HL])
        lOT = carve([HL, S])

        cursor[0] = 0
        SQb = carve([128, 16, DH])
        T1 = [carve([128, 16, DH]) for _ in range(2)]
        T2 = carve([128, 16, DH])
        fqB = carve([128, 2, 4, 2, 64])
        fkT = [carve([128, 4, 192]) for _ in range(2)]
        V = [carve([128, INNER]) for _ in range(VRING)]
        Vsh = [carve([128, INNER]) for _ in range(VRING)]
        fP = carve([128, 8, 128])
        fPT = carve([128, 8, 128])
        fOT = carve([128, 4, 512])
        U = carve([128, 3, 512])
        GL = [carve([128, 512]) for i in range(2)]

        fss = sb("fss", [128, 16])
        fm = sb("fm", [128, 16])
        fi = sb("fi", [128, 16], I32)
        fy = sb("fy", [128, 16])
        ft = sb("ft", [128, 16])
        fnm = sb("fnm", [128, 8])
        fden = sb("fden", [128, 8])
        frd = sb("frd", [128, 8])

        PD = [ctx.enter_context(nc.psum_tensor(f"PD{i}", [128, 1024], F32)) for i in range(3)]
        PH = [ctx.enter_context(nc.psum_tensor(f"PH{i}", [128, 512], F32)) for i in range(2)]

        sems = {}

        def sg(name):
            if name not in sems:
                sems[name] = ctx.enter_context(nc.semaphore("s_" + name))
            return sems[name]

        def slot(*key):
            kind, k, n = tk.at[key]
            return (PD if kind == "D" else PH)[k]

        def fill(pe, *key):
            kind, k, n = tk.at[key]
            if n:
                pe.wait_ge(sg(f"free_{kind}{k}"), n)
            return (PD if kind == "D" else PH)[k][:, :]

        def is_free(eng, *key):
            kind, k, n = tk.at[key]
            eng.wait_ge(sg(f"free_{kind}{k}"), n + 1)

        def filled(*key):
            kind, k, n = tk.at[key]
            return sg(f"full_{kind}{k}")

        def read(eng, *key):
            kind, k, n = tk.at[key]
            eng.wait_ge(sg(f"full_{kind}{k}"), n + 1)
            return (PD if kind == "D" else PH)[k][:, :]

        def freed(*key):
            kind, k, n = tk.at[key]
            return sg(f"free_{kind}{k}")

        def spread(ap):
            return ap.rearrange("p (T u w q) -> p T w u q", T=4, u=4, w=2)

        raw = {}
        cursor[0] = 0
        for n, shape in (("g_wq", [128, 128]), ("g_kv_down", [128, LAT]), ("l_wq", [128, 128]), ("l_wk", [128, 32]),
                         ("l_wv", [128, 32]), ("n1", [128, 1]), ("n2", [128, 1]), ("up", [LAT, 64]), ("downT", [LAT, 128]),
                         ("lg", [128, DEPTH]), ("lb", [128, DEPTH]), ("b1c", [128, DEPTH, 2, len(CH)]),
                         ("w1", [128, DEPTH, 2 * HID]), ("qs", [128, DEPTH, 2, DH]), ("xp", [128, NT, 2, 2, DH]),
                         ("win", [128, 2, 128]), ("identf", [128, 128])):
            raw[n] = carve(shape)

        loads = []

        def ld(dst, src):
            loads.append((dst, src))

        ld(ident[:, :], A["c_ident"])
        ld(causal[:, :], A["c_causal"])
        ld(local[:, :], A["c_local"])
        ld(raw["win"], A["c_win"])
        ld(tri[:, :], A["c_tri"])
        ld(rope[0][:, :, :, :], A["c_rope_g"])
        ld(rope[1][:, :, :, :], A["c_rope_l"])
        ld(raw["xp"], A["c_xpos"])
        ld(raw["g_wq"], A["L0_attn_g_wq"])
        ld(raw["g_kv_down"], A["L0_attn_g_kv_down"])
        ld(raw["up"][:, 0:32], A["L0_attn_g_k_up"])
        ld(raw["up"][:, 32:64], A["L0_attn_g_v_up"])
        ld(raw["l_wq"], A["L0_attn_l_wq"])
        ld(raw["l_wk"], A["L0_attn_l_wk"])
        ld(raw["l_wv"], A["L0_attn_l_wv"])
        ld(raw["n1"], A["L0_attn_norm1_w"].rearrange("(p a) -> p a", a=1))
        ld(raw["n2"], A["L0_attn_norm2_w"].rearrange("(p a) -> p a", a=1))
        ld(w_ao[0][:, :], A["L0_attn_g_wo"])
        ld(w_ao[1][:, :], A["L0_attn_l_wo"])
        ld(wgate[:, :], A["L0_ffn_Wg"])
        ld(bgate[:, :], A["L0_ffn_bg"].partition_broadcast(128))
        ld(rank[:, :], A["c_rank"].partition_broadcast(128))
        for e in range(E):
            ld(W1[:, e, :], A["L0_ffn_W1"][e])
            ld(W2m[:, e, :, :], A["L0_ffn_W2"][e].rearrange("(c p) f -> p c f", p=128))
        ld(b1[:, :, :], A["L0_ffn_b1"])
        ld(b2m[:, :], A["L0_ffn_b2"])
        for i, n in enumerate(("L1_attn_W_q", "L1_attn_W_k", "L1_attn_W_v")):
            ld(lw[:, i, :], A[n])
        ld(lwo[:, :], A["L1_attn_W_o"])
        for l in range(DEPTH):
            ld(wqkv[:, l, :], A["L1_ffn_wqkv"][l])
            ld(wo[:, l, :, :], A["L1_ffn_wo"][l].rearrange("(c p) f -> p c f", p=128))
            ld(raw["w1"][:, l, :], A["L1_ffn_w1"][l])
            for c, (c0, m) in enumerate(CH):
                ld(w2[0:m, l, c, :], A["L1_ffn_w2"][l][c0:c0 + m, :])
                for i in range(2):
                    ld(raw["b1c"][0:m, l, i, c:c + 1],
                       A["L1_ffn_b1"][l][i * HID + c0:i * HID + c0 + m].rearrange("(p a) -> p a", a=1))
            ld(w2[CH[-1][1]:CH[-1][1] + 1, l, len(CH) - 1, :], A["L1_ffn_b2"][l:l + 1, :])
            ld(raw["lg"][:, l:l + 1], A["L1_ffn_ln_g"][l].rearrange("(p a) -> p a", a=1))
            ld(raw["lb"][:, l:l + 1], A["L1_ffn_ln_b"][l].rearrange("(p a) -> p a", a=1))
            ld(raw["qs"][:, l, 0, :], A["L1_ffn_q_scale"][l].partition_broadcast(128))
            ld(raw["qs"][:, l, 1, :], A["L1_ffn_k_scale"][l].partition_broadcast(128))

        with nc.Block() as block:
            @block.sync
            def _(sp):
                for dst, src in loads:
                    sp.dma_start(dst, src).then_inc(sg("weights"), 16)

            @block.gpsimd
            def _(pool):
                pool.memset(xT[:, 0:PAD], 0.0)
                pool.memset(hT[:, :], 0.0)
                pool.memset(ones[:, :], 1.0)

            @block.vector
            def _(dve):
                dve.wait_ge(sg("weights"), 16 * len(loads))
                dve.tensor_copy(ident16[:, :], ident[:, :])
                dve.tensor_copy(identb[:, :], ident[:, :])
                dve.tensor_copy(win[:, :, :], raw["win"])
                dve.tensor_scalar(w_att[0][:, 0:128], raw["g_wq"], raw["n1"][:, 0:1], None, ALU.mult)
                dve.tensor_scalar(w_att[1][:, 0:128], raw["l_wq"], raw["n2"][:, 0:1], None, ALU.mult)
                dve.tensor_scalar(w_att[1][:, 128:160], raw["l_wk"], raw["n2"][:, 0:1], None, ALU.mult)
                dve.tensor_scalar(w_att[1][:, 160:192], raw["l_wv"], raw["n2"][:, 0:1], None, ALU.mult)
                for l in range(DEPTH):
                    dve.tensor_scalar(w1[:, l, :], raw["w1"][:, l, :], raw["lg"][:, l:l + 1], None, ALU.mult)
                    for i in range(2):
                        qs = raw["qs"][:, l, i:i + 1, :]
                        dve.tensor_tensor(xpos[:, l, :, 0, i, :], raw["xp"][:, :, 0, i, :],
                                          qs.to_broadcast([128, NT, DH]), ALU.mult)
                        for hh in range(2):
                            a, b = 32 * hh, 32 * (1 - hh)
                            dve.tensor_tensor(xpos[:, l, :, 1, i, a:a + 32], raw["xp"][:, :, 1, i, a:a + 32],
                                              qs[:, :, b:b + 32].to_broadcast([128, NT, 32]), ALU.mult)
                dve.wait_ge(sg("w_down"), 1)
                dve.tensor_copy(raw["downT"], PH[0][0:LAT, 0:128]).then_inc(sg("w_downT"), 1)
                dve.wait_ge(sg("w_kv"), 1)
                dve.tensor_scalar(w_att[0][:, 128:192], PD[0][:, 0:64], raw["n1"][:, 0:1], None, ALU.mult)
                for l in range(DEPTH):
                    for i in range(2):
                        for c, (c0, m) in enumerate(CH):
                            k = (l * 2 + i) * len(CH) + c
                            dve.tensor_tensor(fb1[0:m, l, i, c:c + 1], PD[1][0:m, k:k + 1],
                                              raw["b1c"][0:m, l, i, c:c + 1], ALU.add)

            @block.tensor
            def _(pe):
                pe.wait_ge(sg("weights"), 16 * len(loads))
                pe.transpose(PH[0][0:LAT, 0:128], raw["g_kv_down"], ident[:, :]).then_inc(sg("w_down"), 1)
                for l in range(DEPTH):
                    for i in range(2):
                        for c, (c0, m) in enumerate(CH):
                            k = (l * 2 + i) * len(CH) + c
                            pe.matmul(PD[1][0:m, k:k + 1], raw["w1"][:, l, i * HID + c0:i * HID + c0 + m],
                                      raw["lb"][:, l:l + 1], start=True, stop=True)
                pe.wait_ge(sg("w_downT"), 1)
                pe.matmul(PD[0][:, 0:64], raw["downT"], raw["up"], start=True, stop=True).then_inc(sg("w_kv"), 1)

        x_in, x_out = A["L0_attn_hidden"], A["out"]
        with nc.Fori(0, B) as b:
            with nc.Block() as block:
                @block.sync
                def _(sp):
                    src = x_in[bass.ds(b, 1)].rearrange("b (T u w q) d -> (b u) q T w d", T=4, u=4, w=2)
                    dst = x_out[bass.ds(b, 1)].rearrange("b (T u w q) d -> (b u) q T w d", T=4, u=4, w=2)
                    Xv = X[:, :, :].rearrange("p (T w) d -> p T w d", w=2)
                    Nv = N[:, :, :].rearrange("p (T w) d -> p T w d", w=2)
                    for u in range(4):
                        for T in range(4):
                            sp.dma_start(Xv[32 * u:32 * u + 32, T], src[u, :, T]).then_inc(sg("x_in"), 16)
                    for l in range(DEPTH):
                        for t in range(NT):
                            i = l * NT + t
                            is_free(sp, "fv", l, t)
                            if i >= VRING:
                                read(sp, "fO", (i - VRING) // NT, (i - VRING) % NT, 0)
                            before = V[(i - 1) % VRING][64:128, :] if t > 0 else V[i % VRING][0:64, :]
                            sp.dma_start(Vsh[i % VRING][0:64, :], before).then_inc(sg(f"v_shift{i % VRING}"), 16)
                            sp.dma_start(Vsh[i % VRING][64:128, :], V[i % VRING][0:64, :]).then_inc(sg(f"v_shift{i % VRING}"), 16)
                    sp.wait_ge(sg("final"), 1)
                    for u in range(4):
                        for T in range(4):
                            sp.dma_start(dst[u, :, T], Nv[32 * u:32 * u + 32, T]).then_inc(sg("x_out"), 16)
                    sp.wait_ge(sg("x_out"), 256)

                @block.tensor
                def _(pe):
                    def by_tiles(p, t):
                        v = p.rearrange("p (T w u q) -> p T u w q", T=4, w=2, u=4)
                        return v[:, t // 2, 2 * (t % 2):2 * (t % 2) + 2]

                    def to_t(i, src, place):
                        pe.wait_ge(sg("src"), i + 1)
                        p = fill(pe, "toT", i)
                        for t in range(NT):
                            ins = pe.transpose(place(p, t), src[:, t, :], ident[:, :])
                        ins.then_inc(filled("toT", i), 1)

                    def in_order(p, t):
                        return spread(p)[:, t // 2, t % 2]

                    def as_is(p, t):
                        return p[:, 128 * t:128 * t + 128]

                    nP = 0
                    for a in range(2):
                        to_t(a, N, in_order)
                        pe.wait_ge(sg("xT"), a + 1)
                        nq = 192 if a == 0 else 160
                        for i in range(2):
                            p = fill(pe, "qkv", a, i).rearrange("p (t n) -> p t n", t=4)
                            for t in range(4):
                                c = PAD + 128 * (4 * i + t)
                                ins = pe.matmul(p[:, t, 0:nq], xT[:, c:c + 128], w_att[a][:, 0:nq], start=True, stop=True)
                            ins.then_inc(filled("qkv", a, i), 1)
                        if a == 1:
                            p = fill(pe, "vwin").rearrange("p (u n) -> p u n", u=16)
                            for u in range(16):
                                for w in range(2):
                                    c = 64 * u + 32 * w
                                    ins = pe.matmul(p[64 * w:64 * w + 64, u, 0:32], xT[:, c:c + 64], w_att[1][:, 160:192],
                                                    start=True, stop=True)
                            ins.then_inc(filled("vwin"), 1)
                        pe.wait_ge(sg("split"), a + 1)
                        for i in range(2):
                            p = fill(pe, "qT", a, i).bitcast(F16).rearrange("p (j n) -> p j n", j=2)
                            for j in range(2):
                                for t in range(NT):
                                    src = Qs[:, t, 2 * i + j].rearrange("p s n -> p (s n)")
                                    ins = pe.transpose(p[:, j, 128 * t:128 * t + 128], src, ident16[:, :])
                            ins.then_inc(filled("qT", a, i), 1)
                        for i in range(2):
                            p = fill(pe, "kT", a, i).bitcast(F16).rearrange("p (j n) -> p j n", j=2)
                            for j in range(2):
                                for t in range(NT):
                                    src = Kpad[:, t, 2 * i + j].rearrange("p s g d -> p (s g d)")
                                    ins = pe.transpose(p[:, j, 128 * t:128 * t + 128], src, ident16[:, :])
                            ins.then_inc(filled("kT", a, i), 1)
                        pe.wait_ge(sg("QT"), 2 * a + 2)
                        pe.wait_ge(sg("KT"), 2 * a + 2)
                        pe.wait_ge(sg("V"), a + 1)
                        for half in range(2):
                            if a == 0:
                                units = attention_units(0, half)
                                ready = []

                                def values(g, kc, first):
                                    kcs = 4 * half + 4
                                    n = min(512, 512 - 128 * (kc - 4 * half))
                                    o = slot("O", 0, half, g)
                                    if kc == 0:
                                        fill(pe, "O", 0, half, g)
                                    pe.wait_ge(sg("P"), first + 2)
                                    for j in range(4):
                                        pb = P[(first + j // 2) % PRING].rearrange("p (j n) -> p j n", j=2)
                                        ins = pe.matmul(o[32 * j:32 * j + 32, 512 - n:512], Vaug[:, kc, g, :],
                                                        pb[:, j % 2, 0:n], start=(kc == 0), stop=(kc == kcs - 1),
                                                        skip_group_check=True)
                                        if j % 2 and not (j == 3 and kc == kcs - 1):
                                            ins.then_inc(sg("pv"), 1)
                                    if kc == kcs - 1:
                                        ins.then_inc(filled("O", 0, half, g), 1)

                                lag = None
                                for (g, kc, jp) in units:
                                    if jp == 0:
                                        first = nP
                                    n = min(512, 512 - 128 * (kc - 4 * half))
                                    p = fill(pe, "S", 0, half, g, kc, jp).rearrange("p (j n) -> p j n", j=2)
                                    q0 = 512 * half + 512 - n
                                    for j in range(2):
                                        diag = kc >= 4 * half
                                        c = PAD + 128 * kc
                                        if diag:
                                            pe.matmul(p[:, j, 0:128], causal[:, :], ident16[:, :],
                                                      start=True, stop=False, skip_group_check=True)
                                        ins = pe.matmul(p[:, j, 0:n], KT[:, g, c:c + 128], QT[:, 2 * jp + j, q0:q0 + n],
                                                        start=not diag, stop=True, skip_group_check=True)
                                    ins.then_inc(filled("S", 0, half, g, kc, jp), 1)
                                    nP += 1
                                    if jp == 1:
                                        if lag is not None:
                                            values(*lag)
                                        lag = (g, kc, first)
                                values(*lag)
                                for i in range(2):
                                    p = fill(pe, "Ot", 0, half, i).rearrange("p (g t n) -> p g t n", g=2, t=4)
                                    for gg in range(2):
                                        g = 2 * i + gg
                                        pe.wait_ge(sg("OT"), 4 * half + g + 1)
                                        for t in range(4):
                                            ins = pe.transpose(p[:, gg, t, :], OT[:, g, 128 * t:128 * t + 128], ident[:, :])
                                    ins.then_inc(filled("Ot", 0, half, i), 1)
                            else:
                                first = nP
                                for g in range(KV):
                                    p = fill(pe, "S", 1, half, g)
                                    for k in range(2):
                                        pe.matmul(p[:, 512 * k:512 * k + 512].rearrange("p (a b) -> p a b", b=32), local[:, :],
                                                  ident16[:, 0:32].unsqueeze(1).to_broadcast([128, 16, 32]),
                                                  start=True, stop=False, skip_group_check=True)
                                    for u8 in range(8):
                                        for w in range(2):
                                            t0 = 64 * (8 * half + u8) + 32 * w
                                            o = p[64 * w:64 * w + 64, 128 * u8:128 * u8 + 128].rearrange("p (j q) -> p j q", j=4)
                                            ins = pe.matmul(o, KT[:, g, t0:t0 + 64], QT[:, :, t0:t0 + 32],
                                                            start=False, stop=True, skip_group_check=True)
                                    ins.then_inc(filled("S", 1, half, g), 1)
                                    nP += 1
                                o = fill(pe, "O", 1, half)
                                pe.wait_ge(sg("P"), first + 4)
                                for u8 in range(8):
                                    for g in range(KV):
                                        ins = pe.matmul(o[32 * g:32 * g + 32, 128 * u8:128 * u8 + 128],
                                                        Vwin[:, 8 * half + u8, g].rearrange("p a b -> p (a b)"),
                                                        P[(first + g) % PRING][:, 128 * u8:128 * u8 + 128],
                                                        start=True, stop=True, skip_group_check=True)
                                ins.then_inc(filled("O", 1, half), 1)
                                pe.wait_ge(sg("OT"), 8 + half + 1)
                                p = fill(pe, "Ot", 1, half, 0).rearrange("p (T j n) -> p T j n", T=2, j=4)
                                for T in range(2):
                                    for j in range(4):
                                        c = 256 * j + 128 * T
                                        ins = pe.transpose(p[:, T, j, :], OT.rearrange("p g n -> p (g n)")[:, c:c + 128], ident[:, :])
                                ins.then_inc(filled("Ot", 1, half, 0), 1)
                            pe.wait_ge(sg("A"), 2 * a + half + 1)
                            p = fill(pe, "At", a, half)
                            for t in range(4):
                                ins = pe.transpose(p[:, 128 * t:128 * t + 128], At[:, t, :], ident[:, :])
                            ins.then_inc(filled("At", a, half), 1)
                            pe.wait_ge(sg("AT"), 2 * a + half + 1)
                            p = fill(pe, "wo", a, half)
                            for t in range(4):
                                ins = pe.matmul(p[:, 128 * t:128 * t + 128], AT[:, 128 * t:128 * t + 128], w_ao[a][:, :],
                                                start=True, stop=True)
                            ins.then_inc(filled("wo", a, half), 1)

                    to_t(2, X, as_is)
                    pe.wait_ge(sg("xT"), 3)
                    p = fill(pe, "gate")
                    for t in range(NT):
                        ins = pe.matmul(p[:, E * t:E * t + E], xT[:, PAD + 128 * t:PAD + 128 * t + 128], wgate[:, :], start=True, stop=True)
                    ins.then_inc(filled("gate"), 1)
                    for i in range(2 * E + 1):
                        if i < 2 * E:
                            hb, e = divmod(i, E)
                            for k in range(2):
                                p = fill(pe, "h", i, k)
                                for c in range(2):
                                    hc = 2 * k + c
                                    ins = pe.matmul(p[:, 512 * c:512 * c + 512], W1[:, e, 128 * hc:128 * hc + 128],
                                                    xT[:, PAD + 512 * hb:PAD + 512 * hb + 512], start=True, stop=True)
                                ins.then_inc(filled("h", i, k), 1)
                        if i > 0:
                            hb, e = divmod(i - 1, E)
                            p = fill(pe, "eo", i - 1)
                            pe.wait_ge(sg("gelu"), 4 * i)
                            hv = hbuf[(i - 1) % 3]
                            for t in range(4):
                                for c in range(HC):
                                    ins = pe.matmul(p[:, 128 * t:128 * t + 128], hv[:, c, 128 * t:128 * t + 128], W2m[:, e, c, :],
                                                    start=(c == 0), stop=(c == HC - 1))
                            ins.then_inc(filled("eo", i - 1), 1)
                    pe.wait_ge(sg("gates"), 1)
                    p = fill(pe, "GT")
                    for t in range(NT):
                        ins = pe.transpose(p[0:E, 128 * t:128 * t + 128], gates[:, t, :], ident[:, :])
                    ins.then_inc(filled("GT"), 1)
                    pe.wait_ge(sg("GT"), 1)
                    p = fill(pe, "b2")
                    for t in range(NT):
                        ins = pe.matmul(p[:, 128 * t:128 * t + 128], GT[:, 128 * t:128 * t + 128], b2m[:, :], start=True, stop=True)
                    ins.then_inc(filled("b2"), 1)

                    to_t(3, X, in_order)
                    pe.wait_ge(sg("xT"), 4)

                    def project(name, w):
                        p = fill(pe, name)
                        for k in range(2):
                            ins = pe.matmul(p[0:HL, 512 * k:512 * k + 512], lw[:, w, :],
                                            xT[:, PAD + 512 * k:PAD + 512 * k + 512], start=True, stop=True)
                        ins.then_inc(filled(name), 1)

                    project("lq", 0)
                    project("lk", 1)
                    p = fill(pe, "lkv")
                    for t in range(NT):
                        ins = pe.matmul(p[:, 128 * t:128 * t + 128], xT[:, PAD + 128 * t:PAD + 128 * t + 128],
                                        lw[:, 1:3, :].rearrange("p a b -> p (a b)"), start=True, stop=True)
                    ins.then_inc(filled("lkv"), 1)
                    project("lv", 2)
                    pe.wait_ge(sg("l_tok"), 1)
                    p = fill(pe, "lM")
                    for t in range(NT - 1):
                        ins = pe.matmul(p[0:HL, HL * t:HL * t + HL], lvt[:, t, :], lkt[:, t, :], start=True, stop=True)
                    ins.then_inc(filled("lM"), 1)
                    pe.wait_ge(sg("l_v"), 1)
                    p = fill(pe, "ls")
                    for t in range(NT):
                        ins = pe.matmul(p[:, 128 * t:128 * t + 128], lvT[:, 128 * t:128 * t + 128],
                                        lqT[:, 128 * t:128 * t + 128], start=True, stop=True)
                    ins.then_inc(filled("ls"), 1)
                    pe.wait_ge(sg("l_A"), 1)
                    p = fill(pe, "lo")
                    for t in range(NT):
                        c = 128 * t
                        pe.matmul(p[:, c:c + HL], lA[:, t, :], lkt[:, t, :], start=True, stop=(t == 0))
                        if t:
                            pe.matmul(p[:, c:c + HL], lqT[:, c:c + 128], lM[:, t, :], start=False, stop=True)
                        ins = pe.matmul(p[:, c + HL:c + HL + 1], lqz[:, c:c + 128], ones[0:HL, :], start=True, stop=True)
                    ins.then_inc(filled("lo"), 1)
                    pe.wait_ge(sg("l_O"), 1)
                    p = fill(pe, "loT")
                    for t in range(NT):
                        ins = pe.transpose(by_tiles(p[0:HL, :], t), lO[:, t, :], ident[:, :])
                    ins.then_inc(filled("loT"), 1)
                    pe.wait_ge(sg("l_OT"), 1)
                    p = fill(pe, "lwo")
                    for t in range(NT):
                        ins = pe.matmul(p[:, 128 * t:128 * t + 128], lOT[:, 128 * t:128 * t + 128], lwo[:, :], start=True, stop=True)
                    ins.then_inc(filled("lwo"), 1)

                    for l in range(DEPTH):
                        to_t(4 + 4 * l, X, in_order)
                        pe.wait_ge(sg("hT"), 2 * l + 1)
                        for i in range(NT + 4):
                            t = i - 2
                            if 0 <= t < NT:
                                p = fill(pe, "fS", l, t)
                                for w in range(2):
                                    pe.matmul(p[:, 512 * w:512 * w + 512].rearrange("p (a b) -> p a b", b=128), win[:, min(2 * t + w, 1), :],
                                              identb[:, :].unsqueeze(1).to_broadcast([128, 4, 128]),
                                              start=True, stop=False, skip_group_check=True)
                                is_free(pe, "fT", l, t)
                                for w in range(2):
                                    for c in range(4):
                                        ins = pe.matmul(p[:, 512 * w + 128 * c:512 * w + 128 * c + 128],
                                                        fqB[:, w, c].rearrange("p r n -> p (r n)"),
                                                        fkT[t % 2][:, c, 64 * w:64 * w + 128],
                                                        start=False, stop=True, skip_group_check=True)
                                    ins.then_inc(filled("fS", l, t) if w else sg("scores"), 1)
                            if i < NT:
                                p = fill(pe, "fqk", l, i)
                                for k in range(2):
                                    ins = pe.matmul(p[:, 512 * k:512 * k + 512], hT[:, 128 * i:128 * i + 128],
                                                    wqkv[:, l, 512 * k:512 * k + 512], start=True, stop=True)
                                ins.then_inc(filled("fqk", l, i), 1)
                            if i - 4 in (3, 7):
                                g = (i - 4) // 4
                                is_free(pe, "fO", l, i - 4, 0)
                                is_free(pe, "fO", l, i - 4, 1)
                                p = fill(pe, "fwo", l, g)
                                for t in range(4):
                                    for c in range(4):
                                        ins = pe.matmul(p[:, 128 * t:128 * t + 128], fOT[:, c, 128 * t:128 * t + 128], wo[:, l, c, :],
                                                        start=(c == 0), stop=(c == 3))
                                ins.then_inc(filled("fwo", l, g), 1)
                            t = i - 3
                            k = l * NT + t
                            if 0 <= t < NT:
                                is_free(pe, "fPT", l, t)
                                is_free(pe, "fv", l, t)
                                for w in (1, 0):
                                    if w == 0:
                                        pe.wait_ge(sg(f"v_shift{k % VRING}"), 32 * (k // VRING + 1))
                                    p = fill(pe, "fO", l, t, 1 - w)
                                    for c in range(4):
                                        vv = (Vsh if w == 0 else V)[k % VRING]
                                        ins = pe.matmul(p[:, 128 * c:128 * c + 128], vv[:, 128 * c:128 * c + 128],
                                                        fPT[:, 4 * w + c, :], start=True, stop=True)
                                    ins.then_inc(filled("fO", l, t, 1 - w), 1)
                            t = i - 1
                            k = l * NT + t
                            if 0 <= t < NT:
                                pe.wait_ge(sg("unit"), k + 1)
                                p = fill(pe, "fT", l, t)
                                for h in (4, 5, 6, 7, 0, 1, 2, 3):
                                    ins = pe.transpose(p[:, 128 * h:128 * h + 128],
                                                       T1[k % 2].rearrange("p a b -> p (a b)")[:, 128 * h:128 * h + 128], ident[:, :])
                                ins.then_inc(filled("fT", l, t), 1)
                            if i < NT:
                                p = fill(pe, "fv", l, i)
                                pe.matmul(p, hT[:, 128 * i:128 * i + 128], wqkv[:, l, 1024:1536],
                                          start=True, stop=True).then_inc(filled("fv", l, i), 1)
                            t = i - 2
                            k = l * NT + t
                            if 0 <= t < NT:
                                p = fill(pe, "fPT", l, t)
                                for h in range(8):
                                    if h % 4 == 0:
                                        pe.wait_ge(sg("softmax"), 2 * k + 1 + h // 4)
                                    ins = pe.transpose(p[:, 128 * h:128 * h + 128], fP[:, h, :], ident[:, :])
                                ins.then_inc(filled("fPT", l, t), 1)
                        to_t(5 + 4 * l, X, in_order)
                        pe.wait_ge(sg("hT"), 2 * l + 2)
                        p = fill(pe, "toT", 6 + 4 * l)
                        for t in range(NT):
                            ins = pe.transpose(p[:, 128 * t:128 * t + 128], hT[:, 128 * t:128 * t + 128], ident[:, :])
                        ins.then_inc(filled("toT", 6 + 4 * l), 1)
                        to_t(7 + 4 * l, N, by_tiles)
                        pe.wait_ge(sg("xT"), 5 + l)
                        for hb in range(2):
                            for c, (c0, m) in enumerate(CH):
                                p = fill(pe, "fw1", l, hb, c)
                                for k in range(2):
                                    ins = pe.matmul(p[0:m, 512 * k:512 * k + 512], w1[:, l, HID * k + c0:HID * k + c0 + m],
                                                    xT[:, PAD + 512 * hb:PAD + 512 * hb + 512], start=True, stop=True)
                                ins.then_inc(filled("fw1", l, hb, c), 1)
                            pe.wait_ge(sg("U"), (2 * l + hb + 1) * len(CH))
                            p = fill(pe, "fw2", l, hb)
                            for t in range(4):
                                for c, (c0, m) in enumerate(CH):
                                    last = c == len(CH) - 1
                                    mm = m + 1 if last else m
                                    ins = pe.matmul(p[:, 128 * t:128 * t + 128], U[0:mm, c, 128 * t:128 * t + 128], w2[0:mm, l, c, :],
                                                    start=(c == 0), stop=last)
                            ins.then_inc(filled("fw2", l, hb), 1)

                def head_outputs(eng, l, t, w):
                    p = read(eng, "fO", l, t, 1 - w).rearrange("p (c r w q) -> p c r w q", c=4, r=2, w=2)
                    if (l or t) and t % 4 == 0:
                        k = l * NT + t - 4
                        read(eng, "fwo", k // NT, (k % NT) // 4)
                    to = fOT.rearrange("p c (T w u q) -> p c T w u q", T=2, w=2, u=4)
                    for r in range(2):
                        rr = slice(64 * r, 64 * r + 64)
                        o = to[rr, :, (t % 4) // 2, :, 2 * (t % 2) + w, :]
                        if eng is nc.scalar:
                            ins = eng.activation(o, p[rr, :, r], ACT.Copy)
                        else:
                            ins = eng.tensor_copy(o, p[rr, :, r])
                    ins.then_inc(freed("fO", l, t, 1 - w), 1)

                def numerators_read(k):
                    n = [len(attention_units(0, 0)), len(attention_units(0, 1))]
                    if k >= sum(n):
                        j = k - sum(n)
                        t = tk.at[("O", 1, j // KV)]
                        return sg(f"full_{t[0]}{t[1]}"), t[2] + 1
                    half = int(k >= n[0])
                    i = k - half * n[0]
                    g, kc, jp = attention_units(0, half)[i]
                    if kc == 4 * half + 3 and jp == 1:
                        t = tk.at[("O", 0, half, g)]
                        return sg(f"full_{t[0]}{t[1]}"), t[2] + 1
                    done = 4 * half + g
                    return sg("pv"), k + 1 - done

                @block.scalar
                def _(act):
                    def out_xT(i, k):
                        p = read(act, "toT", i)
                        act.activation(xT[:, PAD:PAD + S], p, ACT.Copy).then_inc(freed("toT", i), 1)
                        act.wait_ge(freed("toT", i), tk.at[("toT", i)][2] + 1)
                        act.sem_inc(sg("xT"), 1)

                    nP = 0
                    gone_units = 0
                    for a in range(2):
                        out_xT(a, a)
                        act.wait_ge(sg("set"), 7)
                        for i in range(2):
                            p = read(act, "qkv", a, i).rearrange("p (t n) -> p t n", t=4)
                            if a == 0:
                                act.activation(Vaug[:, 4 * i:4 * i + 4, :, 0:HD],
                                               p[:, :, 160:192].rearrange("p t (g d) -> p t g d", g=KV), ACT.Copy).then_inc(sg("V_part"), 1)
                            act.activation(QK[:, 4 * i:4 * i + 4, :], p[:, :, 0:160], ACT.Copy).then_inc(sg("qk"), 1)
                            if a == 0:
                                act.wait_ge(sg("V_part"), i + 1)
                            act.wait_ge(sg("qk"), 2 * a + i + 1)
                            act.sem_inc(freed("qkv", a, i), 1)
                        if a == 0:
                            act.sem_inc(sg("V"), 1)
                        else:
                            p = read(act, "vwin").rearrange("p (u n) -> p u n", u=16)
                            for w in range(2):
                                act.activation(Vwin[64 * w:64 * w + 64, :, :, w, 0:HD],
                                               p[64 * w:64 * w + 64, :, 0:32].rearrange("p u (g d) -> p u g d", g=KV),
                                               ACT.Copy).then_inc(sg("V_part"), 1)
                            act.wait_ge(sg("V_part"), 4)
                            act.sem_inc(freed("vwin"), 1)
                            act.sem_inc(sg("V"), 1)
                        act.wait_ge(sg("qn"), a + 1)
                        for s in range(2):
                            act.activation(Qs[:, :, :, s, :], QR[:, :, 0:128].rearrange("p t (j n) -> p t j n", j=GQ),
                                           ACT.Copy).then_inc(sg("q_hi"), 1)
                        for i in range(2):
                            p = read(act, "qT", a, i).bitcast(F16).rearrange("p (j n) -> p j n", j=2)
                            act.activation(QT[:, 2 * i:2 * i + 2, :], p, ACT.Copy).then_inc(sg("QT"), 1)
                            act.wait_ge(sg("QT"), 2 * a + i + 1)
                            act.sem_inc(freed("qT", a, i), 1)
                        for half in range(2):
                            for u in attention_units(a, half):
                                if a == 0:
                                    n = min(512, 512 - 128 * (u[1] - 4 * half))
                                else:
                                    n = 512
                                p = read(act, "S", a, half, *u).rearrange("p (j n) -> p j n", j=2)
                                if nP >= PRING:
                                    act.wait_ge(*numerators_read(nP - PRING))
                                pb = P[nP % PRING].rearrange("p (j n) -> p j n", j=2)
                                act.activation(pb[:, :, 0:n], p[:, :, 0:n], ACT.Exp, scale=INV_SQRT_HD).then_inc(freed("S", a, half, *u), 1)
                                nP += 1
                                act.wait_ge(freed("S", a, half, *u), tk.at[("S", a, half, *u)][2] + 1)
                                act.sem_inc(sg("P"), 1)
                            p = read(act, "At", a, half)
                            act.activation(AT, p, ACT.Copy).then_inc(sg("AT"), 1)
                            act.wait_ge(sg("AT"), 2 * a + half + 1)
                            act.sem_inc(freed("At", a, half), 1)
                    out_xT(2, 2)
                    act.wait_ge(sg("g_lg"), 1)
                    act.activation(gtmp[1][:, :, :], gtmp[0][:, :, :], ACT.Exp).then_inc(sg("g_exp"), 1)
                    for i in range(2 * E):
                        hb, e = divmod(i, E)
                        if i >= 3:
                            read(act, "eo", i - 3)
                        for k in range(2):
                            p = read(act, "h", i, k)
                            for c in range(2):
                                hc = 2 * k + c
                                act.activation(hbuf[i % 3][:, hc, :], p[:, 512 * c:512 * c + 512], ACT.Gelu_apprx_tanh,
                                               bias=b1[:, e, hc:hc + 1]).then_inc(sg("gelu"), 1)
                            act.wait_ge(sg("gelu"), 4 * i + 2 * k + 2)
                            act.sem_inc(freed("h", i, k), 1)
                    p = read(act, "GT")
                    act.activation(GT, p[0:E, :], ACT.Copy).then_inc(sg("GT"), 1)
                    act.wait_ge(sg("GT"), 1)
                    act.sem_inc(freed("GT"), 1)
                    out_xT(3, 3)
                    for i in range(3):
                        act.wait_ge(sg("l_min"), i + 1)
                        if i < 2:
                            act.activation(lm[i][0:HL, :], lm[i][0:HL, :], ACT.Exp).then_inc(sg("l_exp"), 1)
                        else:
                            act.activation(lm[i][:, 0:NT * HL], lm[i][:, 0:NT * HL], ACT.Exp).then_inc(sg("l_exp"), 1)
                    p = read(act, "lv")
                    act.activation(lvT, p[0:HL, :], ACT.Copy).then_inc(sg("l_v"), 1)
                    act.wait_ge(sg("l_v"), 1)
                    act.sem_inc(freed("lv"), 1)
                    p = read(act, "loT")
                    act.activation(lOT, p[0:HL, :], ACT.Copy).then_inc(sg("l_OT"), 1)
                    act.wait_ge(sg("l_OT"), 1)
                    act.sem_inc(freed("loT"), 1)
                    for l in range(DEPTH):
                        def shifted(i, k):
                            p = read(act, "toT", i)
                            act.activation(hT[0:64, :], p[0:64, :], ACT.Copy).then_inc(sg("h_part"), 1)
                            act.activation(hT[64:128, 1:S], p[64:128, 0:S - 1], ACT.Copy).then_inc(sg("h_part"), 1)
                            act.wait_ge(sg("h_part"), 2 * k)
                            act.sem_inc(freed("toT", i), 1)
                            act.sem_inc(sg("hT"), 1)

                        shifted(4 + 4 * l, 2 * l + 1)
                        for i in range(NT + 3):
                            t = i - 2
                            k = l * NT + t
                            for w in range(2):
                                if 0 <= t < NT:
                                    act.wait_ge(sg("largest"), 2 * k + 1 + w)
                                    p = slot("fS", l, t)
                                    if k and w == 0:
                                        read(act, "fPT", (k - 1) // NT, (k - 1) % NT)
                                    for h in range(4 * w, 4 * w + 4):
                                        ins = act.activation(fP[:, h, :], p[:, 128 * h:128 * h + 128], ACT.Exp,
                                                             bias=fnm[:, h:h + 1], accum_out=fden[:, h:h + 1])
                                    ins.then_inc(freed("fS", l, t) if w else sg("exps"), 1)
                                if i < NT and w == 0:
                                    p = read(act, "fqk", l, i)
                                    if l or i:
                                        act.wait_ge(sg("sums"), l * NT + i)
                                    act.activation(SQb.rearrange("p a b -> p (a b)"), p, ACT.Square).then_inc(sg("squares"), 1)
                            t = i - 3
                            if 0 <= t < NT:
                                head_outputs(act, l, t, 1)
                            t = i - 1
                            k = l * NT + t
                            if 0 <= t < NT:
                                p = read(act, "fT", l, t).rearrange("p (h n) -> p h n", h=8)
                                if k >= 1:
                                    read(act, "fS", (k - 1) // NT, (k - 1) % NT)
                                else:
                                    act.wait_ge(sg("blocks"), 1)
                                act.activation(fkT[t % 2][:, :, 64:192], p[:, 4:8, :], ACT.Copy)
                                before = p[:, 4:8, 64:128] if t == 0 else fkT[(t - 1) % 2][:, :, 128:192]
                                act.activation(fkT[t % 2][:, :, 0:64], before, ACT.Copy)
                                for r in range(2):
                                    rr = slice(64 * r, 64 * r + 64)
                                    ins = act.activation(fqB[rr, :, :, r, :], p[rr, 0:4, :].rearrange("p c (w q) -> p w c q", w=2), ACT.Copy)
                                ins.then_inc(freed("fT", l, t), 1)
                            if i < NT:
                                k = l * NT + i
                                p = read(act, "fv", l, i)
                                if k >= VRING:
                                    read(act, "fO", (k - VRING) // NT, (k - VRING) % NT, 1)
                                    j = k - VRING + 1
                                    act.wait_ge(sg(f"v_shift{j % VRING}"), 32 * (j // VRING + 1))
                                act.activation(V[k % VRING], p, ACT.Copy).then_inc(freed("fv", l, i), 1)
                            t = i - 2
                            k = l * NT + t
                            if 0 <= t < NT:
                                p = read(act, "fPT", l, t)
                                if k:
                                    read(act, "fO", (k - 1) // NT, (k - 1) % NT, 1)
                                act.activation(fPT.rearrange("p a b -> p (a b)"), p, ACT.Copy).then_inc(freed("fPT", l, t), 1)
                        shifted(5 + 4 * l, 2 * l + 2)
                        out_xT(7 + 4 * l, 4 + l)
                        for hb in range(2):
                            for c, (c0, m) in enumerate(CH):
                                p = read(act, "fw1", l, hb, c)
                                k = (2 * l + hb) * len(CH) + c
                                if k >= 2:
                                    act.wait_ge(sg("U"), k - 1)
                                act.activation(GL[k % 2][0:m, :], p[0:m, 512:1024], ACT.Gelu,
                                               bias=fb1[0:m, l, 1, c:c + 1]).then_inc(sg("GL"), 1)

                @block.vector
                def _(dve):
                    chain = [0]

                    def link(ins):
                        chain[0] += 1
                        ins.then_inc(sg("dve_chain"), 1)
                        dve.wait_ge(sg("dve_chain"), chain[0])

                    def rsqrt(n):
                        m, y, t = st_m[:, 0:n], st_y[:, 0:n], st_t[:, 0:n]
                        link(dve.tensor_scalar(st_i[:, 0:n], m.bitcast(I32), 1, None, ALU.logical_shift_right))
                        link(dve.tensor_scalar(y.bitcast(I32), st_i[:, 0:n], -1.0, 1597463007.0, ALU.mult, ALU.add))
                        for _ in range(3):
                            link(dve.tensor_tensor(t, y, y, ALU.mult))
                            link(dve.scalar_tensor_tensor(out=t, in0=t, scalar=-0.5, in1=m, op0=ALU.mult, op1=ALU.mult))
                            link(dve.scalar_tensor_tensor(out=y, in0=t, scalar=1.5, in1=y, op0=ALU.add, op1=ALU.mult))

                    def per_token(n):
                        return st_y[:, 0:NT].unsqueeze(2).to_broadcast([128, NT, n])

                    def layer_norm(src, dst, free=None):
                        link(dve.tensor_reduce(st_a[:, 0:NT], src, AX, ALU.add))
                        link(dve.tensor_scalar(st_a[:, 0:NT], st_a[:, 0:NT], -1.0 / D, None, ALU.mult))
                        link(dve.tensor_tensor(dst, src, st_a[:, 0:NT].unsqueeze(2).to_broadcast([128, NT, D]), ALU.add))
                        if free is not None:
                            dve.sem_inc(free, 1)
                        link(dve.tensor_tensor(Q[:, :, :], dst, dst, ALU.mult))
                        link(dve.tensor_reduce(st_a[:, 0:NT], Q[:, :, :], AX, ALU.add))
                        link(dve.tensor_scalar(st_m[:, 0:NT], st_a[:, 0:NT], 1.0 / D, 1e-5, ALU.mult, ALU.add))
                        rsqrt(NT)
                        link(dve.tensor_tensor(dst, dst, per_token(D), ALU.mult))

                    def signal(name):
                        dve.sem_inc(sg(name), 1)

                    dve.wait_ge(sg("x_in"), 256)
                    for a in range(2):
                        src = (X, R)[a][:, :, :]
                        link(dve.tensor_tensor(Q[:, :, :], src, src, ALU.mult))
                        link(dve.tensor_reduce(st_a[:, 0:NT], Q[:, :, :], AX, ALU.add))
                        link(dve.tensor_scalar(st_m[:, 0:NT], st_a[:, 0:NT], 1.0 / D, 1e-6, ALU.mult, ALU.add))
                        rsqrt(NT)
                        link(dve.tensor_tensor(N[:, :, :], src, per_token(D), ALU.mult))
                        signal("src")
                        dve.wait_ge(sg("qk"), 2 * a + 2)
                        nh = H + KV
                        qv = QK.rearrange("p t (h d) -> p t h d", h=nh)
                        rv = QR.rearrange("p t (h d) -> p t h d", h=nh)
                        sw = QK.rearrange("p t (h d s) -> p t h d s", h=nh, s=2)
                        tmp = arena_rope.rearrange("p t (h d s) -> p t h d s", h=nh, s=2)
                        for t in range(NT):
                            dve.tensor_tensor(rv[:, t], qv[:, t],
                                              rope[a][:, t, 0:1, :].to_broadcast([128, nh, HD]), ALU.mult)
                            for s in range(2):
                                ins = dve.tensor_tensor(tmp[:, t, :, :, s], sw[:, t, :, :, 1 - s],
                                                  rope[a][:, t, 1:2, :].rearrange("p o (d s) -> p o d s", s=2)[:, :, :, s].to_broadcast([128, nh, HD // 2]), ALU.mult)
                        link(ins)
                        link(dve.tensor_tensor(QR, QR, arena_rope, ALU.add))
                        link(dve.tensor_tensor(arena_rope, QR, QR, ALU.mult))
                        link(dve.tensor_reduce(st_a[:, 0:160], arena_rope.rearrange("p t (h d) -> p (t h) d", h=nh), AX, ALU.add))
                        link(dve.tensor_scalar(st_m[:, :], st_a[:, :], 1.0 / HD, 1e-6, ALU.mult, ALU.add))
                        rsqrt(160)
                        QRf = QR.rearrange("p t (h d) -> p (t h) d", h=nh)
                        link(dve.tensor_tensor(QRf, QRf, st_y[:, :].unsqueeze(2).to_broadcast([128, 160, HD]), ALU.mult))
                        signal("qn")
                        kv = QR[:, :, 128:160]
                        dve.wait_ge(sg("set"), 7)
                        for s in (0, 2):
                            for g in range(KV):
                                ins = dve.tensor_copy(Kpad[:, :, g, s, g, :], kv[:, :, 8 * g:8 * g + 8])
                        link(ins)
                        for s in (1, 3):
                            for g in range(KV):
                                ins = dve.tensor_tensor(Kpad[:, :, g, s, g, :], kv[:, :, 8 * g:8 * g + 8],
                                                        Kpad[:, :, g, s - 1, g, :], ALU.subtract)
                        dve.wait_ge(sg("q_hi"), 2 * a + 2)
                        for s in (2, 3):
                            ins = dve.tensor_tensor(Qs[:, :, :, s, :], QR[:, :, 0:128].rearrange("p t (j n) -> p t j n", j=GQ),
                                                    Qs[:, :, :, s - 2, :], ALU.subtract)
                        link(ins)
                        signal("split")
                        for i in range(2):
                            p = read(dve, "kT", a, i).bitcast(F16).rearrange("p (j n) -> p j n", j=2)
                            if i == 0:
                                link(dve.memset(KT[:, :, 0:PAD], 0.0))
                            link(dve.tensor_copy(KT[:, 2 * i:2 * i + 2, PAD:PAD + S], p))
                            dve.sem_inc(freed("kT", a, i), 1)
                            signal("KT")
                        for half in range(2):
                            Av = At.rearrange("p t (g j d) -> p t g j d", g=KV, j=GQ)
                            if a == 0:
                                for g in range(KV):
                                    p = read(dve, "O", 0, half, g)
                                    if half:
                                        read(dve, "Ot", 0, 0, g // 2)
                                    pv = p.rearrange("p (T u w q) -> p T w u q", T=2, u=4, w=2)
                                    ov = OT[:, g, :].rearrange("p (T w u q) -> p T w u q", T=2, u=4, w=2)
                                    for T in range(2):
                                        ins = dve.tensor_copy(ov[:, T], pv[:, T])
                                    link(ins)
                                    dve.sem_inc(freed("O", 0, half, g), 1)
                                    signal("OT")
                                for i in range(2):
                                    p = read(dve, "Ot", 0, half, i).rearrange("p (g t j n) -> p g t j n", g=2, t=4, j=4)
                                    for gg in range(2):
                                        rd = rden[:, 0:16].rearrange("p (t j) -> p t j", t=4)
                                        link(dve.reciprocal(rd, p[:, gg, :, :, HD]))
                                        link(dve.tensor_tensor(Av[:, :, 2 * i + gg], p[:, gg, :, :, 0:HD],
                                                               rd.unsqueeze(3).to_broadcast([128, 4, 4, HD]), ALU.mult))
                                    dve.sem_inc(freed("Ot", 0, half, i), 1)
                            else:
                                p = read(dve, "O", 1, half)
                                link(dve.tensor_copy(OT.rearrange("p g n -> p (g n)")[:, 0:1024].rearrange("p (j u q) -> p u j q", j=4, u=8),
                                                     p.rearrange("p (u j q) -> p u j q", u=8, j=4)))
                                dve.sem_inc(freed("O", 1, half), 1)
                                signal("OT")
                                p = read(dve, "Ot", 1, half, 0).rearrange("p (T j g w n) -> p T j g w n", T=2, j=4, g=4, w=2)
                                for T in range(2):
                                    for w in range(2):
                                        rd = rden[:, 0:16].rearrange("p (g j) -> p g j", g=4)
                                        pv = p[:, T, :, :, w].rearrange("p j g n -> p g j n")
                                        link(dve.reciprocal(rd, pv[:, :, :, HD]))
                                        link(dve.tensor_tensor(Av[:, 2 * T + w], pv[:, :, :, 0:HD],
                                                               rd.unsqueeze(3).to_broadcast([128, 4, 4, HD]), ALU.mult))
                                dve.sem_inc(freed("Ot", 1, half, 0), 1)
                            signal("A")
                            p = read(dve, "wo", a, half).rearrange("p (t n) -> p t n", t=4)
                            base_ = (X, R)[a]
                            link(dve.tensor_tensor(R[:, 4 * half:4 * half + 4, :], base_[:, 4 * half:4 * half + 4, :], p, ALU.add))
                            dve.sem_inc(freed("wo", a, half), 1)
                    link(dve.tensor_tensor(R[:, :, :], R[:, :, :], X[:, :, :], ALU.add))
                    layer_norm(R[:, :, :], X[:, :, :])
                    signal("src")
                    p = read(dve, "gate")[:, 0:NT * E].rearrange("p (t e) -> p t e", t=NT)
                    bc = lambda v: v.unsqueeze(2).to_broadcast([128, NT, E])
                    lg, pr, c0_, c1_ = (g[:, :, :] for g in gtmp)
                    one = gone[0][:, :]
                    link(dve.tensor_tensor(lg, p, bgate[:, :].unsqueeze(1).to_broadcast([128, NT, E]), ALU.add))
                    dve.sem_inc(freed("gate"), 1)
                    link(dve.tensor_reduce(one, lg, AX, ALU.max))
                    link(dve.tensor_tensor(lg, lg, bc(one), ALU.subtract))
                    signal("g_lg")
                    dve.wait_ge(sg("g_exp"), 1)
                    link(dve.tensor_reduce(one, pr, AX, ALU.add))
                    link(dve.reciprocal(gone[1][:, :], one))
                    link(dve.tensor_tensor(pr, pr, bc(gone[1][:, :]), ALU.mult))
                    link(dve.tensor_copy(lg, pr))
                    rk = rank[:, :].unsqueeze(1).to_broadcast([128, NT, E])
                    for k in range(2):
                        link(dve.tensor_reduce(one, lg, AX, ALU.max))
                        link(dve.tensor_tensor(c0_, lg, bc(one), ALU.is_equal))
                        link(dve.tensor_tensor(c0_, c0_, rk, ALU.mult))
                        link(dve.tensor_reduce(one, c0_, AX, ALU.max))
                        link(dve.tensor_tensor(c0_, c0_, bc(one), ALU.is_equal))
                        if k == 0:
                            link(dve.tensor_copy(c1_, c0_))
                            link(dve.scalar_tensor_tensor(out=lg, in0=c0_, scalar=-2.0, in1=lg, op0=ALU.mult, op1=ALU.add))
                        else:
                            link(dve.tensor_tensor(c1_, c1_, c0_, ALU.add))
                    link(dve.tensor_tensor(pr, pr, c1_, ALU.mult))
                    link(dve.tensor_reduce(one, pr, AX, ALU.add))
                    link(dve.tensor_scalar(one, one, 1e-8, None, ALU.add))
                    link(dve.reciprocal(gone[1][:, :], one))
                    link(dve.tensor_tensor(gates[:, :, :], pr, bc(gone[1][:, :]), ALU.mult))
                    signal("gates")
                    for i in range(2 * E):
                        hb, e = divmod(i, E)
                        p = read(dve, "eo", i)
                        for t in range(4):
                            tt = 4 * hb + t
                            acc = X if e == 0 else R
                            ins = dve.scalar_tensor_tensor(out=R[:, tt, :], in0=p[:, 128 * t:128 * t + 128],
                                                           scalar=gates[:, tt, e:e + 1], in1=acc[:, tt, :],
                                                           op0=ALU.mult, op1=ALU.add)
                        link(ins)
                        dve.sem_inc(freed("eo", i), 1)
                    p = read(dve, "b2").rearrange("p (t n) -> p t n", t=NT)
                    link(dve.tensor_tensor(R[:, :, :], R[:, :, :], p, ALU.add))
                    dve.sem_inc(freed("b2"), 1)
                    layer_norm(R[:, :, :], X[:, :, :])
                    signal("src")
                    dve.memset(lone, 1.0)
                    pq = read(dve, "lq")[0:HL, :]
                    link(dve.tensor_scalar(lm[0][0:HL, :], pq, 0.0, None, ALU.min))
                    signal("l_min")
                    pk = read(dve, "lk")[0:HL, :]
                    link(dve.tensor_scalar(lm[1][0:HL, :], pk, 0.0, None, ALU.min))
                    signal("l_min")
                    pt = read(dve, "lkv").rearrange("p (t n) -> p t n", t=NT)
                    m2 = lm[2][:, 0:NT * HL].rearrange("p (t n) -> p t n", t=NT)
                    link(dve.tensor_scalar(m2, pt[:, :, 0:HL], 0.0, None, ALU.min))
                    signal("l_min")
                    dve.wait_ge(sg("l_exp"), 1)
                    link(dve.scalar_tensor_tensor(out=lqT, in0=pq, scalar=0.0, in1=lm[0][0:HL, :], op0=ALU.max, op1=ALU.add))
                    dve.sem_inc(freed("lq"), 1)
                    dve.wait_ge(sg("l_exp"), 2)
                    link(dve.scalar_tensor_tensor(out=lkT, in0=pk, scalar=0.0, in1=lm[1][0:HL, :], op0=ALU.max, op1=ALU.add))
                    dve.sem_inc(freed("lk"), 1)
                    dve.wait_ge(sg("l_exp"), 3)
                    dve.tensor_copy(lvt, pt[:, :, HL:128])
                    link(dve.scalar_tensor_tensor(out=lkt, in0=pt[:, :, 0:HL], scalar=0.0, in1=m2, op0=ALU.max, op1=ALU.add))
                    dve.sem_inc(freed("lkv"), 1)
                    signal("l_tok")
                    link(dve.tensor_tensor_scan(lz, lone, lkT, 0.0, ALU.mult, ALU.add))
                    link(dve.tensor_tensor(lqz, lqT, lz, ALU.mult))
                    p = read(dve, "lM")[0:HL, :].rearrange("p (t n) -> p t n", t=NT)
                    link(dve.tensor_copy(lM[:, 1, :], p[:, 0, :]))
                    for t in range(2, NT):
                        link(dve.tensor_tensor(lM[:, t, :], lM[:, t - 1, :], p[:, t - 1, :], ALU.add))
                    dve.sem_inc(freed("lM"), 1)
                    p = read(dve, "ls").rearrange("p (t n) -> p t n", t=NT)
                    link(dve.tensor_tensor(lA, p, tri[:, :].unsqueeze(1).to_broadcast([128, NT, 128]), ALU.mult))
                    dve.sem_inc(freed("ls"), 1)
                    signal("l_A")
                    p = read(dve, "lo").rearrange("p (t n) -> p t n", t=NT)
                    link(dve.tensor_scalar(st_a[:, 0:NT], p[:, :, HL], 1e-6, None, ALU.max))
                    link(dve.reciprocal(st_y[:, 0:NT], st_a[:, 0:NT]))
                    link(dve.tensor_tensor(lO, p[:, :, 0:HL], per_token(HL), ALU.mult))
                    dve.sem_inc(freed("lo"), 1)
                    signal("l_O")
                    p = read(dve, "lwo").rearrange("p (t n) -> p t n", t=NT)
                    link(dve.tensor_tensor(R[:, :, :], X[:, :, :], p, ALU.add))
                    dve.sem_inc(freed("lwo"), 1)
                    layer_norm(R[:, :, :], X[:, :, :])
                    signal("src")
                    link(dve.tensor_copy(R[:, :, :], X[:, :, :]))
                    for l in range(DEPTH):
                        for i in range(NT + 4):
                            def rotary(s):
                                hs = slice(NH * s, NH * s + NH)
                                x = read(dve, "fqk", l, i).rearrange("p (h n) -> p h n", h=16)[:, hs, :]
                                if k:
                                    dve.wait_ge(sg("rot"), 2 * k)
                                dve.tensor_tensor(T1[k % 2][:, hs, :], x, xpos[:, l, i, 0, s:s + 1, :].to_broadcast([128, NH, DH]), ALU.mult)
                                return dve.tensor_tensor(T2[:, hs, :].rearrange("p h (a b) -> p h a b", a=2),
                                                         x.rearrange("p h (a b) -> p h a b", a=2)[:, :, ::-1, :],
                                                         xpos[:, l, i, 1, s:s + 1, :].rearrange("p o (a b) -> p o a b", a=2).to_broadcast([128, NH, 2, 32]),
                                                         ALU.mult)

                            t = i - 2
                            if 0 <= t < NT:
                                kk = l * NT + t
                                for w in range(2):
                                    if w == 0:
                                        dve.wait_ge(sg("scores"), kk + 1)
                                    else:
                                        read(dve, "fS", l, t)
                                    p = slot("fS", l, t)[:, 512 * w:512 * w + 512].rearrange("p (h n) -> p h n", h=4)
                                    dve.tensor_reduce(fnm[:, 4 * w:4 * w + 4], p, AX, ALU.max, negate=True).then_inc(sg("largest"), 1)
                            t = i - 1
                            if 0 <= t < NT:
                                kk = l * NT + t
                                dve.wait_ge(sg("inverse"), kk + 1)
                                dve.wait_ge(sg("rot"), 2 * kk + 2)
                                v = T1[kk % 2]
                                dve.tensor_tensor(v, v, fy[:, :].unsqueeze(2).to_broadcast([128, 16, DH]), ALU.mult).then_inc(sg("unit"), 1)
                            k = l * NT + i
                            if i < NT:
                                dve.wait_ge(sg("squares"), k + 1)
                                dve.tensor_reduce(fss[:, :], SQb, AX, ALU.add).then_inc(sg("sums"), 1)
                                dve.wait_ge(sg("sums"), k + 1)
                                if k:
                                    dve.wait_ge(sg("unit"), k)
                                link(dve.tensor_scalar(fm[:, :], fss[:, :], 1e-24, None, ALU.max))
                                link(dve.tensor_scalar(fi[:, :], fm[:, :].bitcast(I32), 1, None, ALU.logical_shift_right))
                                dve.tensor_scalar(fy[:, :].bitcast(I32), fi[:, :], -1.0, 1597463007.0, ALU.mult, ALU.add).then_inc(sg("guess"), 1)
                            if i - 4 in (3, 7):
                                g = (i - 4) // 4
                                p = read(dve, "fwo", l, g).rearrange("p (t n) -> p t n", t=4)
                                link(dve.tensor_tensor(X[:, 4 * g:4 * g + 4, :], X[:, 4 * g:4 * g + 4, :], p, ALU.add))
                                dve.sem_inc(freed("fwo", l, g), 1)
                            t = i - 2
                            if 0 <= t < NT:
                                for w in range(2):
                                    if w == 0:
                                        dve.wait_ge(sg("exps"), l * NT + t + 1)
                                    else:
                                        is_free(dve, "fS", l, t)
                                    ws = slice(4 * w, 4 * w + 4)
                                    link(dve.reciprocal(frd[:, ws], fden[:, ws]))
                                    dve.tensor_tensor(fP[:, ws], fP[:, ws], frd[:, ws].unsqueeze(2).to_broadcast([128, 4, 128]),
                                                      ALU.mult).then_inc(sg("softmax"), 1)
                            if i < NT:
                                if k >= 2:
                                    read(dve, "fT", (k - 2) // NT, (k - 2) % NT)
                                rotary(0).then_inc(sg("prod"), 1)
                                rotary(1).then_inc(freed("fqk", l, i), 1)
                            t = i - 3
                            if 0 <= t < NT:
                                head_outputs(dve, l, t, 0)
                        signal("src")
                        p = read(dve, "toT", 6 + 4 * l).rearrange("p (t n) -> p t n", t=NT)
                        layer_norm(p, N[:, :, :], free=freed("toT", 6 + 4 * l))
                        signal("src")
                        signal("src")
                        for hb in range(2):
                            if l or hb:
                                read(dve, "fw2", l if hb else l - 1, 1 - hb)
                            link(dve.memset(U[64:96, 2, :], 1.0))
                            for c, (c0, m) in enumerate(CH):
                                k = (2 * l + hb) * len(CH) + c
                                p = read(dve, "fw1", l, hb, c)
                                dve.wait_ge(sg("GL"), k + 1)
                                link(dve.scalar_tensor_tensor(out=U[0:m, c, :], in0=p[0:m, 0:512], scalar=fb1[0:m, l, 0, c:c + 1],
                                                              in1=GL[k % 2][0:m, :], op0=ALU.add, op1=ALU.mult))
                                dve.sem_inc(freed("fw1", l, hb, c), 1)
                                signal("U")
                            p = read(dve, "fw2", l, hb).rearrange("p (t n) -> p t n", t=4)
                            link(dve.tensor_tensor(X[:, 4 * hb:4 * hb + 4, :], X[:, 4 * hb:4 * hb + 4, :], p, ALU.add))
                            dve.sem_inc(freed("fw2", l, hb), 1)
                        if l < DEPTH - 1:
                            signal("src")
                    link(dve.tensor_tensor(R[:, :, :], R[:, :, :], X[:, :, :], ALU.add))
                    layer_norm(R[:, :, :], N[:, :, :])
                    signal("final")

                @block.gpsimd
                def _(pool):
                    pool.memset(Kpad.rearrange("p a b c d e -> p (a b c d e)"), 0.0).then_inc(sg("set"), 1)
                    pool.memset(Vaug.rearrange("p a b c -> p (a b c)"), 0.0).then_inc(sg("set"), 1)
                    pool.memset(Vwin.rearrange("p a b c d -> p (a b c d)"), 0.0).then_inc(sg("set"), 1)
                    pool.wait_ge(sg("set"), 3)
                    pool.memset(Vaug[:, :, :, HD:HD + 1], 1.0).then_inc(sg("set"), 1)
                    pool.wait_ge(sg("set"), 4)
                    pool.memset(Vwin[0:64, :, :, 0, HD:HD + 1], 1.0).then_inc(sg("set"), 1)
                    pool.wait_ge(sg("set"), 5)
                    pool.memset(Vwin[64:128, :, :, 1, HD:HD + 1], 1.0).then_inc(sg("set"), 1)
                    pool.wait_ge(sg("set"), 6)
                    pool.memset(Vwin[0:WIN, 0:1, :, 0, HD:HD + 1], 0.0).then_inc(sg("set"), 1)
                    steps = [0]

                    def link(ins):
                        steps[0] += 1
                        ins.then_inc(sg("pool_chain"), 1)
                        pool.wait_ge(sg("pool_chain"), steps[0])

                    pool.wait_ge(sg("src"), 5)
                    pool.memset(fqB.rearrange("p a b c d -> p (a b c d)"), 0.0).then_inc(sg("blocks"), 1)
                    for k in range(DEPTH * NT):
                        pool.wait_ge(sg("guess"), k + 1)
                        for j in range(3):
                            link(pool.tensor_tensor(ft[:, :], fy[:, :], fy[:, :], ALU.mult))
                            link(pool.tensor_tensor(ft[:, :], ft[:, :], fm[:, :], ALU.mult))
                            link(pool.tensor_scalar(ft[:, :], ft[:, :], -0.5, 1.5, ALU.mult, ALU.add))
                            ins = pool.tensor_tensor(fy[:, :], fy[:, :], ft[:, :], ALU.mult)
                            if j < 2:
                                link(ins)
                        ins.then_inc(sg("inverse"), 1)
                        for s in range(2):
                            if s == 0:
                                pool.wait_ge(sg("prod"), k + 1)
                            else:
                                is_free(pool, "fqk", k // NT, k % NT)
                            hs = slice(NH * s, NH * s + NH)
                            pool.tensor_tensor(T1[k % 2][:, hs, :], T1[k % 2][:, hs, :], T2[:, hs, :], ALU.add).then_inc(sg("rot"), 1)
            with nc.Block() as block:
                @block.sync
                def _(sp):
                    for s in sems.values():
                        sp.sem_clear(s)


_INS = ['L0_attn_hidden', 'L0_attn_norm1_w', 'L0_attn_norm2_w', 'L0_attn_g_wq', 'L0_attn_g_kv_down', 'L0_attn_g_k_up',
        'L0_attn_g_v_up', 'L0_attn_g_wo', 'L0_attn_l_wq', 'L0_attn_l_wk', 'L0_attn_l_wv', 'L0_attn_l_wo', 'L0_ffn_Wg',
        'L0_ffn_bg', 'L0_ffn_W1', 'L0_ffn_b1', 'L0_ffn_W2', 'L0_ffn_b2', 'L1_attn_W_q', 'L1_attn_W_k', 'L1_attn_W_v',
        'L1_attn_W_o', 'L1_ffn_wqkv', 'L1_ffn_q_scale', 'L1_ffn_k_scale', 'L1_ffn_wo', 'L1_ffn_ln_g', 'L1_ffn_ln_b',
        'L1_ffn_w1', 'L1_ffn_b1', 'L1_ffn_w2', 'L1_ffn_b2']


def kernel(**inputs):
    import concourse.bacc as _bacc
    from concourse.bass_utils import run_bass_kernel_spmd as _run

    nc = _bacc.Bacc("TRN2", target_bir_lowering=False, num_devices=1)
    arrays, handles = {}, {}
    given = {n: np.ascontiguousarray(inputs[n]) for n in _INS}
    for n in ("L0_attn_g_wq", "L0_attn_l_wq"):
        given[n] = np.ascontiguousarray(given[n].reshape(D, KV, GQ, HD).transpose(0, 2, 1, 3).reshape(D, H * HD))
    given["L0_ffn_b1"] = np.ascontiguousarray(given["L0_ffn_b1"].reshape(E, HC, 128).transpose(2, 0, 1))
    given.update(constant_tables())
    given["c_rank"] = np.arange(E, 0, -1).astype(np.float32)
    for name, a in given.items():
        arrays[f"in_{name}"] = a
        handles[name] = nc.dram_tensor(f"in_{name}", a.shape, mybir.dt.from_np(a.dtype), kind="ExternalInput").ap()
    handles["out"] = nc.dram_tensor("out_y", (B, S, D), F32, kind="ExternalOutput").ap()
    build(nc, handles)
    r = _run(nc, [arrays], core_ids=[0])
    return r.results[0]["out_y"]
```

```python
import numpy as np
import concourse.bass as bass
from concourse import mybir
from concourse.alu_op_type import AluOpType as ALU
from contextlib import ExitStack

ACT = mybir.ActivationFunctionType
AX = mybir.AxisListType.X
F32, F16, BF16, I32 = mybir.dt.float32, mybir.dt.float16, mybir.dt.bfloat16, mybir.dt.int32

B, S, D = 4, 1024, 128
NT = S // 128
H, KV, HD = 16, 4, 8
GQ = H // KV
LAT = 32
WIN = 32
PAD = WIN
E, HF = 8, 512
HC = HF // 128
HL = 64
NH, DH, W2 = 8, 64, 64
INNER = NH * DH
DEPTH = 2
HID = int(D * 4 * 2 / 3)
CH = [(c * 128, min(128, HID - c * 128)) for c in range((HID + 127) // 128)]
HALF_STEPS = {NT: "hF", NT + 1: "hB", NT + 2: "nF"}
VRING = 5
PRING = 6
INV_SQRT_HD = 1.0 / float(np.sqrt(np.float32(HD)))


def constant_tables():
    f = np.float32
    t = {}
    t["c_ident"] = np.eye(128, dtype=f)
    k, q = np.arange(128)[None, :], np.arange(128)[:, None]
    t["c_causal"] = np.where(k > q, -30000.0, 0.0).astype(np.float16)
    loc = np.zeros((128, 128), np.float16)
    kk = np.arange(64)[None, :]
    qq = np.arange(WIN)[:, None]
    ok = (kk <= qq + WIN) & (qq + WIN - kk < WIN)
    loc[:WIN] = np.tile(np.where(ok, 0.0, -30000.0), (1, 2))
    t["c_local"] = loc
    t["c_tri"] = (np.arange(128)[:, None] <= np.arange(128)[None, :]).astype(f)
    jl = np.arange(128)[:, None]
    il = np.arange(64)[None, :]
    ok = (il <= jl) & (jl <= il + W2)
    m = np.tile(np.where(ok, 0.0, -1e30), (1, 2)).astype(f)
    first = m.copy()
    first[:64] = -1e30
    t["c_win"] = np.stack([first, m], 1)
    for name, base in (("g", 1000000.0), ("l", 10000.0)):
        inv = (f(1.0) / (f(base) ** (np.arange(0, HD, 2, dtype=f) / f(HD)))).astype(f)
        fr = (np.arange(S, dtype=f)[:, None] * inv[None, :]).astype(f)
        c, s = np.cos(fr), np.sin(fr)
        tab = np.stack([np.repeat(c, 2, axis=1), np.stack([-s, s], -1).reshape(S, HD)], 1)
        t["c_rope_" + name] = np.ascontiguousarray(tab.reshape(NT, 128, 2, HD).transpose(1, 0, 2, 3)).astype(f)
    half = np.arange(0, DH, 2, dtype=f)
    inv = (f(1.0) / (f(10000.0) ** (half / f(DH)))).astype(f)
    pos = np.arange(S, dtype=f)
    fr = (pos[:, None] * inv[None, :]).astype(f)
    base = ((half + f(0.4 * DH)) / f(1.4 * DH)).astype(f)
    power = ((pos - f(S // 2)) / f(W2 // 2)).astype(f)
    sc = (base[None, :] ** power[:, None]).astype(f)
    c, s = np.cos(fr), np.sin(fr)
    cc, ss, scc = (np.concatenate([a, a], 1) for a in (c, s, sc))
    sg = np.concatenate([-ss[:, :DH // 2], ss[:, DH // 2:]], 1)
    tab = np.stack([np.stack([8 * cc * scc, cc / scc], 1), np.stack([8 * sg * scc, sg / scc], 1)], 1)
    t["c_xpos"] = np.ascontiguousarray(tab.reshape(NT, 128, 2, 2, DH).transpose(1, 0, 2, 3, 4)).astype(f)
    return t


class Tickets:

    def __init__(self):
        self.at, self.used, self.next = {}, {}, {"D": 0, "H": 0}
        self.size = {"D": 3, "H": 2}

    def add(self, kind, *key):
        k = self.next[kind] % self.size[kind]
        self.next[kind] += 1
        n = self.used.get((kind, k), 0)
        self.used[(kind, k)] = n + 1
        assert key not in self.at, key
        self.at[key] = (kind, k, n)


def attention_units(a, half):
    if a == 0:
        return [(g, kc, jp) for g in range(KV) for kc in range(4 * half + 4) for jp in range(2)]
    return [(g,) for g in range(KV)]


def plan():
    t = Tickets()
    for a in range(2):
        t.add("D", "toT", a)
        for i in range(2):
            t.add("D", "qkv", a, i)
        if a == 1:
            t.add("D", "vwin")
        for i in range(2):
            t.add("D", "qT", a, i)
        for i in range(2):
            t.add("D", "kT", a, i)
        for half in range(2):
            units = attention_units(a, half)
            if a == 0:
                for u in units:
                    t.add("D", "S", a, half, *u)
                for g in range(KV):
                    t.add("H", "O", a, half, g)
                for i in range(2):
                    t.add("D", "Ot", a, half, i)
            else:
                for u in units:
                    t.add("D", "S", a, half, *u)
                t.add("D", "O", a, half)
                t.add("D", "Ot", a, half, 0)
            t.add("H", "At", a, half)
            t.add("H", "wo", a, half)
    t.add("D", "toT", 2)
    t.add("H", "gate")
    for i in range(2 * E + 1):
        if i < 2 * E:
            t.add("D", "h", i, 0)
            t.add("D", "h", i, 1)
        if i > 0:
            t.add("H", "eo", i - 1)
    t.add("D", "GT")
    t.add("D", "b2")
    t.add("D", "toT", 3)
    for n in ("lq", "lk", "lkv", "lv"):
        t.add("D", n)
    t.add("H", "lM")
    for n in ("ls", "lo", "loT", "lwo"):
        t.add("D", n)
    for h in range(2):
        t.add("D", "xF", 0, h)
    for l in range(DEPTH):
        for i in range(NT + 4):
            if 0 <= i - 2 < NT:
                t.add("D", "fS", l, i - 2)
            if i < NT:
                t.add("D", "fqk", l, i)
            if i - 4 in (3, 7):
                t.add("H", "fwo", l, (i - 4) // 4)
            if 0 <= i - 3 < NT:
                t.add("H", "fO", l, i - 3, 0)
                t.add("H", "fO", l, i - 3, 1)
            if 0 <= i - 1 < NT:
                t.add("D", "fT", l, i - 1)
            if i < NT:
                t.add("H", "fv", l, i)
            if 0 <= i - 2 < NT:
                t.add("D", "fPT", l, i - 2)
            if i in HALF_STEPS:
                t.add("D", HALF_STEPS[i], l, 0)
        for c in range(len(CH)):
            t.add("D", "fw1", l, 0, c)
            t.add("D", ("hF", "hB", "nF")[c], l, 1)
        t.add("H", "fw2", l, 0)
        for c in range(len(CH)):
            t.add("D", "fw1", l, 1, c)
        if l < DEPTH - 1:
            t.add("D", "xF", l + 1, 0)
        t.add("H", "fw2", l, 1)
        if l < DEPTH - 1:
            t.add("D", "xF", l + 1, 1)
    return t


def build(nc, A):
    tk = plan()
    ctx = ExitStack()
    with ctx:
        def sb(name, shape, dt=F32):
            return ctx.enter_context(nc.sbuf_tensor(name, shape, dt))

        ident = sb("ident", [128, 128])
        ident16 = sb("ident16", [128, 128], F16)
        causal = sb("causal", [128, 128], F16)
        local = sb("local", [128, 128], F16)
        identb = sb("identb", [128, 128], BF16)
        win = sb("win", [128, 2, 128], BF16)
        tri = sb("tri", [128, 128])
        ones = sb("ones", [128, 1])
        rope = [sb(f"rope{a}", [128, NT, 2, HD]) for a in range(2)]
        w_att = [sb("w_global", [128, 192]), sb("w_local", [128, 192])]
        w_ao = [sb("wo_global", [128, 128]), sb("wo_local", [128, 128])]
        wgate = sb("wgate", [128, E])
        bgate = sb("bgate", [128, E])
        rank = sb("rank", [128, E])
        W1 = sb("W1", [128, E, HF])
        b1 = sb("b1", [128, E, HC])
        W2m = sb("W2m", [128, E, HC, 128])
        b2m = sb("b2m", [E, 128])
        lw = sb("lw", [128, 3, HL])
        lwo = sb("lwo", [HL, 128])
        wqkv = sb("wqkv", [128, DEPTH, 3 * INNER])
        wo = sb("wo", [128, DEPTH, 4, 128])
        w1 = sb("w1", [128, DEPTH, 2 * HID])
        fb1 = sb("fb1", [128, DEPTH, 2, len(CH)])
        w2 = sb("w2", [128, DEPTH, len(CH), 128])
        xpos = sb("xpos", [128, DEPTH, NT, 2, 2, DH])

        X = sb("X", [128, NT, 128])
        R = sb("R", [128, NT, 128])
        N = sb("N", [128, NT, 128])
        Q = sb("Q", [128, NT, 128])
        xT = sb("xT", [128, PAD + S])
        hT = sb("hT", [128, S])
        st_a = sb("st_a", [128, 160])
        st_m = sb("st_m", [128, 160])
        st_i = sb("st_i", [128, 160], I32)
        st_y = sb("st_y", [128, 160])
        st_t = sb("st_t", [128, 160])
        rden = sb("rden", [128, 64])
        gates = sb("gates", [128, NT, E])
        gtmp = [sb(f"gtmp{i}", [128, NT, E]) for i in range(4)]
        gone = [sb(f"gone{i}", [128, NT]) for i in range(3)]

        arena_bytes = 97 * 1024
        arena = sb("arena", [128, arena_bytes // 4])
        cursor = [0]

        def carve(shape, dt=F32):
            n = int(np.prod(shape[1:]))
            size = {F32: 4, F16: 2}[dt]
            words = (n * size + 31) // 32 * 8
            v = arena[0:shape[0], cursor[0]:cursor[0] + words]
            if dt is F16:
                v = v.bitcast(F16)
            v = v[:, 0:n]
            cursor[0] += words
            assert cursor[0] * 4 <= arena_bytes, cursor[0] * 4
            names = "abcde"[:len(shape) - 1]
            if len(shape) > 2:
                v = v.rearrange(f"p ({' '.join(names)}) -> p {' '.join(names)}", **{c: s for c, s in zip(names[1:], shape[2:])})
            return v

        cursor[0] = 0
        QK = carve([128, NT, 160])
        QR = carve([128, NT, 160])
        Qs = carve([128, NT, GQ, 4, 32], F16)
        arena_rope = carve([128, NT, 160])
        QT = carve([128, GQ, S], F16)
        KT = carve([128, KV, PAD + S], F16)
        P = [carve([128, 1024]) for _ in range(PRING)]
        OT = carve([128, KV, 512])
        At = carve([128, NT // 2, 128])
        AT = carve([128, 512])
        Kpad = carve([128, NT, KV, 4, KV, HD], F16)
        Vaug = carve([128, NT, KV, 32])
        Vwin = carve([128, 16, KV, 2, 16])

        cursor[0] = 0
        hbuf = [carve([128, HC, 512]) for _ in range(3)]
        GT = carve([E, S])

        cursor[0] = 0
        lqT, lkT, lvT, lz, lqz = (carve([HL, S]) for _ in range(5))
        lm = [carve([128, S]) for _ in range(3)]
        lone = carve([HL, S])
        lkt = carve([128, NT, HL])
        lvt = carve([128, NT, HL])
        lM = carve([HL, NT, HL])
        lA = carve([128, NT, 128])
        lO = carve([128, NT, HL])
        lOT = carve([HL, S])

        cursor[0] = 0
        SQb = carve([128, 16, DH])
        T1 = [carve([128, 16, DH]) for _ in range(2)]
        T2 = carve([128, 16, DH])
        fqB = carve([128, 2, 4, 2, 64])
        fkT = [carve([128, 4, 192]) for _ in range(2)]
        V = [carve([128, INNER]) for _ in range(VRING)]
        Vsh = [carve([128, INNER]) for _ in range(VRING)]
        fP = carve([128, 8, 128])
        fPT = carve([128, 8, 128])
        fOT = carve([128, 4, 512])
        U = carve([128, 3, 512])
        GL = [carve([128, 512]) for i in range(2)]

        fss = sb("fss", [128, 16])
        fm = sb("fm", [128, 16])
        fi = sb("fi", [128, 16], I32)
        fy = sb("fy", [128, 16])
        ft = sb("ft", [128, 16])
        fnm = sb("fnm", [128, 8])
        fden = sb("fden", [128, 8])
        frd = sb("frd", [128, 8])

        PD = [ctx.enter_context(nc.psum_tensor(f"PD{i}", [128, 1024], F32)) for i in range(3)]
        PH = [ctx.enter_context(nc.psum_tensor(f"PH{i}", [128, 512], F32)) for i in range(2)]

        sems = {}

        def sg(name):
            if name not in sems:
                sems[name] = ctx.enter_context(nc.semaphore("s_" + name))
            return sems[name]

        def slot(*key):
            kind, k, n = tk.at[key]
            return (PD if kind == "D" else PH)[k]

        def fill(pe, *key):
            kind, k, n = tk.at[key]
            if n:
                pe.wait_ge(sg(f"free_{kind}{k}"), n)
            return (PD if kind == "D" else PH)[k][:, :]

        def is_free(eng, *key):
            kind, k, n = tk.at[key]
            eng.wait_ge(sg(f"free_{kind}{k}"), n + 1)

        def filled(*key):
            kind, k, n = tk.at[key]
            return sg(f"full_{kind}{k}")

        def read(eng, *key):
            kind, k, n = tk.at[key]
            eng.wait_ge(sg(f"full_{kind}{k}"), n + 1)
            return (PD if kind == "D" else PH)[k][:, :]

        def freed(*key):
            kind, k, n = tk.at[key]
            return sg(f"free_{kind}{k}")

        def spread(ap):
            return ap.rearrange("p (T u w q) -> p T w u q", T=4, u=4, w=2)

        raw = {}
        cursor[0] = 0
        for n, shape in (("g_wq", [128, 128]), ("g_kv_down", [128, LAT]), ("l_wq", [128, 128]), ("l_wk", [128, 32]),
                         ("l_wv", [128, 32]), ("n1", [128, 1]), ("n2", [128, 1]), ("up", [LAT, 64]), ("downT", [LAT, 128]),
                         ("lg", [128, DEPTH]), ("lb", [128, DEPTH]), ("b1c", [128, DEPTH, 2, len(CH)]),
                         ("w1", [128, DEPTH, 2 * HID]), ("qs", [128, DEPTH, 2, DH]), ("xp", [128, NT, 2, 2, DH]),
                         ("win", [128, 2, 128]), ("identf", [128, 128])):
            raw[n] = carve(shape)

        loads = []

        def ld(dst, src):
            loads.append((dst, src))

        ld(ident[:, :], A["c_ident"])
        ld(causal[:, :], A["c_causal"])
        ld(local[:, :], A["c_local"])
        ld(raw["win"], A["c_win"])
        ld(tri[:, :], A["c_tri"])
        ld(rope[0][:, :, :, :], A["c_rope_g"])
        ld(rope[1][:, :, :, :], A["c_rope_l"])
        ld(raw["xp"], A["c_xpos"])
        ld(raw["g_wq"], A["L0_attn_g_wq"])
        ld(raw["g_kv_down"], A["L0_attn_g_kv_down"])
        ld(raw["up"][:, 0:32], A["L0_attn_g_k_up"])
        ld(raw["up"][:, 32:64], A["L0_attn_g_v_up"])
        ld(raw["l_wq"], A["L0_attn_l_wq"])
        ld(raw["l_wk"], A["L0_attn_l_wk"])
        ld(raw["l_wv"], A["L0_attn_l_wv"])
        ld(raw["n1"], A["L0_attn_norm1_w"].rearrange("(p a) -> p a", a=1))
        ld(raw["n2"], A["L0_attn_norm2_w"].rearrange("(p a) -> p a", a=1))
        ld(w_ao[0][:, :], A["L0_attn_g_wo"])
        ld(w_ao[1][:, :], A["L0_attn_l_wo"])
        ld(wgate[:, :], A["L0_ffn_Wg"])
        ld(bgate[:, :], A["L0_ffn_bg"].partition_broadcast(128))
        ld(rank[:, :], A["c_rank"].partition_broadcast(128))
        ld(W1[:, :, :], A["L0_ffn_W1"].rearrange("e p h -> p e h"))
        ld(W2m[:, :, :, :].rearrange("p e c f -> p (e c) f"),
           A["L0_ffn_W2"].rearrange("e (c p) f -> p (e c) f", p=128))
        ld(b1[:, :, :], A["L0_ffn_b1"])
        ld(b2m[:, :], A["L0_ffn_b2"])
        for i, n in enumerate(("L1_attn_W_q", "L1_attn_W_k", "L1_attn_W_v")):
            ld(lw[:, i, :], A[n])
        ld(lwo[:, :], A["L1_attn_W_o"])
        ld(wqkv[:, :, :], A["L1_ffn_wqkv"].rearrange("l p n -> p l n"))
        ld(wo[:, :, :, :].rearrange("p l c f -> p (l c) f"), A["L1_ffn_wo"].rearrange("l (c p) f -> p (l c) f", p=128))
        ld(raw["w1"], A["L1_ffn_w1"].rearrange("l p n -> p l n"))
        for c, (c0, m) in enumerate(CH):
            ld(w2[0:m, :, c, :], A["L1_ffn_w2"][:, c0:c0 + m, :].rearrange("l p f -> p l f"))
        ld(w2[CH[-1][1]:CH[-1][1] + 1, :, len(CH) - 1, :], A["L1_ffn_b2"].rearrange("(o l) f -> o l f", o=1))
        ld(raw["b1c"], A["L1_ffn_b1"])
        ld(raw["lg"], A["L1_ffn_ln_g"])
        ld(raw["lb"], A["L1_ffn_ln_b"])
        ld(raw["qs"][:, :, 0, :], A["L1_ffn_q_scale"].partition_broadcast(128))
        ld(raw["qs"][:, :, 1, :], A["L1_ffn_k_scale"].partition_broadcast(128))

        with nc.Block() as block:
            @block.sync
            def _(sp):
                for dst, src in loads:
                    sp.dma_start(dst, src).then_inc(sg("weights"), 16)

            @block.gpsimd
            def _(pool):
                pool.memset(xT[:, 0:PAD], 0.0)
                pool.memset(hT[:, :], 0.0)
                pool.memset(ones[:, :], 1.0)

            @block.vector
            def _(dve):
                dve.wait_ge(sg("weights"), 16 * len(loads))
                dve.tensor_copy(ident16[:, :], ident[:, :])
                dve.tensor_copy(identb[:, :], ident[:, :])
                dve.tensor_copy(win[:, :, :], raw["win"])
                dve.tensor_scalar(w_att[0][:, 0:128], raw["g_wq"], raw["n1"][:, 0:1], None, ALU.mult)
                dve.tensor_scalar(w_att[1][:, 0:128], raw["l_wq"], raw["n2"][:, 0:1], None, ALU.mult)
                dve.tensor_scalar(w_att[1][:, 128:160], raw["l_wk"], raw["n2"][:, 0:1], None, ALU.mult)
                dve.tensor_scalar(w_att[1][:, 160:192], raw["l_wv"], raw["n2"][:, 0:1], None, ALU.mult)
                for l in range(DEPTH):
                    dve.tensor_scalar(w1[:, l, :], raw["w1"][:, l, :], raw["lg"][:, l:l + 1], None, ALU.mult)
                    for i in range(2):
                        qs = raw["qs"][:, l, i:i + 1, :]
                        dve.tensor_tensor(xpos[:, l, :, 0, i, :], raw["xp"][:, :, 0, i, :],
                                          qs.to_broadcast([128, NT, DH]), ALU.mult)
                        for hh in range(2):
                            a, b = 32 * hh, 32 * (1 - hh)
                            dve.tensor_tensor(xpos[:, l, :, 1, i, a:a + 32], raw["xp"][:, :, 1, i, a:a + 32],
                                              qs[:, :, b:b + 32].to_broadcast([128, NT, 32]), ALU.mult)
                dve.wait_ge(sg("w_down"), 1)
                dve.tensor_copy(raw["downT"], PH[0][0:LAT, 0:128]).then_inc(sg("w_downT"), 1)
                dve.wait_ge(sg("w_kv"), 1)
                dve.tensor_scalar(w_att[0][:, 128:192], PD[0][:, 0:64], raw["n1"][:, 0:1], None, ALU.mult)
                for l in range(DEPTH):
                    for i in range(2):
                        for c, (c0, m) in enumerate(CH):
                            k = (l * 2 + i) * len(CH) + c
                            dve.tensor_tensor(fb1[0:m, l, i, c:c + 1], PD[1][0:m, k:k + 1],
                                              raw["b1c"][0:m, l, i, c:c + 1], ALU.add)

            @block.tensor
            def _(pe):
                pe.wait_ge(sg("weights"), 16 * len(loads))
                pe.transpose(PH[0][0:LAT, 0:128], raw["g_kv_down"], ident[:, :]).then_inc(sg("w_down"), 1)
                for l in range(DEPTH):
                    for i in range(2):
                        for c, (c0, m) in enumerate(CH):
                            k = (l * 2 + i) * len(CH) + c
                            pe.matmul(PD[1][0:m, k:k + 1], raw["w1"][:, l, i * HID + c0:i * HID + c0 + m],
                                      raw["lb"][:, l:l + 1], start=True, stop=True)
                pe.wait_ge(sg("w_downT"), 1)
                pe.matmul(PD[0][:, 0:64], raw["downT"], raw["up"], start=True, stop=True).then_inc(sg("w_kv"), 1)

        x_in, x_out = A["L0_attn_hidden"], A["out"]
        def batch(x, i):
            return x[i].rearrange("b (T u w q) d -> (b u) q T w d", T=4, u=4, w=2)

        Xv = X[:, :, :].rearrange("p (T w) d -> p T w d", w=2)
        Nv = N[:, :, :].rearrange("p (T w) d -> p T w d", w=2)

        def load_x(sp, src, h):
            for u in range(4):
                for T in (2 * h, 2 * h + 1):
                    sp.dma_start(Xv[32 * u:32 * u + 32, T], src[u, :, T]).then_inc(sg("x_in"), 16)

        with nc.Block() as block:
            @block.sync
            def _(sp):
                for h in range(2):
                    load_x(sp, batch(x_in, slice(0, 1)), h)

        with nc.Fori(0, B) as b:
            with nc.Block() as block:
                @block.sync
                def _(sp):
                    sp.wait_ge(sg("src"), 1)
                    sp.sem_clear(sg("x_in"))
                    for l in range(DEPTH):
                        for t in range(NT):
                            i = l * NT + t
                            is_free(sp, "fv", l, t)
                            if i >= VRING:
                                read(sp, "fO", (i - VRING) // NT, (i - VRING) % NT, 0)
                            before = V[(i - 1) % VRING][64:128, :] if t > 0 else V[i % VRING][0:64, :]
                            sp.dma_start(Vsh[i % VRING][0:64, :], before).then_inc(sg(f"v_shift{i % VRING}"), 16)
                            sp.dma_start(Vsh[i % VRING][64:128, :], V[i % VRING][0:64, :]).then_inc(sg(f"v_shift{i % VRING}"), 16)
                    for h in range(2):
                        sp.wait_ge(sg("x_read"), h + 1)
                        load_x(sp, batch(x_in, bass.ds(b + 1, 1)), h)
                        sp.wait_ge(sg("final"), h + 1)
                        dst = batch(x_out, bass.ds(b, 1))
                        for u in range(4):
                            for T in (2 * h, 2 * h + 1):
                                sp.dma_start(dst[u, :, T], Nv[32 * u:32 * u + 32, T]).then_inc(sg("x_out"), 16)
                    sp.wait_ge(sg("x_out"), 256)

                @block.tensor
                def _(pe):
                    def by_tiles(p, t):
                        v = p.rearrange("p (T w u q) -> p T u w q", T=4, w=2, u=4)
                        return v[:, t // 2, 2 * (t % 2):2 * (t % 2) + 2]

                    def to_t(i, src, place):
                        pe.wait_ge(sg("src"), i + 1)
                        p = fill(pe, "toT", i)
                        for t in range(NT):
                            ins = pe.transpose(place(p, t), src[:, t, :], ident[:, :])
                        ins.then_inc(filled("toT", i), 1)

                    def in_order(p, t):
                        return spread(p)[:, t // 2, t % 2]

                    def as_is(p, t):
                        return p[:, 128 * t:128 * t + 128]

                    nP = 0
                    for a in range(2):
                        to_t(a, N, in_order)
                        is_free(pe, "toT", a)
                        nq = 192 if a == 0 else 160
                        for i in range(2):
                            p = fill(pe, "qkv", a, i).rearrange("p (t n) -> p t n", t=4)
                            for t in range(4):
                                c = PAD + 128 * (4 * i + t)
                                ins = pe.matmul(p[:, t, 0:nq], xT[:, c:c + 128], w_att[a][:, 0:nq], start=True, stop=True)
                            ins.then_inc(filled("qkv", a, i), 1)
                        if a == 1:
                            p = fill(pe, "vwin").rearrange("p (u n) -> p u n", u=16)
                            for u in range(16):
                                for w in range(2):
                                    c = 64 * u + 32 * w
                                    ins = pe.matmul(p[64 * w:64 * w + 64, u, 0:32], xT[:, c:c + 64], w_att[1][:, 160:192],
                                                    start=True, stop=True)
                            ins.then_inc(filled("vwin"), 1)
                        pe.wait_ge(sg("split"), a + 1)
                        for i in range(2):
                            p = fill(pe, "qT", a, i).bitcast(F16).rearrange("p (j n) -> p j n", j=2)
                            for j in range(2):
                                for t in range(NT):
                                    src = Qs[:, t, 2 * i + j].rearrange("p s n -> p (s n)")
                                    ins = pe.transpose(p[:, j, 128 * t:128 * t + 128], src, ident16[:, :])
                            ins.then_inc(filled("qT", a, i), 1)
                        for i in range(2):
                            p = fill(pe, "kT", a, i).bitcast(F16).rearrange("p (j n) -> p j n", j=2)
                            for j in range(2):
                                for t in range(NT):
                                    src = Kpad[:, t, 2 * i + j].rearrange("p s g d -> p (s g d)")
                                    ins = pe.transpose(p[:, j, 128 * t:128 * t + 128], src, ident16[:, :])
                            ins.then_inc(filled("kT", a, i), 1)
                        for i in range(2):
                            is_free(pe, "qT", a, i)
                            is_free(pe, "kT", a, i)
                        if a == 1:
                            is_free(pe, "vwin")
                        for half in range(2):
                            if a == 0:
                                units = attention_units(0, half)
                                ready = []

                                def values(g, kc, first):
                                    kcs = 4 * half + 4
                                    n = min(512, 512 - 128 * (kc - 4 * half))
                                    o = slot("O", 0, half, g)
                                    if kc == 0:
                                        fill(pe, "O", 0, half, g)
                                    for jp in range(2):
                                        is_free(pe, "S", 0, half, g, kc, jp)
                                    for j in range(4):
                                        pb = P[(first + j // 2) % PRING].rearrange("p (j n) -> p j n", j=2)
                                        ins = pe.matmul(o[32 * j:32 * j + 32, 512 - n:512], Vaug[:, kc, g, :],
                                                        pb[:, j % 2, 0:n], start=(kc == 0), stop=(kc == kcs - 1),
                                                        skip_group_check=True)
                                        if j % 2 and not (j == 3 and kc == kcs - 1):
                                            ins.then_inc(sg("pv"), 1)
                                    if kc == kcs - 1:
                                        ins.then_inc(filled("O", 0, half, g), 1)

                                lag = None
                                for (g, kc, jp) in units:
                                    if jp == 0:
                                        first = nP
                                    n = min(512, 512 - 128 * (kc - 4 * half))
                                    p = fill(pe, "S", 0, half, g, kc, jp).rearrange("p (j n) -> p j n", j=2)
                                    q0 = 512 * half + 512 - n
                                    for j in range(2):
                                        diag = kc >= 4 * half
                                        c = PAD + 128 * kc
                                        if diag:
                                            pe.matmul(p[:, j, 0:128], causal[:, :], ident16[:, :],
                                                      start=True, stop=False, skip_group_check=True)
                                        ins = pe.matmul(p[:, j, 0:n], KT[:, g, c:c + 128], QT[:, 2 * jp + j, q0:q0 + n],
                                                        start=not diag, stop=True, skip_group_check=True)
                                    ins.then_inc(filled("S", 0, half, g, kc, jp), 1)
                                    nP += 1
                                    if jp == 1:
                                        if lag is not None:
                                            values(*lag)
                                        lag = (g, kc, first)
                                values(*lag)
                                for i in range(2):
                                    p = fill(pe, "Ot", 0, half, i).rearrange("p (g t n) -> p g t n", g=2, t=4)
                                    for gg in range(2):
                                        g = 2 * i + gg
                                        pe.wait_ge(sg("OT"), 4 * half + g + 1)
                                        for t in range(4):
                                            ins = pe.transpose(p[:, gg, t, :], OT[:, g, 128 * t:128 * t + 128], ident[:, :])
                                    ins.then_inc(filled("Ot", 0, half, i), 1)
                            else:
                                first = nP
                                for g in range(KV):
                                    p = fill(pe, "S", 1, half, g)
                                    for k in range(2):
                                        pe.matmul(p[:, 512 * k:512 * k + 512].rearrange("p (a b) -> p a b", b=32), local[:, :],
                                                  ident16[:, 0:32].unsqueeze(1).to_broadcast([128, 16, 32]),
                                                  start=True, stop=False, skip_group_check=True)
                                    for u8 in range(8):
                                        for w in range(2):
                                            t0 = 64 * (8 * half + u8) + 32 * w
                                            o = p[64 * w:64 * w + 64, 128 * u8:128 * u8 + 128].rearrange("p (j q) -> p j q", j=4)
                                            ins = pe.matmul(o, KT[:, g, t0:t0 + 64], QT[:, :, t0:t0 + 32],
                                                            start=False, stop=True, skip_group_check=True)
                                    ins.then_inc(filled("S", 1, half, g), 1)
                                    nP += 1
                                o = fill(pe, "O", 1, half)
                                for g in range(KV):
                                    is_free(pe, "S", 1, half, g)
                                for u8 in range(8):
                                    for g in range(KV):
                                        ins = pe.matmul(o[32 * g:32 * g + 32, 128 * u8:128 * u8 + 128],
                                                        Vwin[:, 8 * half + u8, g].rearrange("p a b -> p (a b)"),
                                                        P[(first + g) % PRING][:, 128 * u8:128 * u8 + 128],
                                                        start=True, stop=True, skip_group_check=True)
                                ins.then_inc(filled("O", 1, half), 1)
                                pe.wait_ge(sg("OT"), 8 + half + 1)
                                p = fill(pe, "Ot", 1, half, 0).rearrange("p (T j n) -> p T j n", T=2, j=4)
                                for T in range(2):
                                    for j in range(4):
                                        c = 256 * j + 128 * T
                                        ins = pe.transpose(p[:, T, j, :], OT.rearrange("p g n -> p (g n)")[:, c:c + 128], ident[:, :])
                                ins.then_inc(filled("Ot", 1, half, 0), 1)
                            pe.wait_ge(sg("A"), 2 * a + half + 1)
                            p = fill(pe, "At", a, half)
                            for t in range(4):
                                ins = pe.transpose(p[:, 128 * t:128 * t + 128], At[:, t, :], ident[:, :])
                            ins.then_inc(filled("At", a, half), 1)
                            is_free(pe, "At", a, half)
                            p = fill(pe, "wo", a, half)
                            for t in range(4):
                                ins = pe.matmul(p[:, 128 * t:128 * t + 128], AT[:, 128 * t:128 * t + 128], w_ao[a][:, :],
                                                start=True, stop=True)
                            ins.then_inc(filled("wo", a, half), 1)

                    to_t(2, X, as_is)
                    is_free(pe, "toT", 2)
                    p = fill(pe, "gate")
                    for t in range(NT):
                        ins = pe.matmul(p[:, E * t:E * t + E], xT[:, PAD + 128 * t:PAD + 128 * t + 128], wgate[:, :], start=True, stop=True)
                    ins.then_inc(filled("gate"), 1)
                    for i in range(2 * E + 1):
                        if i < 2 * E:
                            hb, e = divmod(i, E)
                            for k in range(2):
                                p = fill(pe, "h", i, k)
                                for c in range(2):
                                    hc = 2 * k + c
                                    ins = pe.matmul(p[:, 512 * c:512 * c + 512], W1[:, e, 128 * hc:128 * hc + 128],
                                                    xT[:, PAD + 512 * hb:PAD + 512 * hb + 512], start=True, stop=True)
                                ins.then_inc(filled("h", i, k), 1)
                        if i > 0:
                            hb, e = divmod(i - 1, E)
                            p = fill(pe, "eo", i - 1)
                            for k in range(2):
                                is_free(pe, "h", i - 1, k)
                            hv = hbuf[(i - 1) % 3]
                            for t in range(4):
                                for c in range(HC):
                                    ins = pe.matmul(p[:, 128 * t:128 * t + 128], hv[:, c, 128 * t:128 * t + 128], W2m[:, e, c, :],
                                                    start=(c == 0), stop=(c == HC - 1))
                            ins.then_inc(filled("eo", i - 1), 1)
                    pe.wait_ge(sg("gates"), 1)
                    p = fill(pe, "GT")
                    for t in range(NT):
                        ins = pe.transpose(p[0:E, 128 * t:128 * t + 128], gates[:, t, :], ident[:, :])
                    ins.then_inc(filled("GT"), 1)
                    is_free(pe, "GT")
                    p = fill(pe, "b2")
                    for t in range(NT):
                        ins = pe.matmul(p[:, 128 * t:128 * t + 128], GT[:, 128 * t:128 * t + 128], b2m[:, :], start=True, stop=True)
                    ins.then_inc(filled("b2"), 1)

                    to_t(3, X, in_order)
                    is_free(pe, "toT", 3)

                    def project(name, w):
                        p = fill(pe, name)
                        for k in range(2):
                            ins = pe.matmul(p[0:HL, 512 * k:512 * k + 512], lw[:, w, :],
                                            xT[:, PAD + 512 * k:PAD + 512 * k + 512], start=True, stop=True)
                        ins.then_inc(filled(name), 1)

                    project("lq", 0)
                    project("lk", 1)
                    p = fill(pe, "lkv")
                    for t in range(NT):
                        ins = pe.matmul(p[:, 128 * t:128 * t + 128], xT[:, PAD + 128 * t:PAD + 128 * t + 128],
                                        lw[:, 1:3, :].rearrange("p a b -> p (a b)"), start=True, stop=True)
                    ins.then_inc(filled("lkv"), 1)
                    project("lv", 2)
                    pe.wait_ge(sg("l_tok"), 1)
                    p = fill(pe, "lM")
                    for t in range(NT - 1):
                        ins = pe.matmul(p[0:HL, HL * t:HL * t + HL], lvt[:, t, :], lkt[:, t, :], start=True, stop=True)
                    ins.then_inc(filled("lM"), 1)
                    is_free(pe, "lv")
                    p = fill(pe, "ls")
                    for t in range(NT):
                        ins = pe.matmul(p[:, 128 * t:128 * t + 128], lvT[:, 128 * t:128 * t + 128],
                                        lqT[:, 128 * t:128 * t + 128], start=True, stop=True)
                    ins.then_inc(filled("ls"), 1)
                    pe.wait_ge(sg("l_A"), 1)
                    p = fill(pe, "lo")
                    for t in range(NT):
                        c = 128 * t
                        pe.matmul(p[:, c:c + HL], lA[:, t, :], lkt[:, t, :], start=True, stop=(t == 0))
                        if t:
                            pe.matmul(p[:, c:c + HL], lqT[:, c:c + 128], lM[:, t, :], start=False, stop=True)
                        ins = pe.matmul(p[:, c + HL:c + HL + 1], lqz[:, c:c + 128], ones[0:HL, :], start=True, stop=True)
                    ins.then_inc(filled("lo"), 1)
                    pe.wait_ge(sg("l_O"), 1)
                    p = fill(pe, "loT")
                    for t in range(NT):
                        ins = pe.transpose(by_tiles(p[0:HL, :], t), lO[:, t, :], ident[:, :])
                    ins.then_inc(filled("loT"), 1)
                    is_free(pe, "loT")
                    p = fill(pe, "lwo")
                    for t in range(NT):
                        ins = pe.matmul(p[:, 128 * t:128 * t + 128], lOT[:, 128 * t:128 * t + 128], lwo[:, :], start=True, stop=True)
                    ins.then_inc(filled("lwo"), 1)

                    def half_to_features(name, l, h, src, place):
                        p = fill(pe, name, l, h)[:, 0:512]
                        for t in range(4):
                            if place == "in order":
                                o = p.rearrange("p (T u w q) -> p T w u q", T=2, u=4, w=2)[:, t // 2, t % 2]
                            else:
                                o = p.rearrange("p (T w u q) -> p T u w q", T=2, w=2, u=4)[:, t // 2, 2 * (t % 2):2 * (t % 2) + 2]
                            ins = pe.transpose(o, src[:, 4 * h + t, :], ident[:, :])
                        ins.then_inc(filled(name, l, h), 1)

                    def half_step(name, l, h):
                        if name == "xF":
                            if l == 0:
                                pe.wait_ge(sg("src"), 5)
                            else:
                                is_free(pe, "fw2", l - 1, h)
                            half_to_features(name, l, h, X, "in order")
                        elif name == "hF":
                            is_free(pe, "fwo", l, h)
                            half_to_features(name, l, h, X, "in order")
                        elif name == "hB":
                            is_free(pe, "hF", l, h)
                            p = fill(pe, "hB", l, h)
                            for t in range(4):
                                c = 512 * h + 128 * t
                                ins = pe.transpose(p[:, 128 * t:128 * t + 128], hT[:, c:c + 128], ident[:, :])
                            ins.then_inc(filled("hB", l, h), 1)
                        else:
                            pe.wait_ge(sg("ln"), 2 * l + h + 1)
                            half_to_features(name, l, h, N, "by tiles")

                    def hidden(l, h, c):
                        c0, m = CH[c]
                        is_free(pe, "nF", l, h)
                        p = fill(pe, "fw1", l, h, c)
                        for k in range(2):
                            ins = pe.matmul(p[0:m, 512 * k:512 * k + 512], w1[:, l, HID * k + c0:HID * k + c0 + m],
                                            xT[:, PAD + 512 * h:PAD + 512 * h + 512], start=True, stop=True)
                        ins.then_inc(filled("fw1", l, h, c), 1)

                    def second_product(l, h):
                        pe.wait_ge(sg("U"), (2 * l + h + 1) * len(CH))
                        p = fill(pe, "fw2", l, h)
                        for t in range(4):
                            for c, (c0, m) in enumerate(CH):
                                last = c == len(CH) - 1
                                mm = m + 1 if last else m
                                ins = pe.matmul(p[:, 128 * t:128 * t + 128], U[0:mm, c, 128 * t:128 * t + 128], w2[0:mm, l, c, :],
                                                start=(c == 0), stop=last)
                        ins.then_inc(filled("fw2", l, h), 1)

                    for h in range(2):
                        half_step("xF", 0, h)
                    for l in range(DEPTH):
                        for i in range(NT + 4):
                            if i in (0, 4):
                                is_free(pe, "xF", l, i // 4)
                            t = i - 2
                            if 0 <= t < NT:
                                p = fill(pe, "fS", l, t)
                                for w in range(2):
                                    pe.matmul(p[:, 512 * w:512 * w + 512].rearrange("p (a b) -> p a b", b=128), win[:, min(2 * t + w, 1), :],
                                              identb[:, :].unsqueeze(1).to_broadcast([128, 4, 128]),
                                              start=True, stop=False, skip_group_check=True)
                                is_free(pe, "fT", l, t)
                                for w in range(2):
                                    for c in range(4):
                                        ins = pe.matmul(p[:, 512 * w + 128 * c:512 * w + 128 * c + 128],
                                                        fqB[:, w, c].rearrange("p r n -> p (r n)"),
                                                        fkT[t % 2][:, c, 64 * w:64 * w + 128],
                                                        start=False, stop=True, skip_group_check=True)
                                    ins.then_inc(filled("fS", l, t) if w else sg("scores"), 1)
                            if i < NT:
                                p = fill(pe, "fqk", l, i)
                                for k in range(2):
                                    ins = pe.matmul(p[:, 512 * k:512 * k + 512], hT[:, 128 * i:128 * i + 128],
                                                    wqkv[:, l, 512 * k:512 * k + 512], start=True, stop=True)
                                ins.then_inc(filled("fqk", l, i), 1)
                            if i - 4 in (3, 7):
                                g = (i - 4) // 4
                                is_free(pe, "fO", l, i - 4, 0)
                                is_free(pe, "fO", l, i - 4, 1)
                                p = fill(pe, "fwo", l, g)
                                for t in range(4):
                                    for c in range(4):
                                        ins = pe.matmul(p[:, 128 * t:128 * t + 128], fOT[:, c, 128 * t:128 * t + 128], wo[:, l, c, :],
                                                        start=(c == 0), stop=(c == 3))
                                ins.then_inc(filled("fwo", l, g), 1)
                            t = i - 3
                            k = l * NT + t
                            if 0 <= t < NT:
                                is_free(pe, "fPT", l, t)
                                is_free(pe, "fv", l, t)
                                for w in (1, 0):
                                    if w == 0:
                                        pe.wait_ge(sg(f"v_shift{k % VRING}"), 32 * (k // VRING + 1))
                                    p = fill(pe, "fO", l, t, 1 - w)
                                    for c in range(4):
                                        vv = (Vsh if w == 0 else V)[k % VRING]
                                        ins = pe.matmul(p[:, 128 * c:128 * c + 128], vv[:, 128 * c:128 * c + 128],
                                                        fPT[:, 4 * w + c, :], start=True, stop=True)
                                    ins.then_inc(filled("fO", l, t, 1 - w), 1)
                            t = i - 1
                            k = l * NT + t
                            if 0 <= t < NT:
                                pe.wait_ge(sg("unit"), k + 1)
                                p = fill(pe, "fT", l, t)
                                for h in (4, 5, 6, 7, 0, 1, 2, 3):
                                    ins = pe.transpose(p[:, 128 * h:128 * h + 128],
                                                       T1[k % 2].rearrange("p a b -> p (a b)")[:, 128 * h:128 * h + 128], ident[:, :])
                                ins.then_inc(filled("fT", l, t), 1)
                            if i < NT:
                                p = fill(pe, "fv", l, i)
                                pe.matmul(p, hT[:, 128 * i:128 * i + 128], wqkv[:, l, 1024:1536],
                                          start=True, stop=True).then_inc(filled("fv", l, i), 1)
                            t = i - 2
                            k = l * NT + t
                            if 0 <= t < NT:
                                p = fill(pe, "fPT", l, t)
                                for h in range(8):
                                    if h % 4 == 0:
                                        pe.wait_ge(sg("softmax"), 2 * k + 1 + h // 4)
                                    ins = pe.transpose(p[:, 128 * h:128 * h + 128], fP[:, h, :], ident[:, :])
                                ins.then_inc(filled("fPT", l, t), 1)
                            if i in HALF_STEPS:
                                half_step(HALF_STEPS[i], l, 0)
                        for c in range(len(CH)):
                            hidden(l, 0, c)
                            half_step(("hF", "hB", "nF")[c], l, 1)
                        second_product(l, 0)
                        for c in range(len(CH)):
                            hidden(l, 1, c)
                        if l < DEPTH - 1:
                            half_step("xF", l + 1, 0)
                        second_product(l, 1)
                        if l < DEPTH - 1:
                            half_step("xF", l + 1, 1)

                def head_outputs(eng, l, t, w):
                    p = read(eng, "fO", l, t, 1 - w).rearrange("p (c r w q) -> p c r w q", c=4, r=2, w=2)
                    if (l or t) and t % 4 == 0:
                        k = l * NT + t - 4
                        read(eng, "fwo", k // NT, (k % NT) // 4)
                    to = fOT.rearrange("p c (T w u q) -> p c T w u q", T=2, w=2, u=4)
                    for r in range(2):
                        rr = slice(64 * r, 64 * r + 64)
                        o = to[rr, :, (t % 4) // 2, :, 2 * (t % 2) + w, :]
                        if eng is nc.scalar:
                            ins = eng.activation(o, p[rr, :, r], ACT.Copy)
                        else:
                            ins = eng.tensor_copy(o, p[rr, :, r])
                    ins.then_inc(freed("fO", l, t, 1 - w), 1)

                def numerators_read(k):
                    n = [len(attention_units(0, 0)), len(attention_units(0, 1))]
                    if k >= sum(n):
                        j = k - sum(n)
                        t = tk.at[("O", 1, j // KV)]
                        return sg(f"full_{t[0]}{t[1]}"), t[2] + 1
                    half = int(k >= n[0])
                    i = k - half * n[0]
                    g, kc, jp = attention_units(0, half)[i]
                    if kc == 4 * half + 3 and jp == 1:
                        t = tk.at[("O", 0, half, g)]
                        return sg(f"full_{t[0]}{t[1]}"), t[2] + 1
                    done = 4 * half + g
                    return sg("pv"), k + 1 - done

                @block.scalar
                def _(act):
                    def out_xT(i):
                        p = read(act, "toT", i)
                        act.activation(xT[:, PAD:PAD + S], p, ACT.Copy).then_inc(freed("toT", i), 1)

                    nP = 0
                    gone_units = 0
                    for a in range(2):
                        out_xT(a)
                        act.wait_ge(sg("set"), 7)
                        for i in range(2):
                            p = read(act, "qkv", a, i).rearrange("p (t n) -> p t n", t=4)
                            if a == 0:
                                act.activation(Vaug[:, 4 * i:4 * i + 4, :, 0:HD],
                                               p[:, :, 160:192].rearrange("p t (g d) -> p t g d", g=KV), ACT.Copy)
                            act.activation(QK[:, 4 * i:4 * i + 4, :], p[:, :, 0:160], ACT.Copy).then_inc(freed("qkv", a, i), 1)
                        if a == 1:
                            p = read(act, "vwin").rearrange("p (u n) -> p u n", u=16)
                            for w in range(2):
                                ins = act.activation(Vwin[64 * w:64 * w + 64, :, :, w, 0:HD],
                                               p[64 * w:64 * w + 64, :, 0:32].rearrange("p u (g d) -> p u g d", g=KV),
                                               ACT.Copy)
                            ins.then_inc(freed("vwin"), 1)
                        act.wait_ge(sg("qn"), a + 1)
                        for s in range(2):
                            act.activation(Qs[:, :, :, s, :], QR[:, :, 0:128].rearrange("p t (j n) -> p t j n", j=GQ),
                                           ACT.Copy).then_inc(sg("q_hi"), 1)
                        for i in range(2):
                            p = read(act, "qT", a, i).bitcast(F16).rearrange("p (j n) -> p j n", j=2)
                            act.activation(QT[:, 2 * i:2 * i + 2, :], p, ACT.Copy).then_inc(freed("qT", a, i), 1)
                        for half in range(2):
                            for u in attention_units(a, half):
                                if a == 0:
                                    n = min(512, 512 - 128 * (u[1] - 4 * half))
                                else:
                                    n = 512
                                p = read(act, "S", a, half, *u).rearrange("p (j n) -> p j n", j=2)
                                if nP >= PRING:
                                    act.wait_ge(*numerators_read(nP - PRING))
                                pb = P[nP % PRING].rearrange("p (j n) -> p j n", j=2)
                                act.activation(pb[:, :, 0:n], p[:, :, 0:n], ACT.Exp, scale=INV_SQRT_HD).then_inc(freed("S", a, half, *u), 1)
                                nP += 1
                            p = read(act, "At", a, half)
                            act.activation(AT, p, ACT.Copy).then_inc(freed("At", a, half), 1)
                    out_xT(2)
                    act.wait_ge(sg("g_lg"), 1)
                    act.activation(gtmp[1][:, :, :], gtmp[0][:, :, :], ACT.Exp).then_inc(sg("g_exp"), 1)
                    for i in range(2 * E):
                        hb, e = divmod(i, E)
                        if i >= 3:
                            read(act, "eo", i - 3)
                        for k in range(2):
                            p = read(act, "h", i, k)
                            for c in range(2):
                                hc = 2 * k + c
                                ins = act.activation(hbuf[i % 3][:, hc, :], p[:, 512 * c:512 * c + 512], ACT.Gelu_apprx_tanh,
                                               bias=b1[:, e, hc:hc + 1])
                            ins.then_inc(freed("h", i, k), 1)
                    p = read(act, "GT")
                    act.activation(GT, p[0:E, :], ACT.Copy).then_inc(freed("GT"), 1)
                    out_xT(3)
                    for i in range(3):
                        act.wait_ge(sg("l_min"), i + 1)
                        if i < 2:
                            act.activation(lm[i][0:HL, :], lm[i][0:HL, :], ACT.Exp).then_inc(sg("l_exp"), 1)
                        else:
                            act.activation(lm[i][:, 0:NT * HL], lm[i][:, 0:NT * HL], ACT.Exp).then_inc(sg("l_exp"), 1)
                    p = read(act, "lv")
                    act.activation(lvT, p[0:HL, :], ACT.Copy).then_inc(freed("lv"), 1)
                    p = read(act, "loT")
                    act.activation(lOT, p[0:HL, :], ACT.Copy).then_inc(freed("loT"), 1)
                    def half(name, l, h):
                        if name in ("xF", "hF"):
                            p = read(act, name, l, h)
                            if name == "xF" and l:
                                read(act, "hB", l - 1, 1)
                            n = min(512, S - 1 - 512 * h)
                            act.activation(hT[0:64, 512 * h:512 * h + 512], p[0:64, 0:512], ACT.Copy)
                            act.activation(hT[64:128, 512 * h + 1:512 * h + 1 + n], p[64:128, 0:n], ACT.Copy).then_inc(freed(name, l, h), 1)
                        elif name == "nF":
                            p = read(act, name, l, h)
                            act.activation(xT[:, PAD + 512 * h:PAD + 512 * h + 512], p[:, 0:512], ACT.Copy).then_inc(freed(name, l, h), 1)

                    def gelu(l, h, c):
                        c0, m = CH[c]
                        p = read(act, "fw1", l, h, c)
                        k = (2 * l + h) * len(CH) + c
                        if k >= 2:
                            act.wait_ge(sg("U"), k - 1)
                        act.activation(GL[k % 2][0:m, :], p[0:m, 512:1024], ACT.Gelu,
                                       bias=fb1[0:m, l, 1, c:c + 1]).then_inc(sg("GL"), 1)

                    for h in range(2):
                        half("xF", 0, h)
                    for l in range(DEPTH):
                        for i in range(NT + 3):
                            t = i - 2
                            k = l * NT + t
                            for w in range(2):
                                if 0 <= t < NT:
                                    act.wait_ge(sg("largest"), 2 * k + 1 + w)
                                    p = slot("fS", l, t)
                                    if k and w == 0:
                                        read(act, "fPT", (k - 1) // NT, (k - 1) % NT)
                                    for h in range(4 * w, 4 * w + 4):
                                        ins = act.activation(fP[:, h, :], p[:, 128 * h:128 * h + 128], ACT.Exp,
                                                             bias=fnm[:, h:h + 1], accum_out=fden[:, h:h + 1])
                                    ins.then_inc(freed("fS", l, t) if w else sg("exps"), 1)
                                if i < NT and w == 0:
                                    p = read(act, "fqk", l, i)
                                    if l or i:
                                        act.wait_ge(sg("sums"), l * NT + i)
                                    act.activation(SQb.rearrange("p a b -> p (a b)"), p, ACT.Square).then_inc(sg("squares"), 1)
                            t = i - 3
                            if 0 <= t < NT:
                                head_outputs(act, l, t, 1)
                            t = i - 1
                            k = l * NT + t
                            if 0 <= t < NT:
                                p = read(act, "fT", l, t).rearrange("p (h n) -> p h n", h=8)
                                if k >= 1:
                                    read(act, "fS", (k - 1) // NT, (k - 1) % NT)
                                else:
                                    act.wait_ge(sg("blocks"), 1)
                                act.activation(fkT[t % 2][:, :, 64:192], p[:, 4:8, :], ACT.Copy)
                                before = p[:, 4:8, 64:128] if t == 0 else fkT[(t - 1) % 2][:, :, 128:192]
                                act.activation(fkT[t % 2][:, :, 0:64], before, ACT.Copy)
                                for r in range(2):
                                    rr = slice(64 * r, 64 * r + 64)
                                    ins = act.activation(fqB[rr, :, :, r, :], p[rr, 0:4, :].rearrange("p c (w q) -> p w c q", w=2), ACT.Copy)
                                ins.then_inc(freed("fT", l, t), 1)
                            if i < NT:
                                k = l * NT + i
                                p = read(act, "fv", l, i)
                                if k >= VRING:
                                    read(act, "fO", (k - VRING) // NT, (k - VRING) % NT, 1)
                                    j = k - VRING + 1
                                    act.wait_ge(sg(f"v_shift{j % VRING}"), 32 * (j // VRING + 1))
                                act.activation(V[k % VRING], p, ACT.Copy).then_inc(freed("fv", l, i), 1)
                            t = i - 2
                            k = l * NT + t
                            if 0 <= t < NT:
                                p = read(act, "fPT", l, t)
                                if k:
                                    read(act, "fO", (k - 1) // NT, (k - 1) % NT, 1)
                                act.activation(fPT.rearrange("p a b -> p (a b)"), p, ACT.Copy).then_inc(freed("fPT", l, t), 1)
                            if i in HALF_STEPS:
                                half(HALF_STEPS[i], l, 0)
                        for c in range(len(CH)):
                            gelu(l, 0, c)
                            half(("hF", "hB", "nF")[c], l, 1)
                        for c in range(len(CH)):
                            gelu(l, 1, c)
                        if l < DEPTH - 1:
                            for h in range(2):
                                half("xF", l + 1, h)

                @block.vector
                def _(dve):
                    chain = [0]

                    def link(ins):
                        chain[0] += 1
                        ins.then_inc(sg("dve_chain"), 1)
                        dve.wait_ge(sg("dve_chain"), chain[0])

                    counts = {}

                    def signals(ins, name):
                        counts[name] = counts.get(name, 0) + 1
                        ins.then_inc(sg(name), 1)
                        dve.wait_ge(sg(name), counts[name])

                    def frees(ins, *key):
                        ins.then_inc(freed(*key), 1)
                        is_free(dve, *key)

                    def rsqrt(n):
                        m, y, t = st_m[:, 0:n], st_y[:, 0:n], st_t[:, 0:n]
                        link(dve.tensor_scalar(st_i[:, 0:n], m.bitcast(I32), 1, None, ALU.logical_shift_right))
                        link(dve.tensor_scalar(y.bitcast(I32), st_i[:, 0:n], -1.0, 1597463007.0, ALU.mult, ALU.add))
                        for _ in range(3):
                            link(dve.tensor_tensor(t, y, y, ALU.mult))
                            link(dve.scalar_tensor_tensor(out=t, in0=t, scalar=-0.5, in1=m, op0=ALU.mult, op1=ALU.mult))
                            link(dve.scalar_tensor_tensor(out=y, in0=t, scalar=1.5, in1=y, op0=ALU.add, op1=ALU.mult))

                    def per_token(n, nt=NT):
                        return st_y[:, 0:nt].unsqueeze(2).to_broadcast([128, nt, n])

                    def layer_norm(src, dst, name, key=None):
                        nt = src.shape[1]
                        link(dve.tensor_reduce(st_a[:, 0:nt], src, AX, ALU.add))
                        link(dve.tensor_scalar(st_a[:, 0:nt], st_a[:, 0:nt], -1.0 / D, None, ALU.mult))
                        ins = dve.tensor_tensor(dst, src, st_a[:, 0:nt].unsqueeze(2).to_broadcast([128, nt, D]), ALU.add)
                        if key is None:
                            link(ins)
                        else:
                            frees(ins, *key)
                        link(dve.tensor_tensor(Q[:, 0:nt, :], dst, dst, ALU.mult))
                        link(dve.tensor_reduce(st_a[:, 0:nt], Q[:, 0:nt, :], AX, ALU.add))
                        link(dve.tensor_scalar(st_m[:, 0:nt], st_a[:, 0:nt], 1.0 / D, 1e-5, ALU.mult, ALU.add))
                        rsqrt(nt)
                        signals(dve.tensor_tensor(dst, dst, per_token(D, nt), ALU.mult), name)

                    def signal(name):
                        counts[name] = counts.get(name, 0) + 1
                        dve.sem_inc(sg(name), 1)

                    dve.wait_ge(sg("x_in"), 256)
                    for a in range(2):
                        src = (X, R)[a][:, :, :]
                        link(dve.tensor_tensor(Q[:, :, :], src, src, ALU.mult))
                        link(dve.tensor_reduce(st_a[:, 0:NT], Q[:, :, :], AX, ALU.add))
                        link(dve.tensor_scalar(st_m[:, 0:NT], st_a[:, 0:NT], 1.0 / D, 1e-6, ALU.mult, ALU.add))
                        rsqrt(NT)
                        signals(dve.tensor_tensor(N[:, :, :], src, per_token(D), ALU.mult), "src")
                        for i in range(2):
                            is_free(dve, "qkv", a, i)
                        nh = H + KV
                        qv = QK.rearrange("p t (h d) -> p t h d", h=nh)
                        rv = QR.rearrange("p t (h d) -> p t h d", h=nh)
                        sw = QK.rearrange("p t (h d s) -> p t h d s", h=nh, s=2)
                        tmp = arena_rope.rearrange("p t (h d s) -> p t h d s", h=nh, s=2)
                        for t in range(NT):
                            dve.tensor_tensor(rv[:, t], qv[:, t],
                                              rope[a][:, t, 0:1, :].to_broadcast([128, nh, HD]), ALU.mult)
                            for s in range(2):
                                ins = dve.tensor_tensor(tmp[:, t, :, :, s], sw[:, t, :, :, 1 - s],
                                                  rope[a][:, t, 1:2, :].rearrange("p o (d s) -> p o d s", s=2)[:, :, :, s].to_broadcast([128, nh, HD // 2]), ALU.mult)
                        link(ins)
                        link(dve.tensor_tensor(QR, QR, arena_rope, ALU.add))
                        link(dve.tensor_tensor(arena_rope, QR, QR, ALU.mult))
                        link(dve.tensor_reduce(st_a[:, 0:160], arena_rope.rearrange("p t (h d) -> p (t h) d", h=nh), AX, ALU.add))
                        link(dve.tensor_scalar(st_m[:, :], st_a[:, :], 1.0 / HD, 1e-6, ALU.mult, ALU.add))
                        rsqrt(160)
                        QRf = QR.rearrange("p t (h d) -> p (t h) d", h=nh)
                        signals(dve.tensor_tensor(QRf, QRf, st_y[:, :].unsqueeze(2).to_broadcast([128, 160, HD]), ALU.mult), "qn")
                        kv = QR[:, :, 128:160]
                        dve.wait_ge(sg("set"), 7)
                        for s in (0, 2):
                            for g in range(KV):
                                ins = dve.tensor_copy(Kpad[:, :, g, s, g, :], kv[:, :, 8 * g:8 * g + 8])
                        link(ins)
                        for s in (1, 3):
                            for g in range(KV):
                                ins = dve.tensor_tensor(Kpad[:, :, g, s, g, :], kv[:, :, 8 * g:8 * g + 8],
                                                        Kpad[:, :, g, s - 1, g, :], ALU.subtract)
                        dve.wait_ge(sg("q_hi"), 2 * a + 2)
                        for s in (2, 3):
                            ins = dve.tensor_tensor(Qs[:, :, :, s, :], QR[:, :, 0:128].rearrange("p t (j n) -> p t j n", j=GQ),
                                                    Qs[:, :, :, s - 2, :], ALU.subtract)
                        signals(ins, "split")
                        for i in range(2):
                            p = read(dve, "kT", a, i).bitcast(F16).rearrange("p (j n) -> p j n", j=2)
                            if i == 0:
                                link(dve.memset(KT[:, :, 0:PAD], 0.0))
                            frees(dve.tensor_copy(KT[:, 2 * i:2 * i + 2, PAD:PAD + S], p), "kT", a, i)
                        for half in range(2):
                            Av = At.rearrange("p t (g j d) -> p t g j d", g=KV, j=GQ)
                            if a == 0:
                                for g in range(KV):
                                    p = read(dve, "O", 0, half, g)
                                    if half:
                                        read(dve, "Ot", 0, 0, g // 2)
                                    pv = p.rearrange("p (T u w q) -> p T w u q", T=2, u=4, w=2)
                                    ov = OT[:, g, :].rearrange("p (T w u q) -> p T w u q", T=2, u=4, w=2)
                                    for T in range(2):
                                        ins = dve.tensor_copy(ov[:, T], pv[:, T])
                                    frees(ins, "O", 0, half, g)
                                    signal("OT")
                                for i in range(2):
                                    p = read(dve, "Ot", 0, half, i).rearrange("p (g t j n) -> p g t j n", g=2, t=4, j=4)
                                    for gg in range(2):
                                        rd = rden[:, 0:16].rearrange("p (t j) -> p t j", t=4)
                                        link(dve.reciprocal(rd, p[:, gg, :, :, HD]))
                                        link(dve.tensor_tensor(Av[:, :, 2 * i + gg], p[:, gg, :, :, 0:HD],
                                                               rd.unsqueeze(3).to_broadcast([128, 4, 4, HD]), ALU.mult))
                                    dve.sem_inc(freed("Ot", 0, half, i), 1)
                            else:
                                p = read(dve, "O", 1, half)
                                frees(dve.tensor_copy(OT.rearrange("p g n -> p (g n)")[:, 0:1024].rearrange("p (j u q) -> p u j q", j=4, u=8),
                                                     p.rearrange("p (u j q) -> p u j q", u=8, j=4)), "O", 1, half)
                                signal("OT")
                                p = read(dve, "Ot", 1, half, 0).rearrange("p (T j g w n) -> p T j g w n", T=2, j=4, g=4, w=2)
                                for T in range(2):
                                    for w in range(2):
                                        rd = rden[:, 0:16].rearrange("p (g j) -> p g j", g=4)
                                        pv = p[:, T, :, :, w].rearrange("p j g n -> p g j n")
                                        link(dve.reciprocal(rd, pv[:, :, :, HD]))
                                        link(dve.tensor_tensor(Av[:, 2 * T + w], pv[:, :, :, 0:HD],
                                                               rd.unsqueeze(3).to_broadcast([128, 4, 4, HD]), ALU.mult))
                                dve.sem_inc(freed("Ot", 1, half, 0), 1)
                            signal("A")
                            p = read(dve, "wo", a, half).rearrange("p (t n) -> p t n", t=4)
                            base_ = (X, R)[a]
                            frees(dve.tensor_tensor(R[:, 4 * half:4 * half + 4, :], base_[:, 4 * half:4 * half + 4, :], p, ALU.add), "wo", a, half)
                    link(dve.tensor_tensor(R[:, :, :], R[:, :, :], X[:, :, :], ALU.add))
                    layer_norm(R[:, :, :], X[:, :, :], "src")
                    p = read(dve, "gate")[:, 0:NT * E].rearrange("p (t e) -> p t e", t=NT)
                    bc = lambda v: v.unsqueeze(2).to_broadcast([128, NT, E])
                    lg, pr, c0_, c1_ = (g[:, :, :] for g in gtmp)
                    one = gone[0][:, :]
                    frees(dve.tensor_tensor(lg, p, bgate[:, :].unsqueeze(1).to_broadcast([128, NT, E]), ALU.add), "gate")
                    link(dve.tensor_reduce(one, lg, AX, ALU.max))
                    signals(dve.tensor_tensor(lg, lg, bc(one), ALU.subtract), "g_lg")
                    dve.wait_ge(sg("g_exp"), 1)
                    link(dve.tensor_reduce(one, pr, AX, ALU.add))
                    link(dve.reciprocal(gone[1][:, :], one))
                    link(dve.tensor_tensor(pr, pr, bc(gone[1][:, :]), ALU.mult))
                    link(dve.tensor_copy(lg, pr))
                    rk = rank[:, :].unsqueeze(1).to_broadcast([128, NT, E])
                    for k in range(2):
                        link(dve.tensor_reduce(one, lg, AX, ALU.max))
                        link(dve.tensor_tensor(c0_, lg, bc(one), ALU.is_equal))
                        link(dve.tensor_tensor(c0_, c0_, rk, ALU.mult))
                        link(dve.tensor_reduce(one, c0_, AX, ALU.max))
                        link(dve.tensor_tensor(c0_, c0_, bc(one), ALU.is_equal))
                        if k == 0:
                            link(dve.tensor_copy(c1_, c0_))
                            link(dve.scalar_tensor_tensor(out=lg, in0=c0_, scalar=-2.0, in1=lg, op0=ALU.mult, op1=ALU.add))
                        else:
                            link(dve.tensor_tensor(c1_, c1_, c0_, ALU.add))
                    link(dve.tensor_tensor(pr, pr, c1_, ALU.mult))
                    link(dve.tensor_reduce(one, pr, AX, ALU.add))
                    link(dve.tensor_scalar(one, one, 1e-8, None, ALU.add))
                    link(dve.reciprocal(gone[1][:, :], one))
                    signals(dve.tensor_tensor(gates[:, :, :], pr, bc(gone[1][:, :]), ALU.mult), "gates")
                    for i in range(2 * E):
                        hb, e = divmod(i, E)
                        p = read(dve, "eo", i)
                        for t in range(4):
                            tt = 4 * hb + t
                            acc = X if e == 0 else R
                            ins = dve.scalar_tensor_tensor(out=R[:, tt, :], in0=p[:, 128 * t:128 * t + 128],
                                                           scalar=gates[:, tt, e:e + 1], in1=acc[:, tt, :],
                                                           op0=ALU.mult, op1=ALU.add)
                        frees(ins, "eo", i)
                    p = read(dve, "b2").rearrange("p (t n) -> p t n", t=NT)
                    frees(dve.tensor_tensor(R[:, :, :], R[:, :, :], p, ALU.add), "b2")
                    layer_norm(R[:, :, :], X[:, :, :], "src")
                    dve.memset(lone, 1.0)
                    pq = read(dve, "lq")[0:HL, :]
                    signals(dve.tensor_scalar(lm[0][0:HL, :], pq, 0.0, None, ALU.min), "l_min")
                    pk = read(dve, "lk")[0:HL, :]
                    signals(dve.tensor_scalar(lm[1][0:HL, :], pk, 0.0, None, ALU.min), "l_min")
                    pt = read(dve, "lkv").rearrange("p (t n) -> p t n", t=NT)
                    m2 = lm[2][:, 0:NT * HL].rearrange("p (t n) -> p t n", t=NT)
                    signals(dve.tensor_scalar(m2, pt[:, :, 0:HL], 0.0, None, ALU.min), "l_min")
                    dve.wait_ge(sg("l_exp"), 1)
                    frees(dve.scalar_tensor_tensor(out=lqT, in0=pq, scalar=0.0, in1=lm[0][0:HL, :], op0=ALU.max, op1=ALU.add), "lq")
                    dve.wait_ge(sg("l_exp"), 2)
                    frees(dve.scalar_tensor_tensor(out=lkT, in0=pk, scalar=0.0, in1=lm[1][0:HL, :], op0=ALU.max, op1=ALU.add), "lk")
                    dve.wait_ge(sg("l_exp"), 3)
                    dve.tensor_copy(lvt, pt[:, :, HL:128])
                    frees(dve.scalar_tensor_tensor(out=lkt, in0=pt[:, :, 0:HL], scalar=0.0, in1=m2, op0=ALU.max, op1=ALU.add), "lkv")
                    signal("l_tok")
                    link(dve.tensor_tensor_scan(lz, lone, lkT, 0.0, ALU.mult, ALU.add))
                    link(dve.tensor_tensor(lqz, lqT, lz, ALU.mult))
                    p = read(dve, "lM")[0:HL, :].rearrange("p (t n) -> p t n", t=NT)
                    link(dve.tensor_copy(lM[:, 1, :], p[:, 0, :]))
                    for t in range(2, NT):
                        link(dve.tensor_tensor(lM[:, t, :], lM[:, t - 1, :], p[:, t - 1, :], ALU.add))
                    dve.sem_inc(freed("lM"), 1)
                    p = read(dve, "ls").rearrange("p (t n) -> p t n", t=NT)
                    frees(dve.tensor_tensor(lA, p, tri[:, :].unsqueeze(1).to_broadcast([128, NT, 128]), ALU.mult), "ls")
                    signal("l_A")
                    p = read(dve, "lo").rearrange("p (t n) -> p t n", t=NT)
                    link(dve.tensor_scalar(st_a[:, 0:NT], p[:, :, HL], 1e-6, None, ALU.max))
                    link(dve.reciprocal(st_y[:, 0:NT], st_a[:, 0:NT]))
                    frees(dve.tensor_tensor(lO, p[:, :, 0:HL], per_token(HL), ALU.mult), "lo")
                    signal("l_O")
                    p = read(dve, "lwo").rearrange("p (t n) -> p t n", t=NT)
                    frees(dve.tensor_tensor(R[:, :, :], X[:, :, :], p, ALU.add), "lwo")
                    layer_norm(R[:, :, :], X[:, :, :], "src")
                    link(dve.tensor_copy(R[:, :, :], X[:, :, :]))
                    def half_norm(l, h):
                        p = read(dve, "hB", l, h)[:, 0:512].rearrange("p (t n) -> p t n", t=4)
                        layer_norm(p, N[:, 4 * h:4 * h + 4, :], "ln", ("hB", l, h))

                    def gated(l, h, c):
                        c0, m = CH[c]
                        k = (2 * l + h) * len(CH) + c
                        if c == 0:
                            if l or h:
                                read(dve, "fw2", l if h else l - 1, 1 - h)
                            link(dve.memset(U[64:96, 2, :], 1.0))
                        p = read(dve, "fw1", l, h, c)
                        dve.wait_ge(sg("GL"), k + 1)
                        frees(dve.scalar_tensor_tensor(out=U[0:m, c, :], in0=p[0:m, 0:512], scalar=fb1[0:m, l, 0, c:c + 1],
                                                       in1=GL[k % 2][0:m, :], op0=ALU.add, op1=ALU.mult), "fw1", l, h, c)
                        signal("U")

                    def add_second(l, h):
                        p = read(dve, "fw2", l, h).rearrange("p (t n) -> p t n", t=4)
                        Xh = X[:, 4 * h:4 * h + 4, :]
                        frees(dve.tensor_tensor(Xh, Xh, p, ALU.add), "fw2", l, h)

                    def last_norm(h):
                        hs = slice(4 * h, 4 * h + 4)
                        signals(dve.tensor_tensor(R[:, hs, :], R[:, hs, :], X[:, hs, :], ALU.add), "x_read")
                        layer_norm(R[:, hs, :], N[:, hs, :], "final")

                    for l in range(DEPTH):
                        for i in range(NT + 4):
                            def rotary(s):
                                hs = slice(NH * s, NH * s + NH)
                                x = read(dve, "fqk", l, i).rearrange("p (h n) -> p h n", h=16)[:, hs, :]
                                if k:
                                    dve.wait_ge(sg("rot"), 2 * k)
                                dve.tensor_tensor(T1[k % 2][:, hs, :], x, xpos[:, l, i, 0, s:s + 1, :].to_broadcast([128, NH, DH]), ALU.mult)
                                return dve.tensor_tensor(T2[:, hs, :].rearrange("p h (a b) -> p h a b", a=2),
                                                         x.rearrange("p h (a b) -> p h a b", a=2)[:, :, ::-1, :],
                                                         xpos[:, l, i, 1, s:s + 1, :].rearrange("p o (a b) -> p o a b", a=2).to_broadcast([128, NH, 2, 32]),
                                                         ALU.mult)

                            t = i - 2
                            if 0 <= t < NT:
                                kk = l * NT + t
                                for w in range(2):
                                    if w == 0:
                                        dve.wait_ge(sg("scores"), kk + 1)
                                    else:
                                        read(dve, "fS", l, t)
                                    p = slot("fS", l, t)[:, 512 * w:512 * w + 512].rearrange("p (h n) -> p h n", h=4)
                                    dve.tensor_reduce(fnm[:, 4 * w:4 * w + 4], p, AX, ALU.max, negate=True).then_inc(sg("largest"), 1)
                            t = i - 1
                            if 0 <= t < NT:
                                kk = l * NT + t
                                dve.wait_ge(sg("inverse"), kk + 1)
                                dve.wait_ge(sg("rot"), 2 * kk + 2)
                                v = T1[kk % 2]
                                dve.tensor_tensor(v, v, fy[:, :].unsqueeze(2).to_broadcast([128, 16, DH]), ALU.mult).then_inc(sg("unit"), 1)
                            k = l * NT + i
                            if i < NT:
                                dve.wait_ge(sg("squares"), k + 1)
                                dve.tensor_reduce(fss[:, :], SQb, AX, ALU.add).then_inc(sg("sums"), 1)
                                dve.wait_ge(sg("sums"), k + 1)
                                if k:
                                    dve.wait_ge(sg("unit"), k)
                                link(dve.tensor_scalar(fm[:, :], fss[:, :], 1e-24, None, ALU.max))
                                link(dve.tensor_scalar(fi[:, :], fm[:, :].bitcast(I32), 1, None, ALU.logical_shift_right))
                                dve.tensor_scalar(fy[:, :].bitcast(I32), fi[:, :], -1.0, 1597463007.0, ALU.mult, ALU.add).then_inc(sg("guess"), 1)
                            if i - 4 in (3, 7):
                                g = (i - 4) // 4
                                p = read(dve, "fwo", l, g).rearrange("p (t n) -> p t n", t=4)
                                frees(dve.tensor_tensor(X[:, 4 * g:4 * g + 4, :], X[:, 4 * g:4 * g + 4, :], p, ALU.add), "fwo", l, g)
                            t = i - 2
                            if 0 <= t < NT:
                                for w in range(2):
                                    if w == 0:
                                        dve.wait_ge(sg("exps"), l * NT + t + 1)
                                    else:
                                        is_free(dve, "fS", l, t)
                                    ws = slice(4 * w, 4 * w + 4)
                                    link(dve.reciprocal(frd[:, ws], fden[:, ws]))
                                    dve.tensor_tensor(fP[:, ws], fP[:, ws], frd[:, ws].unsqueeze(2).to_broadcast([128, 4, 128]),
                                                      ALU.mult).then_inc(sg("softmax"), 1)
                            if i < NT:
                                if k >= 2:
                                    read(dve, "fT", (k - 2) // NT, (k - 2) % NT)
                                rotary(0).then_inc(sg("prod"), 1)
                                rotary(1).then_inc(freed("fqk", l, i), 1)
                            t = i - 3
                            if 0 <= t < NT:
                                head_outputs(dve, l, t, 0)
                            if i == NT + 1:
                                half_norm(l, 0)
                        gated(l, 0, 0)
                        gated(l, 0, 1)
                        half_norm(l, 1)
                        gated(l, 0, 2)
                        add_second(l, 0)
                        if l == DEPTH - 1:
                            last_norm(0)
                        for c in range(len(CH)):
                            gated(l, 1, c)
                        add_second(l, 1)
                    last_norm(1)

                @block.gpsimd
                def _(pool):
                    pool.memset(Kpad.rearrange("p a b c d e -> p (a b c d e)"), 0.0).then_inc(sg("set"), 1)
                    pool.memset(Vaug.rearrange("p a b c -> p (a b c)"), 0.0).then_inc(sg("set"), 1)
                    pool.memset(Vwin.rearrange("p a b c d -> p (a b c d)"), 0.0).then_inc(sg("set"), 1)
                    pool.wait_ge(sg("set"), 3)
                    pool.memset(Vaug[:, :, :, HD:HD + 1], 1.0).then_inc(sg("set"), 1)
                    pool.wait_ge(sg("set"), 4)
                    pool.memset(Vwin[0:64, :, :, 0, HD:HD + 1], 1.0).then_inc(sg("set"), 1)
                    pool.wait_ge(sg("set"), 5)
                    pool.memset(Vwin[64:128, :, :, 1, HD:HD + 1], 1.0).then_inc(sg("set"), 1)
                    pool.wait_ge(sg("set"), 6)
                    pool.memset(Vwin[0:WIN, 0:1, :, 0, HD:HD + 1], 0.0).then_inc(sg("set"), 1)
                    steps = [0]

                    def link(ins):
                        steps[0] += 1
                        ins.then_inc(sg("pool_chain"), 1)
                        pool.wait_ge(sg("pool_chain"), steps[0])

                    pool.wait_ge(sg("src"), 5)
                    pool.memset(fqB.rearrange("p a b c d -> p (a b c d)"), 0.0).then_inc(sg("blocks"), 1)
                    for k in range(DEPTH * NT):
                        pool.wait_ge(sg("guess"), k + 1)
                        for j in range(3):
                            link(pool.tensor_tensor(ft[:, :], fy[:, :], fy[:, :], ALU.mult))
                            link(pool.tensor_tensor(ft[:, :], ft[:, :], fm[:, :], ALU.mult))
                            link(pool.tensor_scalar(ft[:, :], ft[:, :], -0.5, 1.5, ALU.mult, ALU.add))
                            ins = pool.tensor_tensor(fy[:, :], fy[:, :], ft[:, :], ALU.mult)
                            if j < 2:
                                link(ins)
                        ins.then_inc(sg("inverse"), 1)
                        for s in range(2):
                            if s == 0:
                                pool.wait_ge(sg("prod"), k + 1)
                            else:
                                is_free(pool, "fqk", k // NT, k % NT)
                            hs = slice(NH * s, NH * s + NH)
                            pool.tensor_tensor(T1[k % 2][:, hs, :], T1[k % 2][:, hs, :], T2[:, hs, :], ALU.add).then_inc(sg("rot"), 1)
            with nc.Block() as block:
                @block.sync
                def _(sp):
                    for name, s in sems.items():
                        if name != "x_in":
                            sp.sem_clear(s)

        with nc.Block() as block:
            @block.sync
            def _(sp):
                sp.wait_ge(sg("x_in"), 256)


_INS = ['L0_attn_hidden', 'L0_attn_norm1_w', 'L0_attn_norm2_w', 'L0_attn_g_wq', 'L0_attn_g_kv_down', 'L0_attn_g_k_up',
        'L0_attn_g_v_up', 'L0_attn_g_wo', 'L0_attn_l_wq', 'L0_attn_l_wk', 'L0_attn_l_wv', 'L0_attn_l_wo', 'L0_ffn_Wg',
        'L0_ffn_bg', 'L0_ffn_W1', 'L0_ffn_b1', 'L0_ffn_W2', 'L0_ffn_b2', 'L1_attn_W_q', 'L1_attn_W_k', 'L1_attn_W_v',
        'L1_attn_W_o', 'L1_ffn_wqkv', 'L1_ffn_q_scale', 'L1_ffn_k_scale', 'L1_ffn_wo', 'L1_ffn_ln_g', 'L1_ffn_ln_b',
        'L1_ffn_w1', 'L1_ffn_b1', 'L1_ffn_w2', 'L1_ffn_b2']


def kernel(**inputs):
    import concourse.bacc as _bacc
    from concourse.bass_utils import run_bass_kernel_spmd as _run

    nc = _bacc.Bacc("TRN2", target_bir_lowering=False, num_devices=1)
    arrays, handles = {}, {}
    given = {n: np.ascontiguousarray(inputs[n]) for n in _INS}
    given["L0_attn_hidden"] = np.concatenate([given["L0_attn_hidden"], np.zeros((1, S, D), np.float32)])
    for n in ("L0_attn_g_wq", "L0_attn_l_wq"):
        given[n] = np.ascontiguousarray(given[n].reshape(D, KV, GQ, HD).transpose(0, 2, 1, 3).reshape(D, H * HD))
    given["L0_ffn_b1"] = np.ascontiguousarray(given["L0_ffn_b1"].reshape(E, HC, 128).transpose(2, 0, 1))
    given["L1_ffn_ln_g"], given["L1_ffn_ln_b"] = (np.ascontiguousarray(given[n].T) for n in ("L1_ffn_ln_g", "L1_ffn_ln_b"))
    b1 = np.zeros((DEPTH, 2, len(CH) * 128), np.float32)
    b1[:, :, :HID] = given["L1_ffn_b1"].reshape(DEPTH, 2, HID)
    given["L1_ffn_b1"] = np.ascontiguousarray(b1.reshape(DEPTH, 2, len(CH), 128).transpose(3, 0, 1, 2))
    given.update(constant_tables())
    given["c_rank"] = np.arange(E, 0, -1).astype(np.float32)
    for name, a in given.items():
        arrays[f"in_{name}"] = a
        handles[name] = nc.dram_tensor(f"in_{name}", a.shape, mybir.dt.from_np(a.dtype), kind="ExternalInput").ap()
    handles["out"] = nc.dram_tensor("out_y", (B, S, D), F32, kind="ExternalOutput").ap()
    build(nc, handles)
    r = _run(nc, [arrays], core_ids=[0])
    return r.results[0]["out_y"]
```
